# Optimizing a Trainium2 kernel written in Bass

```python
import numpy as np
import jax
import jax.numpy as jnp

def _softmax(x, axis=-1):
    return jax.nn.softmax(x, axis=axis)

def _gelu(x):
    return jax.nn.gelu(x, approximate=True)

def _silu(x):
    return jax.nn.silu(x)

def _sigmoid(x):
    return jax.nn.sigmoid(x)

def _layernorm(x, axis=-1, eps=1e-05):
    m = jnp.mean(x, axis=axis, keepdims=True)
    v = jnp.var(x, axis=axis, keepdims=True)
    return (x - m) / jnp.sqrt(v + eps)

def _scatter_add(tgt, idx, src, axis=0):
    return tgt.at[idx].add(src)

def _segment_sum(src, seg, n):
    return jax.ops.segment_sum(src, seg, n)
kernel_name = 'mk_macaron_d1_jaxref_r8_7931ac'

def setup_inputs(seed: int=0):
    np.random.seed(seed)
    _w = jnp.asarray

    def _L0_attn_setup():
        import jax, jax.numpy as jnp
        import numpy as np
        B, T, D, H, LORA = (4, 128, 128, 16, 64)
        HD = D // H
        BLOCK_ID, N_BLOCKS = (6, 12)

        def _ln(x, w, b, eps=1e-05):
            m = x.mean(-1, keepdims=True)
            v = ((x - m) ** 2).mean(-1, keepdims=True)
            return (x - m) * jax.lax.rsqrt(v + eps) * w + b

        def _lora(z, a, b, l):
            return l + jnp.tanh(z @ a.T) @ b.T

        def _reference_tuple_inner(x, xw, rW, kW, vW, gW, r_la, r_lb, r_ll, k_la, k_lb, k_ll, v_la, v_lb, v_ll, g_la, g_lb, g_ll, d_la, d_lb, d_ll, ln_w, ln_b, oW, init_state, u):
            b, t, d = x.shape
            h = init_state.shape[0]
            hd = d // h
            xx = jnp.concatenate([jnp.zeros_like(x[:, :1]), x[:, :-1]], axis=1)
            dx = xx - x
            lerpx = x + dx * xw
            r = (x + dx * _lora(lerpx, r_la, r_lb, r_ll)) @ rW.T
            k = (x + dx * _lora(lerpx, k_la, k_lb, k_ll)) @ kW.T
            v = (x + dx * _lora(lerpx, v_la, v_lb, v_ll)) @ vW.T
            g = (x + dx * _lora(lerpx, g_la, g_lb, g_ll)) @ gW.T
            w = jnp.exp(-jnp.exp(_lora(x + dx * _lora(lerpx, d_la, d_lb, d_ll), d_la, d_lb, d_ll)))
            split = lambda z: z.reshape(b, t, h, hd).transpose(1, 0, 2, 3)
            rs, ws, ks, vs = (split(r), split(w), split(k), split(v))
            uh = u.reshape(h, hd)
            st0 = jnp.broadcast_to(init_state, (b, h, hd, hd))

            def step(st, inp):
                rt, wt, kt, vt = inp
                kv = jnp.einsum('bhi,bhj->bhij', kt, vt)
                y = jnp.einsum('bhi,bhij->bhj', rt, st + uh[None, :, :, None] * kv)
                return (wt[..., None] * st + kv, y)
            st1, ys = jax.lax.scan(step, st0, (rs, ws, ks, vs))
            o = jax.nn.silu(g.reshape(b, t, h, hd)) * _ln(ys.transpose(1, 0, 2, 3), ln_w, ln_b)
            return (o.reshape(b, t, d) @ oW.T, st1)
        key = jax.random.key(seed)
        ks = iter(jax.random.split(key, 64))
        rn = lambda shape, s: jax.random.normal(next(ks), shape, jnp.float32) * s
        inp = {}
        inp['x'] = rn((B, T, D), 1.0)
        r1 = 1.0 - BLOCK_ID / N_BLOCKS
        i = np.arange(D)
        inp['xw'] = jnp.asarray(1.0 - (i / D) ** r1, jnp.float32)
        for nm in ('rW', 'kW', 'vW', 'gW'):
            inp[nm] = rn((D, D), 0.02)
        for p in ('r', 'k', 'v', 'g', 'd'):
            inp[p + '_la'] = rn((LORA, D), 0.001)
            inp[p + '_lb'] = rn((D, LORA), 0.001)
            inp[p + '_ll'] = rn((D,), 1.0)
        inp['ln_w'] = jnp.full((HD,), ((1 + BLOCK_ID) / N_BLOCKS) ** 0.7, jnp.float32)
        inp['ln_b'] = jnp.zeros((HD,), jnp.float32)
        inp['oW'] = rn((D, D), 0.02)
        inp['init_state'] = rn((H, HD, HD), 1.0)
        r0 = BLOCK_ID / (N_BLOCKS - 1)
        ih = i % HD
        inp['u'] = jnp.asarray(r0 * (1 - ih / (D - 1)) + np.remainder(0.1 * (ih + 1), 3.0), jnp.float32)
        return inp
    _L0_attn_in = _L0_attn_setup()

    def _L0_ffn_setup():
        import jax, jax.numpy as jnp
        import numpy as np
        NUM_EXPERTS = 8
        CAP_FACTOR = 1.0
        MIN_CAP = 8
        key = jax.random.key(seed)
        ks = jax.random.split(key, 10)
        G, S, D, H, E = (4, 512, 128, 512, NUM_EXPERTS)
        s = 0.02
        return {'x': jax.random.normal(ks[0], (G, S, D), dtype=jnp.float32), 'gate': jax.random.normal(ks[1], (D, E), dtype=jnp.float32) * s, 'W1': jax.random.normal(ks[2], (E, D, H), dtype=jnp.float32) * s, 'b1': jnp.zeros((E, H), dtype=jnp.float32), 'W2': jax.random.normal(ks[3], (E, H, D), dtype=jnp.float32) * s, 'b2': jnp.zeros((E, D), dtype=jnp.float32), 'Ws1': jax.random.normal(ks[4], (D, H), dtype=jnp.float32) * s, 'bs1': jnp.zeros((H,), dtype=jnp.float32), 'Ws2': jax.random.normal(ks[5], (H, D), dtype=jnp.float32) * s, 'bs2': jnp.zeros((D,), dtype=jnp.float32)}
    _L0_ffn_in = _L0_ffn_setup()
    _d = {'L0_attn_x': _L0_attn_in['x'], 'L0_attn_xw': _L0_attn_in['xw'], 'L0_attn_rW': _L0_attn_in['rW'], 'L0_attn_kW': _L0_attn_in['kW'], 'L0_attn_vW': _L0_attn_in['vW'], 'L0_attn_gW': _L0_attn_in['gW'], 'L0_attn_r_la': _L0_attn_in['r_la'], 'L0_attn_r_lb': _L0_attn_in['r_lb'], 'L0_attn_r_ll': _L0_attn_in['r_ll'], 'L0_attn_k_la': _L0_attn_in['k_la'], 'L0_attn_k_lb': _L0_attn_in['k_lb'], 'L0_attn_k_ll': _L0_attn_in['k_ll'], 'L0_attn_v_la': _L0_attn_in['v_la'], 'L0_attn_v_lb': _L0_attn_in['v_lb'], 'L0_attn_v_ll': _L0_attn_in['v_ll'], 'L0_attn_g_la': _L0_attn_in['g_la'], 'L0_attn_g_lb': _L0_attn_in['g_lb'], 'L0_attn_g_ll': _L0_attn_in['g_ll'], 'L0_attn_d_la': _L0_attn_in['d_la'], 'L0_attn_d_lb': _L0_attn_in['d_lb'], 'L0_attn_d_ll': _L0_attn_in['d_ll'], 'L0_attn_ln_w': _L0_attn_in['ln_w'], 'L0_attn_ln_b': _L0_attn_in['ln_b'], 'L0_attn_oW': _L0_attn_in['oW'], 'L0_attn_init_state': _L0_attn_in['init_state'], 'L0_attn_u': _L0_attn_in['u'], 'L0_ffn_gate': _L0_ffn_in['gate'], 'L0_ffn_W1': _L0_ffn_in['W1'], 'L0_ffn_b1': _L0_ffn_in['b1'], 'L0_ffn_W2': _L0_ffn_in['W2'], 'L0_ffn_b2': _L0_ffn_in['b2'], 'L0_ffn_Ws1': _L0_ffn_in['Ws1'], 'L0_ffn_bs1': _L0_ffn_in['bs1'], 'L0_ffn_Ws2': _L0_ffn_in['Ws2'], 'L0_ffn_bs2': _L0_ffn_in['bs2']}
    _x0 = _d['L0_attn_x']
    _d['L0_attn_x'] = jax.random.normal(jax.random.fold_in(jax.random.key(seed), 1), (8, 1024, 128), dtype=_x0.dtype)
    del _x0
    return _d

def reference(L0_attn_x, L0_attn_xw, L0_attn_rW, L0_attn_kW, L0_attn_vW, L0_attn_gW, L0_attn_r_la, L0_attn_r_lb, L0_attn_r_ll, L0_attn_k_la, L0_attn_k_lb, L0_attn_k_ll, L0_attn_v_la, L0_attn_v_lb, L0_attn_v_ll, L0_attn_g_la, L0_attn_g_lb, L0_attn_g_ll, L0_attn_d_la, L0_attn_d_lb, L0_attn_d_ll, L0_attn_ln_w, L0_attn_ln_b, L0_attn_oW, L0_attn_init_state, L0_attn_u, L0_ffn_gate, L0_ffn_W1, L0_ffn_b1, L0_ffn_W2, L0_ffn_b2, L0_ffn_Ws1, L0_ffn_bs1, L0_ffn_Ws2, L0_ffn_bs2):

    def _L0_attn_ref(x, xw, rW, kW, vW, gW, r_la, r_lb, r_ll, k_la, k_lb, k_ll, v_la, v_lb, v_ll, g_la, g_lb, g_ll, d_la, d_lb, d_ll, ln_w, ln_b, oW, init_state, u):
        import jax, jax.numpy as jnp
        import numpy as np
        B, T, D, H, LORA = (4, 128, 128, 16, 64)
        HD = D // H
        BLOCK_ID, N_BLOCKS = (6, 12)

        def _ln(x, w, b, eps=1e-05):
            m = x.mean(-1, keepdims=True)
            v = ((x - m) ** 2).mean(-1, keepdims=True)
            return (x - m) * jax.lax.rsqrt(v + eps) * w + b

        def _lora(z, a, b, l):
            return l + jnp.tanh(z @ a.T) @ b.T

        def _reference_tuple_inner(x, xw, rW, kW, vW, gW, r_la, r_lb, r_ll, k_la, k_lb, k_ll, v_la, v_lb, v_ll, g_la, g_lb, g_ll, d_la, d_lb, d_ll, ln_w, ln_b, oW, init_state, u):
            b, t, d = x.shape
            h = init_state.shape[0]
            hd = d // h
            xx = jnp.concatenate([jnp.zeros_like(x[:, :1]), x[:, :-1]], axis=1)
            dx = xx - x
            lerpx = x + dx * xw
            r = (x + dx * _lora(lerpx, r_la, r_lb, r_ll)) @ rW.T
            k = (x + dx * _lora(lerpx, k_la, k_lb, k_ll)) @ kW.T
            v = (x + dx * _lora(lerpx, v_la, v_lb, v_ll)) @ vW.T
            g = (x + dx * _lora(lerpx, g_la, g_lb, g_ll)) @ gW.T
            w = jnp.exp(-jnp.exp(_lora(x + dx * _lora(lerpx, d_la, d_lb, d_ll), d_la, d_lb, d_ll)))
            split = lambda z: z.reshape(b, t, h, hd).transpose(1, 0, 2, 3)
            rs, ws, ks, vs = (split(r), split(w), split(k), split(v))
            uh = u.reshape(h, hd)
            st0 = jnp.broadcast_to(init_state, (b, h, hd, hd))

            def step(st, inp):
                rt, wt, kt, vt = inp
                kv = jnp.einsum('bhi,bhj->bhij', kt, vt)
                y = jnp.einsum('bhi,bhij->bhj', rt, st + uh[None, :, :, None] * kv)
                return (wt[..., None] * st + kv, y)
            st1, ys = jax.lax.scan(step, st0, (rs, ws, ks, vs))
            o = jax.nn.silu(g.reshape(b, t, h, hd)) * _ln(ys.transpose(1, 0, 2, 3), ln_w, ln_b)
            return (o.reshape(b, t, d) @ oW.T, st1)
        return _reference_tuple_inner(x, xw, rW, kW, vW, gW, r_la, r_lb, r_ll, k_la, k_lb, k_ll, v_la, v_lb, v_ll, g_la, g_lb, g_ll, d_la, d_lb, d_ll, ln_w, ln_b, oW, init_state, u)[0]

    def _L0_ffn_ref(x, gate, W1, b1, W2, b2, Ws1, bs1, Ws2, bs2):
        import jax, jax.numpy as jnp
        import numpy as np
        NUM_EXPERTS = 8
        CAP_FACTOR = 1.0
        MIN_CAP = 8
        G, S, D = x.shape
        E = gate.shape[1]
        T = G * S
        capacity = max(MIN_CAP, int(CAP_FACTOR * T / E))
        logits = jnp.einsum('gsd,de->gse', x, gate)
        probs = jax.nn.softmax(logits, axis=-1)
        flat_probs = probs.transpose(2, 0, 1).reshape(E, T)
        scores, token_idx = jax.lax.top_k(flat_probs, k=capacity)
        scores = jnp.where(scores > -100000000.0, scores, 0.0)
        flat_x = x.reshape(T, D)
        tok = flat_x[token_idx]
        h = jax.nn.gelu(jnp.einsum('ecd,edh->ech', tok, W1) + b1[:, None, :])
        out_tok = jnp.einsum('ech,ehd->ecd', h, W2) + b2[:, None, :]
        scaled = out_tok * scores[..., None]
        routed = jnp.zeros_like(flat_x).at[token_idx.reshape(-1)].add(scaled.reshape(E * capacity, D)).reshape(G, S, D)
        shared = jax.nn.gelu(jnp.einsum('gsd,dh->gsh', x, Ws1) + bs1)
        shared = jnp.einsum('gsh,hd->gsd', shared, Ws2) + bs2
        return routed + shared
    x = L0_attn_x
    x = x + 0.5 * _L0_ffn_ref(_layernorm(x, axis=-1), L0_ffn_gate, L0_ffn_W1, L0_ffn_b1, L0_ffn_W2, L0_ffn_b2, L0_ffn_Ws1, L0_ffn_bs1, L0_ffn_Ws2, L0_ffn_bs2)
    x = x + _L0_attn_ref(_layernorm(x, axis=-1), L0_attn_xw, L0_attn_rW, L0_attn_kW, L0_attn_vW, L0_attn_gW, L0_attn_r_la, L0_attn_r_lb, L0_attn_r_ll, L0_attn_k_la, L0_attn_k_lb, L0_attn_k_ll, L0_attn_v_la, L0_attn_v_lb, L0_attn_v_ll, L0_attn_g_la, L0_attn_g_lb, L0_attn_g_ll, L0_attn_d_la, L0_attn_d_lb, L0_attn_d_ll, L0_attn_ln_w, L0_attn_ln_b, L0_attn_oW, L0_attn_init_state, L0_attn_u)
    x = x + 0.5 * _L0_ffn_ref(_layernorm(x, axis=-1), L0_ffn_gate, L0_ffn_W1, L0_ffn_b1, L0_ffn_W2, L0_ffn_b2, L0_ffn_Ws1, L0_ffn_bs1, L0_ffn_Ws2, L0_ffn_bs2)
    return x

_drawn_inputs = setup_inputs


def setup_inputs(seed=0):
    import zlib

    import numpy as np

    out = dict(_drawn_inputs(seed))
    spreads = {'L0_attn_ln_w': (0.6857119798660278, 0.6),
     'L0_attn_ln_b': (0.0, 0.8),
     'L0_ffn_b1': (0.0, 0.8),
     'L0_ffn_b2': (0.0, 0.469),
     'L0_ffn_bs1': (0.0, 0.371),
     'L0_ffn_bs2': (0.0, 0.1)}
    factors = {'L0_attn_xw': 55.013,
     'L0_attn_r_la': 54.886,
     'L0_attn_r_lb': 54.301,
     'L0_attn_k_la': 64.0,
     'L0_attn_k_lb': 64.0,
     'L0_attn_v_la': 64.0,
     'L0_attn_v_lb': 64.0,
     'L0_attn_g_la': 60.824,
     'L0_attn_g_lb': 63.974,
     'L0_attn_d_la': 64.0,
     'L0_attn_d_lb': 64.0,
     'L0_attn_d_ll': 3.91,
     'L0_attn_init_state': 8.0,
     'L0_attn_u': 8.0,
     'L0_ffn_gate': 3.016,
     'L0_ffn_W1': 6.08,
     'L0_ffn_W2': 5.539}
    for name, (base, spread) in spreads.items():
        noise = np.random.default_rng([zlib.crc32(name.encode()), seed]).standard_normal(out[name].shape)
        drawn = base * np.exp(spread * noise) if base else spread * noise
        out[name] = jnp.asarray(drawn.astype(out[name].dtype))
    for name, factor in factors.items():
        out[name] = (out[name] * factor).astype(out[name].dtype)
    return out
```

```python
from contextlib import ExitStack

import numpy as np

import concourse.bass as bass
from concourse import mybir

F32 = mybir.dt.float32
I32 = mybir.dt.int32
BF16 = mybir.dt.bfloat16
ALU = mybir.AluOpType
ACT = mybir.ActivationFunctionType
AX_X = mybir.AxisListType.X

P = 128
D = 128
NSEQ, SEQ = 8, 1024
T = NSEQ * SEQ
TILE = 512
CH = TILE // P
NT = T // TILE
E = 8
HID = 512
HK = HID // P
CAP = T // E
SLOTS = CAP // P
HEADS, HD = 16, 8
LORA = 64
EPS = 1e-5
ROW = D + E
TOP_BIT = 30
GROUP = 16


def ge(eng, sem, count):
    if isinstance(count, int) and count <= 0:
        return
    eng.wait_ge(sem, count)


def pipelined(eng, n, lag, body, ways=2):
    first = ways * -(-(lag + ways) // ways)
    for i in range(first):
        body(i, i % ways, lambda k, i=i: 0 <= i - k < n)
    with eng.Fori(first, n - ways + 1, ways) as i:
        for m in range(ways):
            body(i + m, m, lambda k: True)
    for i in range(n, n + lag):
        body(i, i % ways, lambda k, i=i: 0 <= i - k < n)


def setup_block(nc, c, src):
    with ExitStack() as ctx:
        pi = ctx.enter_context(nc.sbuf_tensor("pi", [P, 1], I32))
        pmi = ctx.enter_context(nc.sbuf_tensor("pmi", [P, 2], I32))
        pmf = ctx.enter_context(nc.sbuf_tensor("pmf", [P, 2], F32))
        col = ctx.enter_context(nc.sbuf_tensor("col", [P, 2, P], F32))
        iotas = ctx.enter_context(nc.semaphore("iotas"))
        zeroed = ctx.enter_context(nc.semaphore("zeroed"))
        mods = ctx.enter_context(nc.semaphore("mods"))
        block = ctx.enter_context(nc.Block())

        @block.gpsimd
        def _(pool):
            some = {"allow_small_or_imprecise_dtypes": True}
            pool.iota(pi[:, :], pattern=[[0, 1]], base=0, channel_multiplier=1).then_inc(iotas, 1)
            pool.iota(col[:, 0, :], pattern=[[0, NT], [1, E]], base=0, channel_multiplier=0, **some).then_inc(iotas, 1)
            pool.iota(col[:, 1, :], pattern=[[1, NT], [0, E]], base=0, channel_multiplier=0, **some).then_inc(iotas, 1)
            pool.iota(c.part[:, :], pattern=[[0, 1]], base=0, channel_multiplier=1, **some)
            pool.iota(c.count128[:, :], pattern=[[1, P]], base=0, channel_multiplier=0, **some)
            pool.iota(c.count8[:, :], pattern=[[1, SLOTS]], base=0, channel_multiplier=0, **some)
            pool.iota(c.chunk_of[:, :], pattern=[[1, CH], [CH, NT], [0, E]], base=0, channel_multiplier=0, **some)
            pool.memset(c.minus_half[:, :], -0.5)
            pool.memset(c.ident[:, :], 0.0).then_inc(zeroed, 1)
            pool.wait_ge(zeroed, 1)
            pool.affine_select(out=c.ident[:, :], in_=c.ident[:, :], compare_op=ALU.not_equal, fill=1.0,
                               base=0, pattern=[[-1, P]], channel_multiplier=1)

        @block.vector
        def _(dve):
            dve.wait_ge(iotas, 3)
            dve.tensor_scalar(pmi[:, 0:1], pi[:, :], E - 1, None, ALU.bitwise_and).then_inc(mods, 1)
            dve.tensor_scalar(pmi[:, 1:2], pi[:, :], 3, None, ALU.arith_shift_right).then_inc(mods, 1)
            dve.wait_ge(mods, 2)
            dve.tensor_copy(pmf[:, :], pmi[:, :]).then_inc(mods, 1)
            dve.wait_ge(mods, 3)
            dve.tensor_scalar(c.same_e[:, :], col[:, 0, :], pmf[:, 0:1], None, ALU.is_equal).then_inc(mods, 1)
            dve.wait_ge(mods, 4)
            dve.scalar_tensor_tensor(c.earlier[:, :], col[:, 1, :], pmf[:, 1:2], c.same_e[:, :],
                                     ALU.is_gt, ALU.mult).then_inc(mods, 1)


def clear_semaphores(nc, c):
    nc.clear_and_free_semaphores(c.sems)
    nc.all_engine_barrier()
    c.sems = []


def ffn_block(nc, c, X, x_dram, w, table, acc, tag):
    W1d, b1d, W2d, b2d, gated, Ws1d, bs1d, Ws2d, bs2d = w
    with ExitStack() as ctx:
        def sb(name, shape, dt=F32):
            return ctx.enter_context(nc.sbuf_tensor(name + tag, shape, dt))

        def ps(name, shape):
            return ctx.enter_context(nc.psum_tensor(name + tag, shape, F32))

        def sem(name):
            c.sems.append(nc.alloc_semaphore(name=name + tag))
            return c.sems[-1]

        ps_t = ps("ps_t", [P, 2, TILE])
        ps_h = ps("ps_h", [P, HK, TILE])
        ps_o = ps("ps_o", [P, 2, CH, D])

        gate = sb("gate", [P, E])
        ws1 = sb("ws1", [P, HID])
        ws2 = sb("ws2", [P, HK, D])
        bs1 = sb("bs1", [P, HK])
        bs2 = sb("bs2", [P, D])
        half_bs2 = sb("half_bs2", [P, D])
        b1 = sb("b1", [P, E, HK])
        we1 = sb("we1", [P, 2, HID])
        we2 = sb("we2", [P, 2, HK, D])
        b2 = sb("b2", [P, 2, D])

        XT = sb("XT", [P, NT * TILE])
        XTs = sb("XTs", [P, 2, TILE])
        XN = sb("XN", [P, 4, CH, ROW])
        st = sb("st", [P, 2, CH, 6])
        mv = sb("mv", [P, 2, CH, 2])
        ve = sb("ve", [P, 2, CH])
        rstd = sb("rstd", [P, 2, CH])
        mx = sb("mx", [P, 2, CH])
        lg = sb("lg", [P, 2, CH, E])
        ex = sb("ex", [P, 2, CH, E])
        sm = sb("sm", [P, 2, CH])
        rs = sb("rs", [P, 2, CH])
        probs = sb("probs", [P, CH, NT * E])

        hS = sb("hS", [P, 2, HK, TILE])

        PT = sb("PT", [P, TILE])
        hit = sb("hit", [P, TILE], BF16)
        thr = sb("thr", [P, 1], I32)
        bit = sb("bit", [P, 1], I32)
        cand = sb("cand", [P, 1], I32)
        keep = sb("keep", [P, 2], I32)
        cnt = sb("cnt", [P, 1])
        ties = sb("ties", [P, 2])
        more = sb("more", [P, TILE])
        same = sb("same", [P, TILE])
        rank = sb("rank", [P, TILE])
        limit = sb("limit", [P, 2])
        taken = sb("taken", [P, TILE])
        order = sb("order", [P, TILE])
        slot = sb("slot", [P, TILE])
        slot_i = sb("slot_i", [P, TILE], I32)
        hi_i = sb("hi_i", [P, TILE], I32)
        lo_i = sb("lo_i", [P, TILE], I32)
        hi_f = sb("hi_f", [P, TILE])
        lo_f = sb("lo_f", [P, TILE])
        lo_hot = sb("lo_hot", [P, TILE, SLOTS], BF16)
        ids = sb("ids", [P, TILE, 2, SLOTS], BF16)
        hi_hot = sb("hi_hot", [P, CH, GROUP, P], BF16)
        hi_last = sb("hi_last", [P, GROUP])
        tok_f = sb("tok_f", [P, 2 * SLOTS])
        tok = sb("tok", [P, E * SLOTS], I32)
        tok_s = sb("tok_s", [P, 2, SLOTS], I32)

        G = sb("G", [P, 4, CH, ROW])
        GT = sb("GT", [P, 2, TILE])
        score = sb("score", [P, 2, CH])
        Y = sb("Y", [P, 2, CH, D])

        weights = sem("weights")
        passed = sem("passed")
        x_in = [sem("x_in0"), sem("x_in1")]
        var = sem("var"); varE = sem("varE"); rstd_s = sem("rstd_s"); stats = sem("stats")
        xn = sem("xn"); xt_ps = sem("xt_ps"); xt = sem("xt"); xt_big = sem("xt_big")
        logit = sem("logit"); mxs = sem("mxs"); shifted = sem("shifted"); expd = sem("expd")
        summed = sem("summed"); inv = sem("inv"); prob = sem("prob"); prob_kept = sem("prob_kept")
        stored = [sem("stored%d" % n) for n in range(4)]
        hid = sem("hid"); act_s = sem("act_s"); outp = sem("outp"); xb = sem("xb"); x1 = sem("x1")
        halfb = sem("halfb")
        acc_in = [sem("acc_in0"), sem("acc_in1")]
        pt_ps = sem("pt_ps"); pt = sem("pt"); srch = sem("srch"); counted = sem("counted"); total = sem("total")
        sel = sem("sel"); selp = sem("selp"); listed = sem("listed")
        hot = [sem("hot%d" % g) for g in range(CH)]
        hot_used = sem("hot_used"); hi_copied = sem("hi_copied"); tok_ps = sem("tok_ps"); tokf = sem("tokf"); tok_s_ = sem("tok_s_")
        toks = sem("toks")
        gath = [sem("gath%d" % g) for g in range(4)]
        scat = sem("scat")
        ew = [sem("ew0"), sem("ew1")]
        gt_ps = sem("gt_ps"); gt = sem("gt"); eh = sem("eh"); eact = sem("eact"); eo = sem("eo")
        sc = sem("sc"); ytmp = sem("ytmp"); y = sem("y")

        block = ctx.enter_context(nc.Block())

        def xtile(t):
            return X[:, bass.ds(t * TILE, TILE)].rearrange("p (c d) -> p c d", c=CH)

        def tokens(dram, t, width):
            return dram[bass.ds(t * TILE, TILE), :].rearrange("(c p) d -> p c d", p=P)

        R_W = 16 * 9

        def alone(eng, *waits):
            for s, n in waits:
                ge(eng, s, n)
                eng.sem_inc(passed, 1)

        def b1_flat(e, k):
            return b1[:, :, :].rearrange("p e k -> p (e k)")[:, bass.ds(e * HK + k, 1)]

        def ids_flat(m):
            return ids[:, :, :, :].rearrange("p t a s -> p (t a s)")[:, bass.ds(m * (2 * SLOTS), 2 * SLOTS)]

        def wide(tile, q):
            return tile[:, q, :].rearrange("p (c a) -> p c a", a=1).to_broadcast([P, CH, E])

        def one_hot_group(e, g):
            nc.vector.wait_ge(listed, 1)
            ge(nc.vector, hot_used, (e - 1) * CH + (g + 1))
            for n in range(GROUP):
                op = nc.vector.tensor_scalar(hi_hot[:, g, n, :], c.count128[:, :],
                                             hi_f[:, bass.ds(e + (g * P + n * E), 1)], None, ALU.is_equal)
            op.then_inc(hot[g], 1)

        def one_hot_last(e):
            g = CH - 1
            alone(nc.gpsimd, (listed, 1), (hot_used, e * CH))
            nc.gpsimd.tensor_copy(hi_last[:, :].rearrange("p (n a) -> p n a", a=1),
                                  hi_f[:, g * P:(g + 1) * P].rearrange("p (n e) -> p n e", e=E)[:, :, bass.ds(e, 1)]
                                  ).then_inc(hi_copied, 1)
            alone(nc.gpsimd, (hi_copied, e + 1))
            for n in range(GROUP):
                op = nc.gpsimd.tensor_scalar(hi_hot[:, g, n, :], c.count128[:, :], hi_last[:, n:n + 1], None,
                                             ALU.is_equal)
            op.then_inc(hot[g], 1)

        @block.sync
        def _(sp):
            if x_dram is not None:
                for t in range(2):
                    sp.dma_start(xtile(t), tokens(x_dram, t, D)).then_inc(x_in[t], 16)
            sp.dma_start(gate[:, :], gated).then_inc(weights, 16)
            sp.dma_start(ws1[:, :], Ws1d).then_inc(weights, 16)
            sp.dma_start(ws2[:, :, :], Ws2d.rearrange("(k p) d -> p k d", p=P)).then_inc(weights, 16)
            sp.dma_start(bs2[:, :], bs2d.rearrange("(a d) -> a d", a=1).to_broadcast([P, D])).then_inc(weights, 16)
            with nc.allow_non_contiguous_dma("biases onto partitions, small"):
                for k in range(HK):
                    sp.dma_start(bs1[:, k:k + 1], bs1d[k * P:(k + 1) * P].rearrange("(p a) -> p a", a=1)).then_inc(weights, 16)
                sp.dma_start(b1[:, :, :], b1d.rearrange("e (k p) -> p (e k)", p=P).rearrange("p (e k) -> p e k", e=E)).then_inc(weights, 16)
            if x_dram is not None:
                with sp.Fori(2, NT - 1, 2) as t:
                    for p in range(2):
                        alone(sp, (x_in[p], t * 8))
                        sp.dma_start(xtile(t + p), tokens(x_dram, t + p, D)).then_inc(x_in[p], 16)

            def store_rows(i, p, live):
                if live(0):
                    alone(sp, (prob, i + 1), (stored[p], (i - p) * 4))
                    sp.dma_start(tokens(table, i, ROW), XN[:, p, :, :]).then_inc(stored[p], 16)

            pipelined(sp, NT, 0, store_rows, 4)

            def store_acc(i, p, live):
                if live(0):
                    alone(sp, (x1, i + 1), (acc_in[p], (i - p) * 8))
                    sp.dma_start(tokens(acc, i, D), xtile(i)).then_inc(acc_in[p], 16)

            pipelined(sp, NT, 0, store_acc)

            def load_expert(e, s, used):
                if used:
                    alone(sp, (ytmp, (e - 1) * 2))
                sp.dma_start(we1[:, s, :], W1d[bass.ds(e * D, D), :]).then_inc(ew[s], 16)
                sp.dma_start(we2[:, s, :, :], W2d[bass.ds(e * HID, HID), :].rearrange("(k p) d -> p k d", p=P)).then_inc(ew[s], 16)
                sp.dma_start(b2[:, s, :], b2d[bass.ds(e, 1), :].to_broadcast([P, D])).then_inc(ew[s], 16)

            for e in range(2):
                load_expert(e, e, False)
            with sp.Fori(2, E - 1, 2) as e:
                for s in range(2):
                    load_expert(e + s, s, True)
            for p in range(2):
                sp.wait_ge(acc_in[p], 8 * NT)
            for p in range(4):
                sp.wait_ge(stored[p], 4 * NT)
            sp.wait_ge(scat, 16 * E * SLOTS)

        @block.gpsimd
        def _(pool):
            def route(i, m, live):
                p = m % 2
                if live(0):
                    ge(pool, varE, i + 1)
                    if live(2):
                        ge(pool, xn, i - 1)
                    pool.tensor_tensor(rstd[:, p, :], ve[:, p, :], c.minus_half[:, :].to_broadcast([P, CH]),
                                       ALU.pow).then_inc(rstd_s, 1)
                if live(2):
                    t = i - 2
                    alone(pool, (xt, t + 1))
                    pool.tensor_copy(XT[:, bass.ds(t * TILE, TILE)], XTs[:, p, :]).then_inc(xt_big, 1)
                if live(3):
                    t, q = i - 3, 1 - p
                    alone(pool, (prob, t + 1))
                    pool.tensor_copy(probs[:, :, bass.ds(t * E, E)], XN[:, (m - 3) % 4, :, D:ROW]).then_inc(prob_kept, 1)

            pipelined(pool, NT, 3, route, 4)
            pool.wait_ge(weights, R_W)
            pool.tensor_scalar(half_bs2[:, :], bs2[:, :], 0.5, None, ALU.mult).then_inc(halfb, 1)
            pool.wait_ge(halfb, 1)

            def add_bias(t):
                pool.tensor_tensor(xtile(t), xtile(t),
                                   half_bs2[:, :].rearrange("p (a d) -> p a d", a=1).to_broadcast([P, CH, D]),
                                   ALU.add).then_inc(xb, 1)

            pool.wait_ge(xn, NT)
            with pool.Fori(0, NT) as t:
                add_bias(t)

            pool.wait_ge(listed, 1)
            one_hot_last(0)
            with pool.Fori(1, E) as e:
                one_hot_last(e)

            pool.wait_ge(acc_in[0], 8 * NT)
            pool.wait_ge(acc_in[1], 8 * NT)
            for p in range(4):
                pool.wait_ge(stored[p], 4 * NT)

            def gather(e, s, half, first):
                g = 2 * s + half
                if half == 0:
                    alone(pool, (toks, e + 1), *([] if first else [(scat, (e - 1) * (16 * SLOTS))]))
                    pool.tensor_copy(tok_s[:, s, :], tok[:, bass.ds(e * SLOTS, SLOTS)]).then_inc(tok_s_, 1)
                alone(pool, (tok_s_, e + 1),
                      *([] if first else [(gt_ps, e * 2 + (half - 3)), (sc, e * 2 + (half - 3))]))
                for j in range(CH):
                    pool.indirect_dma_start(
                        G[:, g, j, :], None, table[:, :],
                        bass.IndirectOffsetOnAxis(ap=tok_s[:, s, half * CH + j:half * CH + j + 1], axis=0),
                    ).then_inc(gath[g], 16)

            def scatter(e, s, half):
                alone(pool, (y, e * 2 + (half + 1)), *([(scat, e * (16 * SLOTS))] if half == 0 else []))
                for j in range(CH):
                    pool.indirect_dma_start(
                        acc[:, :],
                        bass.IndirectOffsetOnAxis(ap=tok_s[:, s, half * CH + j:half * CH + j + 1], axis=0),
                        Y[:, half, j, :], None, compute_op=ALU.add,
                    ).then_inc(scat, 16)

            gather(0, 0, 0, True)
            gather(0, 0, 1, True)
            gather(1, 1, 0, True)
            scatter(0, 0, 0)
            gather(1, 1, 1, True)
            scatter(0, 0, 1)
            with pool.Fori(2, E - 1, 2) as e:
                gather(e, 0, 0, False)
                scatter(e - 1, 1, 0)
                gather(e, 0, 1, False)
                scatter(e - 1, 1, 1)
                gather(e + 1, 1, 0, False)
                scatter(e, 0, 0)
                gather(e + 1, 1, 1, False)
                scatter(e, 0, 1)
            scatter(E - 1, 1, 0)
            scatter(E - 1, 1, 1)

        @block.scalar
        def _(act):
            def route(i, p, live):
                if live(1):
                    t, q = i - 1, 1 - p
                    ge(act, xt_ps, t + 1)
                    ge(act, xt_big, t - 1)
                    ge(act, logit, t - 1)
                    act.copy(XTs[:, q, :], ps_t[:, q, :]).then_inc(xt, 1)
                if live(3):
                    t, q = i - 3, 1 - p
                    ge(act, shifted, t + 1)
                    ge(act, prob, t - 1)
                    act.activation(ex[:, q, :, :], lg[:, q, :, :], ACT.Exp).then_inc(expd, 1)

            pipelined(act, NT, 3, route)

            def hidden(i, p, live):
                if live(0):
                    for k in range(HK):
                        ge(act, hid, i * HK + k + 1)
                        if k == 0:
                            ge(act, outp, i - 1)
                        act.activation(hS[:, p, k, :], ps_h[:, k, :], ACT.Gelu_apprx_tanh,
                                       bias=bs1[:, k:k + 1]).then_inc(act_s, 1)

            pipelined(act, NT, 0, hidden)

            def expert_hidden(i, p, e, half):
                for k in range(HK):
                    alone(act, (eh, i * HK + k + 1), *([(eo, i - 1)] if k == 0 else []))
                    act.activation(hS[:, p, k, :], ps_h[:, k, :], ACT.Gelu_apprx_tanh,
                                   bias=b1_flat(e, k)).then_inc(eact, 1)

            for i in range(2):
                expert_hidden(i, i, i // 2, i % 2)
            with act.Fori(1, E) as e:
                for half in range(2):
                    expert_hidden(e * 2 + half, half, e, half)

        @block.tensor
        def _(pe):
            pe.wait_ge(weights, R_W)

            def route(i, m, live):
                p = m % 2
                if live(0):
                    ge(pe, xn, i + 1)
                    ge(pe, xt, i - 1)
                    for n in range(CH):
                        op = pe.transpose(ps_t[:, p, n * P:(n + 1) * P], XN[:, m, n, 0:D], c.ident[:, :])
                    op.then_inc(xt_ps, 1)
                if live(1):
                    t, q = i - 1, 1 - p
                    ge(pe, xt, t + 1)
                    ge(pe, shifted, t - 1)
                    for n in range(CH):
                        op = pe.matmul(ps_o[:, q, 0, n * E:(n + 1) * E], XTs[:, q, n * P:(n + 1) * P], gate[:, :],
                                       start=True, stop=True)
                    op.then_inc(logit, 1)

            pipelined(pe, NT, 1, route, 4)

            pe.wait_ge(prob_kept, NT)
            for b in range(CH):
                op = pe.transpose(ps_t[:, 0, b * P:(b + 1) * P], probs[:, b, :], c.ident[:, :])
            op.then_inc(pt_ps, 1)

            def shared(i, p, live, slots):
                if live(0):
                    for k in range(HK):
                        ge(pe, act_s, i * HK + k + 1 - HK)
                        if k == 0:
                            ge(pe, xt_big, NT)
                        pe.matmul(ps_h[:, k, :], ws1[:, k * P:(k + 1) * P], XT[:, bass.ds(i * TILE, TILE)],
                                  start=True, stop=True).then_inc(hid, 1)
                        if k % 2 == 1:
                            slots(i, k // 2)
                if live(1):
                    t, q = i - 1, 1 - p
                    ge(pe, act_s, t * HK + HK)
                    ge(pe, x1, t - 1)
                    if isinstance(t, int) and t == 0:
                        pe.wait_ge(shifted, NT)
                    for n in range(CH):
                        for k in range(HK):
                            op = pe.matmul(ps_o[:, q, n, :], hS[:, q, k, n * P:(n + 1) * P], ws2[:, k, :],
                                           start=(k == 0), stop=(k == HK - 1))
                        if n == CH - 1:
                            op.then_inc(outp, 1)
                        if n % 2 == 1:
                            slots(i, 2 + n // 2)

            def count_all(i, s):
                ge(pe, counted, i * 4 + s + 1)
                pe.matmul(ps_t[:, 1, 0:1], c.same_e[:, :], cnt[:, :], start=True, stop=True).then_inc(total, 1)

            def nothing(i, s):
                pass

            shared(0, 0, lambda k: k == 0, nothing)
            shared(1, 1, lambda k: True, lambda i, s: count_all(i - 1, s))
            shared(2, 0, lambda k: True, lambda i, s: count_all(i - 1, s))
            with pe.Fori(3, 8, 2) as i:
                shared(i, 1, lambda k: True, lambda i, s: count_all(i - 1, s))
                shared(i + 1, 0, lambda k: True, lambda i, s: count_all(i - 1, s))

            def select(i, s):
                if (i, s) == (9, 1):
                    pe.wait_ge(sel, 2)
                    pe.matmul(ps_t[:, 1, 0:1], c.same_e[:, :], ties[:, 0:1], start=True, stop=True)
                    pe.matmul(ps_t[:, 1, 1:2], c.earlier[:, :], ties[:, 1:2], start=True, stop=True).then_inc(selp, 1)
                if (i, s) == (9, 3):
                    pe.wait_ge(sel, 7)
                    pe.matmul(ps_t[:, 1, 2:3], c.earlier[:, :], order[:, TILE - 1:TILE], start=True, stop=True).then_inc(selp, 1)
                if (i, s) == (10, 1):
                    pe.wait_ge(sel, 8)
                    for b in range(CH):
                        op = pe.transpose(ps_t[:, 0, b * P:(b + 1) * P], slot[:, b * P:(b + 1) * P], c.ident[:, :])
                    op.then_inc(selp, 1)

            shared(9, 1, lambda k: True, select)
            shared(10, 0, lambda k: True, select)

            def list_group(e, g):
                pe.wait_ge(hot[g], e + 1)
                if g == 0:
                    pe.wait_ge(listed, 2)
                    ge(pe, tokf, e)
                for n in range(GROUP):
                    op = pe.matmul(ps_t[:, 1, 0:2 * SLOTS], hi_hot[:, g, n, :],
                                   ids_flat(e + (g * P + n * E)),
                                   start=(g == 0 and n == 0), stop=(g == CH - 1 and n == GROUP - 1))
                op.then_inc(hot_used, 1)
                if g == CH - 1:
                    pass

            shared(11, 1, lambda k: True, nothing)
            shared(12, 0, lambda k: True, lambda i, s: list_group(i - 12, s))
            with pe.Fori(13, NT - 2, 2) as i:
                shared(i, 1, lambda k: True, lambda i, s: list_group(i - 12, s))
                shared(i + 1, 0, lambda k: True, lambda i, s: list_group(i - 12, s))
            shared(15, 1, lambda k: True, lambda i, s: list_group(i - 12, s))
            shared(16, 0, lambda k: k == 1, nothing)
            with pe.Fori(4, E) as e:
                for g in range(CH):
                    list_group(e, g)

            def turn(i, g):
                p = g % 2
                pe.wait_ge(gath[g], gath_count(i, g))
                ge(pe, gt, i - 1)
                if isinstance(i, int) and i < 2:
                    pe.wait_ge(tokf, E)
                for n in range(CH):
                    op = pe.transpose(ps_t[:, p, n * P:(n + 1) * P], G[:, g, n, 0:D], c.ident[:, :])
                op.then_inc(gt_ps, 1)

            def gath_count(i, g):
                return (i - g) * 16 + 64

            def first_layer(i, g):
                p, s = g % 2, g // 2
                ge(pe, gt, i + 1)
                if p == 0:
                    pe.wait_ge(ew[s], ((i - g) // 4 + 1) * 48 if isinstance(i, int) else (i - g) * 12 + 48)
                for k in range(HK):
                    ge(pe, eact, i * HK + k + 1 - HK)
                    if isinstance(i, int) and i == 0 and k == 0:
                        pe.wait_ge(act_s, NT * HK)
                    pe.matmul(ps_h[:, k, :], we1[:, s, k * P:(k + 1) * P], GT[:, p, :],
                              start=True, stop=True).then_inc(eh, 1)

            def second_layer(i, g):
                p, s = g % 2, g // 2
                ge(pe, eact, i * HK + HK)
                ge(pe, ytmp, i - 1)
                if isinstance(i, int) and i == 0:
                    pe.wait_ge(x1, NT)
                for n in range(CH):
                    for k in range(HK):
                        op = pe.matmul(ps_o[:, p, n, :], hS[:, p, k, n * P:(n + 1) * P], we2[:, s, k, :],
                                       start=(k == 0), stop=(k == HK - 1))
                op.then_inc(eo, 1)

            def step(i, g, last=False):
                if not last:
                    turn(i + 1, (g + 1) % 4)
                first_layer(i, g)
                if not (isinstance(i, int) and i == 0):
                    second_layer(i - 1, (g + 3) % 4)

            turn(0, 0)
            for i in range(4):
                step(i, i)
            with pe.Fori(4, 2 * E - 7, 4) as i:
                for g in range(4):
                    step(i + g, g)
            for i in range(2 * E - 4, 2 * E):
                step(i, i % 4, i == 2 * E - 1)
            second_layer(2 * E - 1, 3)

        @block.vector
        def _(dve):
            def route(i, m, live):
                p = m % 2
                if live(0):
                    if x_dram is not None:
                        ge(dve, x_in[p], (i - p) * 8 + 16)
                    ge(dve, var, i - 1)
                    xi = xtile(i)
                    for n in range(CH):
                        op = dve.bn_stats(st[:, p, n, :], xi[:, n, :])
                    op.then_inc(stats, 1)
                if live(1):
                    t, q = i - 1, 1 - p
                    ge(dve, rstd_s, t + 1)
                    b = (m - 1) % 4
                    ge(dve, stored[b], (t - b) * 4)
                    ge(dve, xt_ps, t - 1)
                    ge(dve, prob_kept, t - 3)
                    xi = xtile(t)
                    for n in range(CH):
                        op = dve.tensor_scalar(XN[:, b, n, 0:D], xi[:, n, :], mv[:, q, n, 0:1],
                                               rstd[:, q, n:n + 1], ALU.subtract, ALU.mult)
                    op.then_inc(xn, 1)
                if live(0):
                    alone(dve, (stats, i + 1), (xn, i - 1))
                    for n in range(CH):
                        op = dve.bn_aggr(mv[:, p, n, :], st[:, p, n, :])
                    op.then_inc(var, 1)
                    ge(dve, var, i + 1)
                    ge(dve, rstd_s, i - 1)
                    dve.tensor_scalar(ve[:, p, :], mv[:, p, :, 1], EPS, None, ALU.add).then_inc(varE, 1)
                if live(2):
                    t, q = i - 2, p
                    ge(dve, logit, t + 1)
                    ge(dve, shifted, t - 1)
                    lps = ps_o[:, q, 0, 0:CH * E].rearrange("p (c e) -> p c e", c=CH)
                    dve.tensor_reduce(mx[:, q, :], lps, AX_X, ALU.max).then_inc(mxs, 1)
                    ge(dve, mxs, t + 1)
                    ge(dve, expd, t - 1)
                    dve.tensor_tensor(lg[:, q, :, :], lps, wide(mx, q), ALU.subtract).then_inc(shifted, 1)
                if live(3):
                    t, q = i - 3, 1 - p
                    ge(dve, expd, t + 1)
                    dve.tensor_reduce(sm[:, q, :], ex[:, q, :, :], AX_X, ALU.add).then_inc(summed, 1)
                    ge(dve, summed, t + 1)
                    ge(dve, prob, t - 1)
                    dve.reciprocal(rs[:, q, :], sm[:, q, :]).then_inc(inv, 1)
                    ge(dve, inv, t + 1)
                    dve.scalar_tensor_tensor(XN[:, (m - 3) % 4, :, D:ROW], ex[:, q, :, :], 0.5, wide(rs, q),
                                             ALU.mult, ALU.mult).then_inc(prob, 1)

            pipelined(dve, NT, 3, route, 4)

            dve.memset(thr[:, :], 0).then_inc(srch, 1)
            dve.memset(bit[:, :], 1 << TOP_BIT).then_inc(srch, 1)
            dve.wait_ge(pt_ps, 1)
            dve.tensor_copy(PT[:, :], ps_t[:, 0, :]).then_inc(pt, 1)
            dve.wait_ge(pt, 1)

            def shared_out(i, p, live):
                if live(1):
                    t, q = i - 1, 1 - p
                    ge(dve, outp, t + 1)
                    ge(dve, xb, NT)
                    dve.scalar_tensor_tensor(xtile(t), ps_o[:, q, :, :], 0.5, xtile(t), ALU.mult, ALU.add).then_inc(x1, 1)

            def try_bit(n):
                ge(dve, srch, n * 5 + 2)
                dve.tensor_tensor(cand[:, :], thr[:, :], bit[:, :], ALU.bitwise_or).then_inc(srch, 1)
                ge(dve, srch, n * 5 + 3)
                dve.tensor_scalar(hit[:, :], PT[:, :], cand[:, :].bitcast(F32), None, ALU.is_ge, ALU.add,
                                  accum_out=cnt[:, :]).then_inc(counted, 1)

            def take_bit(n):
                ge(dve, total, n + 1)
                dve.tensor_scalar(keep[:, 0:1], ps_t[:, 1, 0:1], float(CAP), -1.0, ALU.is_ge, ALU.mult).then_inc(srch, 1)
                ge(dve, srch, n * 5 + 4)
                dve.tensor_tensor(keep[:, 1:2], keep[:, 0:1], bit[:, :], ALU.bitwise_and).then_inc(srch, 1)
                ge(dve, srch, n * 5 + 5)
                dve.tensor_tensor(thr[:, :], thr[:, :], keep[:, 1:2], ALU.bitwise_or).then_inc(srch, 1)
                dve.tensor_scalar(bit[:, :], bit[:, :], 1, None, ALU.logical_shift_right).then_inc(srch, 1)

            def with_search(i, p):
                for s in range(4):
                    n = (i - 1) * 4 + s
                    try_bit(n)
                    take_bit(n)
                shared_out(i, p, lambda k: True)

            with_search(1, 1)
            with_search(2, 0)
            with dve.Fori(3, 8, 2) as i:
                with_search(i, 1)
                with_search(i + 1, 0)

            dve.wait_ge(srch, 32 * 5 + 2)
            th = thr[:, :].bitcast(F32)
            dve.tensor_scalar(more[:, :], PT[:, :], th, None, ALU.is_gt, ALU.add, accum_out=ties[:, 0:1]).then_inc(sel, 1)
            dve.tensor_scalar(same[:, :], PT[:, :], th, None, ALU.is_equal, ALU.add, accum_out=ties[:, 1:2]).then_inc(sel, 1)
            dve.wait_ge(sel, 2)
            dve.tensor_tensor_scan(rank[:, :], same[:, :], same[:, :], 0.0, ALU.add, ALU.bypass).then_inc(sel, 1)
            dve.wait_ge(selp, 1)
            dve.tensor_scalar(limit[:, 0:1], ps_t[:, 1, 0:1], -1.0, float(CAP), ALU.mult, ALU.add).then_inc(sel, 1)
            dve.wait_ge(sel, 4)
            dve.tensor_tensor(limit[:, 1:2], limit[:, 0:1], ps_t[:, 1, 1:2], ALU.subtract).then_inc(sel, 1)
            dve.wait_ge(sel, 5)
            dve.scalar_tensor_tensor(rank[:, :], rank[:, :], limit[:, 1:2], same[:, :], ALU.is_le, ALU.mult).then_inc(sel, 1)
            dve.wait_ge(sel, 6)
            dve.tensor_tensor(taken[:, :], more[:, :], rank[:, :], ALU.add).then_inc(srch, 1)
            dve.wait_ge(srch, 32 * 5 + 3)
            dve.tensor_tensor_scan(order[:, :], taken[:, :], taken[:, :], 0.0, ALU.add, ALU.bypass).then_inc(sel, 1)
            shared_out(9, 1, lambda k: True)
            dve.wait_ge(selp, 2)
            dve.wait_ge(sel, 7)
            dve.scalar_tensor_tensor(slot[:, :], order[:, :], ps_t[:, 1, 2:3], taken[:, :], ALU.add, ALU.mult).then_inc(sel, 1)
            dve.wait_ge(selp, 3)
            dve.tensor_scalar(slot_i[:, :], ps_t[:, 0, :], -1.0, None, ALU.add).then_inc(sel, 1)
            dve.wait_ge(sel, 9)
            dve.tensor_scalar(hi_i[:, :], slot_i[:, :], 3, None, ALU.arith_shift_right).then_inc(sel, 1)
            dve.tensor_scalar(lo_i[:, :], slot_i[:, :], SLOTS - 1, None, ALU.bitwise_and).then_inc(sel, 1)
            dve.wait_ge(sel, 11)
            dve.tensor_copy(hi_f[:, :], hi_i[:, :]).then_inc(listed, 1)
            dve.tensor_copy(lo_f[:, :], lo_i[:, :]).then_inc(sel, 1)
            dve.wait_ge(sel, 12)
            shared_out(10, 0, lambda k: True)
            dve.tensor_tensor(lo_hot[:, :, :],
                              c.count8[:, :].rearrange("p (a s) -> p a s", a=1).to_broadcast([P, TILE, SLOTS]),
                              lo_f[:, :].rearrange("p (t a) -> p t a", a=1).to_broadcast([P, TILE, SLOTS]),
                              ALU.is_equal).then_inc(sel, 1)
            dve.wait_ge(sel, 13)
            dve.tensor_scalar(ids[:, :, 0, :], lo_hot[:, :, :], c.part[:, :], None, ALU.mult)
            dve.tensor_tensor(ids[:, :, 1, :], lo_hot[:, :, :],
                              c.chunk_of[:, :].rearrange("p (t a) -> p t a", a=1).to_broadcast([P, TILE, SLOTS]),
                              ALU.mult).then_inc(listed, 1)
            dve.wait_ge(listed, 2)
            shared_out(11, 1, lambda k: True)

            def join(e):
                dve.wait_ge(hot_used, e * CH + CH)
                ge(dve, toks, e)
                dve.tensor_copy(tok_f[:, :], ps_t[:, 1, 0:2 * SLOTS]).then_inc(tokf, 1)
                dve.wait_ge(tokf, e + 1)
                dve.scalar_tensor_tensor(tok[:, bass.ds(e * SLOTS, SLOTS)], tok_f[:, SLOTS:2 * SLOTS], float(P),
                                         tok_f[:, 0:SLOTS], ALU.mult, ALU.add).then_inc(toks, 1)

            def make_list(e):
                for g in range(CH - 1):
                    one_hot_group(e, g)

            make_list(0)
            shared_out(12, 0, lambda k: True)
            with dve.Fori(13, NT - 2, 2) as i:
                for p in range(2):
                    make_list(i + (p - 12))
                    join(i + (p - 13))
                    shared_out(i + p, 1 - p, lambda k: True)
            make_list(3)
            join(2)
            shared_out(15, 1, lambda k: True)
            shared_out(16, 0, lambda k: True)
            with dve.Fori(4, E) as e:
                make_list(e)
                join(e - 1)
            join(E - 1)

            def turn(i, g):
                p = g % 2
                ge(dve, gt_ps, i + 1)
                ge(dve, eh, i * HK - HK)
                dve.tensor_copy(GT[:, p, :], ps_t[:, p, :]).then_inc(gt, 1)

            def scores(i, e, g):
                p = g % 2
                dve.wait_ge(gt_ps, i + 1)
                ge(dve, y, i - 1)
                dve.tensor_copy(score[:, p, :], G[:, g, :, bass.ds(e + D, 1)].rearrange("p c a -> p (c a)")).then_inc(sc, 1)

            def out(i, e, g):
                p, s = g % 2, g // 2
                ge(dve, eo, i + 1)
                ge(dve, scat, (i - 1) * 64)
                dve.tensor_tensor(Y[:, p, :, :], ps_o[:, p, :, :],
                                  b2[:, s, :].rearrange("p (a d) -> p a d", a=1).to_broadcast([P, CH, D]),
                                  ALU.add).then_inc(ytmp, 1)
                ge(dve, ytmp, i + 1)
                ge(dve, sc, i + 1)
                dve.tensor_tensor(Y[:, p, :, :], Y[:, p, :, :],
                                  score[:, p, :].rearrange("p (c a) -> p c a", a=1).to_broadcast([P, CH, D]),
                                  ALU.mult).then_inc(y, 1)

            turn(0, 0)
            scores(0, 0, 0)
            for i in range(4):
                turn(i + 1, (i + 1) % 4)
                if i >= 1:
                    out(i - 1, (i - 1) // 2, (i - 1) % 4)
                scores(i + 1, (i + 1) // 2, (i + 1) % 4)
            with dve.Fori(2, E - 3, 2) as e:
                for g in range(4):
                    turn(e * 2 + (g + 1), (g + 1) % 4)
                    out(e * 2 + (g - 1), None, (g + 3) % 4)
                    scores(e * 2 + (g + 1), e + (g + 1) // 2, (g + 1) % 4)
            for i in range(2 * E - 4, 2 * E):
                if i < 2 * E - 1:
                    turn(i + 1, (i + 1) % 4)
                out(i - 1, None, (i - 1) % 4)
                if i < 2 * E - 1:
                    scores(i + 1, (i + 1) // 2, (i + 1) % 4)
            out(2 * E - 1, None, 3)


VECS = ["xw", "r_ll", "k_ll", "v_ll", "g_ll", "d_ll", "u", "ln_w", "ln_b"]
MATS = ["rW", "kW", "vW", "gW", "oW", "la_rk", "la_vg", "lb_rk", "lb_vg", "la_d", "lb_d"]
BANK_K, BANK_R, BANK_V, BANK_G = 0, 1, 2, 2


def attention_block(nc, c, X, x_dram, a):
    with ExitStack() as ctx:
        def sb(name, shape, dt=F32):
            return ctx.enter_context(nc.sbuf_tensor("t_" + name, shape, dt))

        def ps(name, shape):
            return ctx.enter_context(nc.psum_tensor("t_" + name, shape, F32))

        def sem(name):
            c.sems.append(nc.alloc_semaphore(name="t_" + name))
            return c.sems[-1]

        ps_a = ps("ps_a", [P, 2, TILE])
        ps_v = ps("ps_v", [P, 3, TILE])
        ps_y = ps("ps_y", [P, 2, TILE])
        ps_z = ps("ps_z", [P, TILE])

        vec = sb("vec", [P, len(VECS)])
        mats = sb("mats", [P, len(MATS), P])
        vrep = sb("vrep", [P, HD, P])
        sums = sb("sums", [P, HD + 3, P])
        ident = sb("ident", [P, P])
        eps_col = sb("eps_col", [P, 1])
        minus_half = sb("minus_half", [P, 1])

        st = sb("st", [P, CH, 6])
        mv = sb("mv", [P, 2, CH, 2])
        ve = sb("ve", [P, CH])
        rstd = sb("rstd", [P, CH])
        XN = sb("XN", [P, CH, D])
        xT = sb("xT", [P, 2, TILE + 1])
        dx = sb("dx", [P, 2, TILE])
        lerp = sb("lerp", [P, TILE])
        t_rk = sb("t_rk", [P, TILE])
        t_vg = sb("t_vg", [P, TILE])
        t_d = sb("t_d", [LORA, TILE])
        t_d2 = sb("t_d2", [LORA, TILE])
        corr = sb("corr", [P, 5, TILE])
        mix_d = sb("mix_d", [P, TILE])
        mix = sb("mix", [P, 4, 2, TILE])
        e1 = sb("e1", [P, TILE])
        w = sb("w", [P, 2, TILE])
        kS = sb("kS", [P, 2, TILE])
        rS = sb("rS", [P, 2, TILE])
        vS = sb("vS", [P, 2, TILE])
        ruk = sb("ruk", [P, TILE])
        kv = sb("kv", [P, 2, TILE])
        S = sb("S", [P, 2, HD, TILE + 1])
        prod = sb("prod", [P, HD, TILE])
        bonus = sb("bonus", [P, TILE])
        tg = sb("tg", [P, TILE])
        sg = sb("sg", [P, 2, TILE])
        sq = sb("sq", [P, TILE])
        lnv = sb("lnv", [P, TILE])
        hrstd = sb("hrstd", [P, 2, TILE])
        yn = sb("yn", [P, TILE])
        o = sb("o", [P, TILE])

        loads = sem("loads"); consts = sem("consts"); passed = sem("passed")
        x_in = [sem("x_in0"), sem("x_in1")]
        stats = sem("stats"); aggr = sem("aggr"); ve_s = sem("ve_s"); rstd_s = sem("rstd_s"); xn = sem("xn")
        p_t = sem("p_t"); xt = sem("xt"); dx_s = sem("dx_s"); lerp_s = sem("lerp_s")
        p_rk = sem("p_rk"); p_vg = sem("p_vg"); p_d = sem("p_d")
        th_rk = sem("th_rk"); th_vg = sem("th_vg"); th_d = sem("th_d"); th_d2 = sem("th_d2")
        p_l = sem("p_l"); corr_s = sem("corr_s"); mixed = sem("mixed")
        p_a2 = sem("p_a2"); p_l2 = sem("p_l2"); e1_s = sem("e1_s"); w_s = sem("w_s")
        p_k = sem("p_k"); p_r = sem("p_r"); p_v = sem("p_v"); p_g = sem("p_g"); p_vr = sem("p_vr")
        k_s = sem("k_s"); r_s = sem("r_s"); v_s = sem("v_s"); ruk_s = sem("ruk_s"); carry = sem("carry")
        kv_s = sem("kv_s"); scan_s = sem("scan_s"); prod_s = sem("prod_s")
        p_a = sem("p_a"); bonus_s = sem("bonus_s"); p_y = sem("p_y"); p_yb = sem("p_yb")
        tg_s = sem("tg_s"); sg_s = sem("sg_s"); sq_s = sem("sq_s"); p_var = sem("p_var")
        ln_s = sem("ln_s"); hrstd_s = sem("hrstd_s"); yn_s = sem("yn_s"); aff_s = sem("aff_s")
        o_s = sem("o_s"); p_out = sem("p_out"); x2_s = sem("x2_s")
        LAG = 4

        def mat(name, rows=slice(0, P), cols=slice(0, P)):
            return mats[rows, MATS.index(name), cols]

        def col(name):
            n = VECS.index(name)
            return vec[:, n:n + 1]

        def xtile(t):
            return X[:, bass.ds(t * TILE, TILE)].rearrange("p (c d) -> p c d", c=CH)

        block = ctx.enter_context(nc.Block())

        @block.sync
        def _(sp):
            def load_x(t, p):
                sp.dma_start(xtile(t), x_dram[bass.ds(t * TILE, TILE), :].rearrange("(c p) d -> p c d", p=P)
                             ).then_inc(x_in[p], 16)

            load_x(0, 0)
            sp.dma_start(mats[:, :, :], a["mats"]).then_inc(loads, 16)
            sp.dma_start(vec[:, :], a["vecs"]).then_inc(loads, 16)
            load_x(1, 1)
            sp.dma_start(vrep[:, :, :], a["vrep"]).then_inc(loads, 16)
            sp.dma_start(sums[:, :, :], a["sums"]).then_inc(loads, 16)
            sp.dma_start(ident[:, :], a["ident"]).then_inc(loads, 16)
            with nc.allow_non_contiguous_dma("starting state, one value per state row"):
                sp.dma_start(S[:, 0, :, 0:1], a["init_state"].rearrange("h i (j a) -> (h i) j a", a=1)).then_inc(loads, 16)
            with sp.Fori(2, NT - 1, 2) as t:
                for p in range(2):
                    sp.wait_ge(x_in[p], t * 8)
                    sp.sem_inc(passed, 1)
                    load_x(t + p, p)

        R_LOADS = 16 * 6

        @block.gpsimd
        def _(pool):
            pool.memset(minus_half[:, :], -0.5).then_inc(consts, 1)
            pool.memset(eps_col[:, :], EPS).then_inc(consts, 1)
            pool.memset(xT[:, 0, 0:1], 0.0).then_inc(consts, 1)
            pool.wait_ge(consts, 3)

            def step(i, p, live):
                q = 1 - p

                def add(n, name):
                    t = i - 1
                    ge(pool, corr_s, t * 5 + (n + 1))
                    if n == 0:
                        ge(pool, p_a2, t)
                        dst = mix_d[:, :]
                    else:
                        ge(pool, {"k": p_k, "r": p_r, "v": p_vr, "g": p_g}[name],
                           (t - 1) * HD if name == "v" else t - 1)
                        dst = mix[:, n - 1, q, :]
                    pool.tensor_tensor(dst, corr[:, n, :], xT[:, q, 1:TILE + 1], ALU.add).then_inc(mixed, 1)

                def times_r(j):
                    t = i - 2
                    ge(pool, scan_s, t * HD + (j + 1))
                    if j == 0:
                        ge(pool, r_s, t + 1)
                    ge(pool, p_y, (t - 1) * HD + (j + 1))
                    pool.tensor_tensor(prod[:, j, :], S[:, p, j, 0:TILE], rS[:, p, :], ALU.mult).then_inc(prod_s, 1)

                if live(0):
                    ge(pool, ve_s, i + 1)
                    ge(pool, xn, i)
                    pool.tensor_tensor(rstd[:, :], ve[:, :], minus_half[:, :].to_broadcast([P, CH]), ALU.pow).then_inc(rstd_s, 1)
                for n, name in enumerate("dkrv"):
                    if live(1):
                        add(n, name)
                    if live(2):
                        times_r(n)
                if live(2):
                    times_r(4)
                    times_r(5)
                if live(0):
                    ge(pool, xt, i + 1)
                    ge(pool, corr_s, (i - 1) * 5)
                    ge(pool, lerp_s, i - 1)
                    pool.tensor_tensor(dx[:, p, :], xT[:, p, 0:TILE], xT[:, p, 1:TILE + 1], ALU.subtract).then_inc(dx_s, 1)
                if live(1):
                    add(4, "g")
                if live(2):
                    times_r(6)
                    times_r(7)

            pipelined(pool, NT, LAG - 2, step)

        @block.scalar
        def _(act):
            act.wait_ge(loads, R_LOADS)
            act.wait_ge(consts, 3)

            def tanh(dst, src, ready, n, free, m, done, scale=1.0):
                ge(act, ready, n)
                ge(act, free, m)
                act.activation(dst, src, ACT.Tanh, scale=scale).then_inc(done, 1)

            def step(i, p, live):
                q = 1 - p
                bank = lambda n: ps_a[:, (n + p) % 2, :]
                t1, t2, t3 = i - 1, i - 2, i - 3
                if live(3):
                    tanh(tg[:, :], ps_v[:, BANK_G, :], p_g, t3 + 1, sg_s, t3, tg_s, 0.5)
                if live(1):
                    tanh(t_rk[:, :], bank(0), p_rk, t1 + 1, p_l, (t1 - 1) * 5 + 3, th_rk)
                if live(2):
                    ge(act, p_k, t2 + 1)
                    ge(act, kv_s, (t2 - 1) * HD)
                    act.copy(kS[:, p, :], ps_v[:, BANK_K, :]).then_inc(k_s, 1)
                if live(1):
                    tanh(t_vg[:, :], bank(1), p_vg, t1 + 1, p_l, (t1 - 1) * 5 + 5, th_vg)
                if live(2):
                    ge(act, p_r, t2 + 1)
                    ge(act, prod_s, (t2 - 1) * HD)
                    act.copy(rS[:, p, :], ps_v[:, BANK_R, :]).then_inc(r_s, 1)
                if live(1):
                    tanh(t_d[:, :], bank(2)[0:LORA, :], p_d, t1 + 1, p_l, (t1 - 1) * 5 + 1, th_d)
                if live(2):
                    ge(act, p_v, t2 + 1)
                    ge(act, bonus_s, t2 - 1)
                    act.copy(vS[:, p, :], ps_v[:, BANK_V, :]).then_inc(v_s, 1)
                if live(1):
                    tanh(t_d2[:, :], bank(7)[0:LORA, :], p_a2, t1 + 1, p_l2, t1, th_d2)
                if live(0):
                    ge(act, p_t, i + 1)
                    ge(act, mixed, (i - 1) * 5)
                    ge(act, lerp_s, i - 1)
                    ge(act, xt, i)
                    if p == 1:
                        act.copy(xT[:, 1, 0:1], xT[:, 0, TILE:TILE + 1])
                    act.copy(xT[:, p, 1:TILE + 1], bank(8)).then_inc(xt, 1)
                if live(3):
                    ge(act, p_yb, t3 + 1)
                    ge(act, p_var, t3)
                    act.activation(sq[:, :], ps_y[:, q, :], ACT.Square).then_inc(sq_s, 1)
                if live(1):
                    ge(act, p_l2, t1 + 1)
                    ge(act, w_s, t1)
                    act.activation(e1[:, :], bank(10), ACT.Exp, bias=col("d_ll")).then_inc(e1_s, 1)
                    ge(act, e1_s, t1 + 1)
                    ge(act, scan_s, (t1 - 1) * HD)
                    act.activation(w[:, q, :], e1[:, :], ACT.Exp, scale=-1.0).then_inc(w_s, 1)
                if live(3):
                    ge(act, p_var, t3 + 1)
                    ge(act, hrstd_s, t3)
                    act.activation(lnv[:, :], ps_z[:, :], ACT.Ln, bias=eps_col[:, :]).then_inc(ln_s, 1)
                    ge(act, ln_s, t3 + 1)
                    ge(act, yn_s, t3 - 1)
                    act.activation(hrstd[:, q, :], lnv[:, :], ACT.Exp, scale=-0.5).then_inc(hrstd_s, 1)

            pipelined(act, NT, LAG - 1, step)

        @block.tensor
        def _(pe):
            pe.wait_ge(loads, R_LOADS)

            def mm(dst, lhs, rhs, done, start=True, stop=True):
                pe.matmul(dst, lhs, rhs, start=start, stop=stop).then_inc(done, 1)

            def step(i, p, live):
                q = 1 - p
                bank = lambda n: ps_a[:, (n + p) % 2, :]
                t1, t2, t3, t4 = i - 1, i - 2, i - 3, i - 4

                def y(j):
                    if live(3):
                        ge(pe, prod_s, t3 * HD + (j + 1))
                        if j == 0:
                            ge(pe, yn_s, t3 - 1)
                        mm(ps_y[:, q, :], sums[:, j, :], prod[:, j, :], p_y, j == 0, False)

                def v_of(j):
                    if live(2):
                        if j == 0:
                            ge(pe, k_s, t2 + 1)
                        elif j == 1:
                            ge(pe, r_s, t2 + 1)
                        elif j == 2:
                            ge(pe, v_s, t2 + 1)
                        else:
                            ge(pe, kv_s, t2 * HD + (j - 2))
                        mm(ps_v[:, j % 3, :], vrep[:, j, :], mix[:, 2, p, :], p_vr)

                if live(1):
                    ge(pe, lerp_s, t1 + 1)
                    ge(pe, corr_s, t1 * 5)
                    mm(bank(0), mat("la_rk"), lerp[:, :], p_rk)
                if live(2):
                    ge(pe, mixed, t2 * 5 + 2)
                    ge(pe, kv_s, t2 * HD - 1)
                    mm(ps_v[:, BANK_K, :], mat("kW"), mix[:, 0, p, :], p_k)
                if live(3):
                    ge(pe, ruk_s, t3 + 1)
                    ge(pe, ln_s, t3)
                    mm(ps_z[:, :], sums[:, HD, :], ruk[:, :], p_a)
                if live(1):
                    ge(pe, e1_s, t1)
                    mm(bank(1), mat("la_vg"), lerp[:, :], p_vg)
                if live(2):
                    ge(pe, mixed, t2 * 5 + 3)
                    ge(pe, kv_s, t2 * HD)
                    mm(ps_v[:, BANK_R, :], mat("rW"), mix[:, 1, p, :], p_r)
                y(0)
                if live(1):
                    ge(pe, th_rk, t1 + 1)
                    mm(bank(2)[0:LORA, :], mat("la_d", cols=slice(0, LORA)), lerp[:, :], p_d)
                if live(2):
                    ge(pe, mixed, t2 * 5 + 4)
                    ge(pe, sg_s, t2)
                    mm(ps_v[:, BANK_V, :], mat("vW"), mix[:, 2, p, :], p_v)
                y(1)
                if live(1):
                    ge(pe, th_vg, t1 + 1)
                    ge(pe, th_d, t1 + 1)
                    mm(bank(3), mat("lb_d", rows=slice(0, LORA)), t_d[:, :], p_l)
                v_of(0)
                y(2)
                if live(1):
                    mm(bank(4), mat("lb_rk", rows=slice(LORA, P)), t_rk[LORA:P, :], p_l)
                v_of(1)
                y(3)
                if live(4):
                    ge(pe, o_s, t4 + 1)
                    if live(3):
                        ge(pe, bonus_s, t3 + 1)
                    for n in range(CH):
                        op = pe.matmul(ps_z[:, n * P:(n + 1) * P], o[:, n * P:(n + 1) * P], mat("oW"),
                                       start=True, stop=True)
                    op.then_inc(p_out, 1)
                if live(1):
                    ge(pe, corr_s, t1 * 5 + 1)
                    mm(bank(5), mat("lb_rk", rows=slice(0, LORA)), t_rk[0:LORA, :], p_l)
                v_of(2)
                y(4)
                if live(1):
                    ge(pe, corr_s, t1 * 5 + 2)
                    mm(bank(6), mat("lb_vg", rows=slice(0, LORA)), t_vg[0:LORA, :], p_l)
                v_of(3)
                y(5)
                if live(1):
                    ge(pe, mixed, t1 * 5 + 1)
                    ge(pe, corr_s, t1 * 5 + 3)
                    mm(bank(7)[0:LORA, :], mat("la_d", cols=slice(0, LORA)), mix_d[:, :], p_a2)
                v_of(4)
                y(6)
                if live(0):
                    ge(pe, xn, i + 1)
                    ge(pe, corr_s, t1 * 5 + 4)
                    for n in range(CH):
                        op = pe.transpose(bank(8)[:, n * P:(n + 1) * P], XN[:, n, :], ident[:, :])
                    op.then_inc(p_t, 1)
                v_of(5)
                y(7)
                if live(1):
                    ge(pe, th_d2, t1 + 1)
                    mm(bank(9), mat("lb_vg", rows=slice(LORA, P)), t_vg[LORA:P, :], p_l)
                v_of(6)
                if live(3):
                    ge(pe, bonus_s, t3 + 1)
                    mm(ps_y[:, q, :], sums[:, HD + 1, :], bonus[:, :], p_yb, False, True)
                if live(1):
                    if live(0):
                        ge(pe, xt, i + 1)
                    else:
                        ge(pe, corr_s, t1 * 5 + 4)
                    mm(bank(10), mat("lb_d", rows=slice(0, LORA)), t_d2[:, :], p_l2)
                v_of(7)
                if live(3):
                    ge(pe, sq_s, t3 + 1)
                    ge(pe, x2_s, t3)
                    mm(ps_z[:, :], sums[:, HD + 2, :], sq[:, :], p_var)
                if live(2):
                    ge(pe, mixed, t2 * 5 + 5)
                    ge(pe, kv_s, t2 * HD + 6)
                    mm(ps_v[:, BANK_G, :], mat("gW"), mix[:, 3, p, :], p_g)

            pipelined(pe, NT, LAG, step)

        @block.vector
        def _(dve):
            dve.wait_ge(loads, R_LOADS)
            dve.wait_ge(consts, 3)

            def step(i, p, live):
                q = 1 - p
                bank = lambda n: ps_a[:, (n + p) % 2, :]
                t1, t2, t3, t4 = i - 1, i - 2, i - 3, i - 4

                def correct(n, name, use):
                    if live(1):
                        ge(dve, p_l, t1 * 5 + (n + 1))
                        ge(dve, mixed, (t1 - 1) * 5 + (n + 1))
                        dve.scalar_tensor_tensor(corr[:, n, :], bank(use), col(name + "_ll"), dx[:, q, :],
                                                 ALU.add, ALU.mult).then_inc(corr_s, 1)

                def recur(j):
                    if live(2):
                        ge(dve, p_vr, t2 * HD + (j + 1))
                        ge(dve, scan_s, t2 * HD + (j - 1))
                        dve.tensor_tensor(kv[:, j % 2, :], ps_v[:, j % 3, :], kS[:, p, :], ALU.mult).then_inc(kv_s, 1)
                        ge(dve, kv_s, t2 * HD + (j + 1))
                        if j == 0:
                            ge(dve, w_s, t2 + 1)
                        ge(dve, prod_s, (t2 - 2) * HD + (j + 1))
                        dve.tensor_tensor_scan(S[:, p, j, 1:TILE + 1], w[:, p, :], kv[:, j % 2, :], S[:, p, j, 0:1],
                                               ALU.mult, ALU.add).then_inc(scan_s, 1)

                if live(3):
                    ge(dve, tg_s, t3 + 1)
                    ge(dve, o_s, t3 - 1)
                    dve.scalar_tensor_tensor(sg[:, q, :], tg[:, :], 1.0, ps_v[:, BANK_G, :], ALU.add, ALU.mult).then_inc(sg_s, 1)
                if live(0):
                    ge(dve, x_in[p], (i - p) * 8 + 16)
                    ge(dve, aggr, i)
                    xi = xtile(i)
                    for n in range(CH):
                        op = dve.bn_stats(st[:, n, :], xi[:, n, :])
                    op.then_inc(stats, 1)
                if live(3):
                    ge(dve, p_a, t3 + 1)
                    ge(dve, v_s, t3 + 1)
                    ge(dve, p_yb, t3)
                    dve.tensor_tensor(bonus[:, :], ps_z[:, :], vS[:, q, :], ALU.mult).then_inc(bonus_s, 1)
                if live(0):
                    ge(dve, stats, i + 1)
                    ge(dve, xn, i - 1)
                    dve.sem_inc(passed, 1)
                    for n in range(CH):
                        op = dve.bn_aggr(mv[:, p, n, :], st[:, n, :])
                    op.then_inc(aggr, 1)
                    ge(dve, aggr, i + 1)
                    ge(dve, rstd_s, i)
                    dve.tensor_scalar(ve[:, :], mv[:, p, :, 1], EPS, None, ALU.add).then_inc(ve_s, 1)
                if live(4):
                    ge(dve, hrstd_s, t4 + 1)
                    ge(dve, o_s, t4)
                    dve.tensor_tensor(yn[:, :], ps_y[:, p, :], hrstd[:, p, :], ALU.mult).then_inc(yn_s, 1)
                    ge(dve, yn_s, t4 + 1)
                    dve.tensor_scalar(yn[:, :], yn[:, :], col("ln_w"), col("ln_b"), ALU.mult, ALU.add).then_inc(aff_s, 1)
                    ge(dve, aff_s, t4 + 1)
                    ge(dve, p_out, t4)
                    dve.tensor_tensor(o[:, :], yn[:, :], sg[:, p, :], ALU.mult).then_inc(o_s, 1)
                if live(0):
                    ge(dve, rstd_s, i + 1)
                    ge(dve, p_t, i)
                    xi = xtile(i)
                    for n in range(CH):
                        op = dve.tensor_scalar(XN[:, n, :], xi[:, n, :], mv[:, p, n, 0:1], rstd[:, n:n + 1],
                                               ALU.subtract, ALU.mult)
                    op.then_inc(xn, 1)
                if live(2):
                    ge(dve, k_s, t2 + 1)
                    ge(dve, r_s, t2 + 1)
                    ge(dve, p_a, t2)
                    dve.scalar_tensor_tensor(ruk[:, :], rS[:, p, :], col("u"), kS[:, p, :], ALU.mult, ALU.mult).then_inc(ruk_s, 1)
                    if p == 1:
                        ge(dve, scan_s, t2 * HD)
                        ge(dve, prod_s, (t2 - 1) * HD)
                        dve.tensor_copy(S[:, 1, :, 0:1], S[:, 0, :, TILE:TILE + 1]).then_inc(carry, 1)
                    else:
                        dve.sem_inc(carry, 1)
                    ge(dve, carry, t2 + 1)
                correct(0, "d", 3)
                recur(0)
                correct(1, "k", 4)
                recur(1)
                if live(4):
                    ge(dve, p_out, t4 + 1)
                    dve.scalar_tensor_tensor(xtile(t4), ps_z[:, :].rearrange("p (c d) -> p c d", c=CH), 0.5, xtile(t4),
                                             ALU.mult, ALU.add).then_inc(x2_s, 1)
                correct(2, "r", 5)
                recur(2)
                correct(3, "v", 6)
                recur(3)
                recur(4)
                recur(5)
                correct(4, "g", 9)
                recur(6)
                recur(7)
                if live(0):
                    ge(dve, dx_s, i + 1)
                    ge(dve, p_d, i)
                    dve.scalar_tensor_tensor(lerp[:, :], dx[:, p, :], col("xw"), xT[:, p, 1:TILE + 1],
                                             ALU.mult, ALU.add).then_inc(lerp_s, 1)

            pipelined(dve, NT, LAG, step)
            dve.wait_ge(x2_s, NT)


class Consts:
    pass


def program(nc, a, out):
    with ExitStack() as ctx:
        def sb(name, shape, dt=F32):
            return ctx.enter_context(nc.sbuf_tensor(name, shape, dt))

        c = Consts()
        c.sems = []
        c.ident = sb("ident", [P, P])
        c.same_e = sb("same_e", [P, P])
        c.earlier = sb("earlier", [P, P])
        c.part = sb("part", [P, 1])
        c.count128 = sb("count128", [P, P], BF16)
        c.count8 = sb("count8", [P, SLOTS])
        c.chunk_of = sb("chunk_of", [P, TILE])
        c.minus_half = sb("minus_half", [P, 1])
        X = sb("X", [P, NT * TILE])
        table = nc.dram_tensor("table", (T, ROW), F32, kind="Internal").ap()
        x1_dram = nc.dram_tensor("x1_dram", (T, D), F32, kind="Internal").ap()
        x_dram = a["L0_attn_x"].rearrange("b t d -> (b t) d")
        out_dram = out.rearrange("b t d -> (b t) d")
        f = lambda n: a["L0_ffn_" + n]
        w = (f("W1").rearrange("e d h -> (e d) h"), f("b1"), f("W2").rearrange("e h d -> (e h) d"), f("b2"),
             f("gate"), f("Ws1"), f("bs1"), f("Ws2"), f("bs2"))
        attn = {n: a[n] for n in ("mats", "vecs", "vrep", "sums", "ident")}
        attn["init_state"] = a["L0_attn_init_state"]
        setup_block(nc, c, a)
        ffn_block(nc, c, X, x_dram, w, table, x1_dram, "_a")
        clear_semaphores(nc, c)
        attention_block(nc, c, X, x1_dram, attn)
        clear_semaphores(nc, c)
        ffn_block(nc, c, X, None, w, table, out_dram, "_b")


INPUTS = ["L0_attn_x", "L0_attn_init_state", "L0_ffn_gate", "L0_ffn_W1", "L0_ffn_b1", "L0_ffn_W2",
          "L0_ffn_b2", "L0_ffn_Ws1", "L0_ffn_bs1", "L0_ffn_Ws2", "L0_ffn_bs2"]


def laid_out(inputs):
    at = {n[len("L0_attn_"):]: np.asarray(v) for n, v in inputs.items() if n.startswith("L0_attn_")}
    both = {"la_rk": ("r_la", "k_la"), "la_vg": ("v_la", "g_la"), "lb_rk": ("r_lb", "k_lb"), "lb_vg": ("v_lb", "g_lb")}
    mats = np.zeros((P, len(MATS), P), np.float32)
    for n, name in enumerate(MATS):
        if name in both:
            m = np.concatenate([at[x] for x in both[name]], axis=0 if name.startswith("la") else 1)
        else:
            m = at[{"la_d": "d_la", "lb_d": "d_lb"}.get(name, name)]
        mats[:m.shape[1], n, :m.shape[0]] = m.T
    vrep = np.repeat(at["vW"].reshape(HEADS, HD, D).transpose(2, 1, 0)[:, :, :, None], HD, axis=3).reshape(P, HD, P)
    vecs = np.stack([np.tile(at[v], HEADS) if v.startswith("ln") else at[v] for v in VECS], axis=1)
    head = np.kron(np.eye(HEADS, dtype=np.float32), np.ones((HD, HD), np.float32))
    one = np.tile(np.eye(HD, dtype=np.float32), (1, HEADS))
    sums = [head * (one[j][None, :] - np.float32(1 / HD)) for j in range(HD)]
    sums += [head, np.eye(P, dtype=np.float32) - head / HD, head / HD]
    return {"mats": mats, "vecs": vecs, "vrep": vrep, "sums": np.stack(sums, axis=1).astype(np.float32),
            "ident": np.eye(P, dtype=np.float32)}


def kernel(**inputs):
    import concourse.bacc as bacc
    from concourse.bass_utils import run_bass_kernel_spmd

    nc = bacc.Bacc("TRN2", target_bir_lowering=False, num_devices=1)
    arrays = {n: np.asarray(inputs[n]) for n in INPUTS} | laid_out(inputs)
    arrays = {n: np.ascontiguousarray(v) for n, v in arrays.items()}
    aps = {n: nc.dram_tensor("in_" + n, v.shape, F32, kind="ExternalInput").ap() for n, v in arrays.items()}
    out = nc.dram_tensor("out", (NSEQ, SEQ, D), F32, kind="ExternalOutput").ap()
    program(nc, aps, out)
    ran = run_bass_kernel_spmd(nc, [{"in_" + n: v for n, v in arrays.items()}], core_ids=[0])
    return ran.results[0]["out"]
```

```python
from contextlib import ExitStack

import numpy as np

import concourse.bass as bass
from concourse import mybir

F32 = mybir.dt.float32
I32 = mybir.dt.int32
BF16 = mybir.dt.bfloat16
F32R = mybir.dt.float32r
ALU = mybir.AluOpType
ACT = mybir.ActivationFunctionType
AX_X = mybir.AxisListType.X

P = 128
D = 128
NSEQ, SEQ = 8, 1024
T = NSEQ * SEQ
TILE = 512
CH = TILE // P
NT = T // TILE
E = 8
HID = 512
HK = HID // P
CAP = T // E
SLOTS = CAP // P
HEADS, HD = 16, 8
LORA = 64
EPS = 1e-5
ROW = D + E
ROUNDS = 15
HIGH_PART = -(1 << 12)
EARLY = (NT - 4) // 2
GROUP = 16


def ge(eng, sem, count):
    if isinstance(count, int) and count <= 0:
        return
    eng.wait_ge(sem, count)


def pipelined(eng, n, lag, body, ways=2):
    first = ways * -(-(lag + ways) // ways)
    for i in range(first):
        body(i, i % ways, lambda k, i=i: 0 <= i - k < n)
    with eng.Fori(first, n - ways + 1, ways) as i:
        for m in range(ways):
            body(i + m, m, lambda k: True)
    for i in range(n, n + lag):
        body(i, i % ways, lambda k, i=i: 0 <= i - k < n)


def pipelined_pairs(eng, n, lag, body):
    first = 4 * -(-(lag + 4) // 4)
    for i in range(first):
        body(i, i % 4, i // 2, lambda k, i=i: 0 <= i - k < n)
    with eng.Fori(first // 2, n // 2 - 1, 2) as h:
        for m in range(4):
            body(h * 2 + m, m, h + m // 2, lambda k: True)
    for i in range(n, n + lag):
        body(i, i % 4, i // 2, lambda k, i=i: 0 <= i - k < n)


def setup_block(nc, c, src):
    with ExitStack() as ctx:
        pi = ctx.enter_context(nc.sbuf_tensor("pi", [P, 1], I32))
        pmi = ctx.enter_context(nc.sbuf_tensor("pmi", [P, 2], I32))
        pmf = ctx.enter_context(nc.sbuf_tensor("pmf", [P, 2], F32))
        col = ctx.enter_context(nc.sbuf_tensor("col", [P, 2, P], F32))
        iotas = ctx.enter_context(nc.semaphore("iotas"))
        zeroed = ctx.enter_context(nc.semaphore("zeroed"))
        mods = ctx.enter_context(nc.semaphore("mods"))
        block = ctx.enter_context(nc.Block())

        @block.gpsimd
        def _(pool):
            some = {"allow_small_or_imprecise_dtypes": True}
            pool.iota(pi[:, :], pattern=[[0, 1]], base=0, channel_multiplier=1).then_inc(iotas, 1)
            pool.iota(col[:, 0, :], pattern=[[0, NT], [1, E]], base=0, channel_multiplier=0, **some).then_inc(iotas, 1)
            pool.iota(col[:, 1, :], pattern=[[1, NT], [0, E]], base=0, channel_multiplier=0, **some).then_inc(iotas, 1)
            pool.iota(c.part[:, :], pattern=[[0, 1]], base=0, channel_multiplier=1, **some)
            pool.iota(c.count_rows[:, :, :], pattern=[[1, P], [0, GROUP]], base=0, channel_multiplier=0, **some)
            pool.iota(c.chunk_of[:, :], pattern=[[1, CH], [CH, NT], [0, E]], base=0, channel_multiplier=0, **some)
            pool.memset(c.minus_half[:, :], -0.5)
            pool.memset(c.ident[:, :], 0.0).then_inc(zeroed, 1)
            pool.wait_ge(zeroed, 1)
            pool.affine_select(out=c.ident[:, :], in_=c.ident[:, :], compare_op=ALU.not_equal, fill=1.0,
                               base=0, pattern=[[-1, P]], channel_multiplier=1)

        @block.vector
        def _(dve):
            dve.wait_ge(iotas, 3)
            dve.tensor_scalar(pmi[:, 0:1], pi[:, :], E - 1, None, ALU.bitwise_and).then_inc(mods, 1)
            dve.tensor_scalar(pmi[:, 1:2], pi[:, :], 3, None, ALU.arith_shift_right).then_inc(mods, 1)
            dve.wait_ge(mods, 2)
            dve.tensor_copy(pmf[:, :], pmi[:, :]).then_inc(mods, 1)
            dve.wait_ge(mods, 3)
            dve.tensor_scalar(c.same_e[:, :], col[:, 0, :], pmf[:, 0:1], None, ALU.is_equal).then_inc(mods, 1)
            dve.wait_ge(mods, 4)
            dve.scalar_tensor_tensor(c.earlier[:, :], col[:, 1, :], pmf[:, 1:2], c.same_e[:, :],
                                     ALU.is_gt, ALU.mult).then_inc(mods, 1)


def clear_semaphores(nc, c):
    nc.clear_and_free_semaphores(c.sems)
    nc.all_engine_barrier()
    c.sems = []


def ffn_block(nc, c, X, x_dram, w, table, acc, tag):
    W1d, b1d, W2d, b2d, gated, Ws1d, bs1d, Ws2d, bs2d = w
    with ExitStack() as ctx:
        def sb(name, shape, dt=F32):
            return ctx.enter_context(nc.sbuf_tensor(name + tag, shape, dt))

        def ps(name, shape):
            return ctx.enter_context(nc.psum_tensor(name + tag, shape, F32))

        def sem(name):
            c.sems.append(nc.alloc_semaphore(name=name + tag))
            return c.sems[-1]

        ps_t = ps("ps_t", [P, 2, TILE])
        ps_h = ps("ps_h", [P, HK, TILE])
        ps_o = ps("ps_o", [P, 2, CH, D])

        gate = sb("gate", [P, E])
        ws1 = sb("ws1", [P, HID])
        ws2 = sb("ws2", [P, HK, D])
        bs1 = sb("bs1", [P, HK])
        bs2 = sb("bs2", [P, D])
        half_bs2 = sb("half_bs2", [P, D])
        b1 = sb("b1", [P, E, HK])
        we1 = sb("we1", [P, 2, HID])
        we2 = sb("we2", [P, 2, HK, D])
        b2 = sb("b2", [P, 2, D])

        XT = sb("XT", [P, NT * TILE])
        XTs = sb("XTs", [P, 2, TILE])
        XN = sb("XN", [P, 4, CH, ROW])
        st = sb("st", [P, 2, CH, 6])
        mv = sb("mv", [P, 2, CH, 2])
        ve = sb("ve", [P, 2, CH])
        rstd = sb("rstd", [P, 2, CH])
        mx = sb("mx", [P, 2, CH])
        lg = sb("lg", [P, 2, CH, E])
        ex = sb("ex", [P, 2, CH, E])
        sm = sb("sm", [P, 2, CH])
        rs = sb("rs", [P, 2, CH])
        probs = sb("probs", [P, CH, NT * E])

        hS = sb("hS", [P, 2, HK, TILE])

        PT = sb("PT", [P, TILE])
        hit = sb("hit", [P, 3, TILE], BF16)
        thr = sb("thr", [P, 1], I32)
        step_up = sb("step_up", [P, 3], I32)
        cand = sb("cand", [P, 3], I32)
        fits = sb("fits", [P, 3], I32)
        most = sb("most", [P, 1], I32)
        cnt = sb("cnt", [P, 3])
        ties = sb("ties", [P, 2])
        more = sb("more", [P, TILE])
        same = sb("same", [P, TILE])
        rank = sb("rank", [P, TILE])
        limit = sb("limit", [P, 2])
        taken = sb("taken", [P, TILE])
        order = sb("order", [P, TILE])
        slot = sb("slot", [P, TILE])
        slot_i = sb("slot_i", [P, TILE], I32)
        hi_i = sb("hi_i", [P, TILE], I32)
        lo_i = sb("lo_i", [P, TILE], I32)
        hi_f = sb("hi_f", [P, E, CH, GROUP], BF16)
        lo_f = sb("lo_f", [P, TILE], BF16)
        lo_hot = sb("lo_hot", [P, SLOTS, TILE], BF16)
        ids = sb("ids", [P, 2, SLOTS, TILE], BF16)
        hi_hot = sb("hi_hot", [P, CH, P, GROUP], BF16)
        tok_f = sb("tok_f", [P, 2 * SLOTS])
        tok = sb("tok", [P, E * SLOTS], I32)
        tok_g = sb("tok_g", [P, 2, SLOTS], I32)
        tok_s = sb("tok_s", [P, 2, SLOTS], I32)

        G = sb("G", [P, 4, CH, ROW])
        GT = sb("GT", [P, 2, TILE])
        score = sb("score", [P, 2, CH])
        Y = sb("Y", [P, 4, CH, D])

        weights = sem("weights")
        passed = sem("passed")
        x_in = [sem("x_in0"), sem("x_in1")]
        var = sem("var"); varE = sem("varE"); rstd_s = sem("rstd_s"); stats = sem("stats")
        xn = sem("xn"); xt_ps = sem("xt_ps"); xt = sem("xt"); xt_big = sem("xt_big")
        logit = sem("logit"); mxs = sem("mxs"); shifted = sem("shifted"); expd = sem("expd")
        summed = sem("summed"); inv = sem("inv"); prob = sem("prob"); prob_kept = sem("prob_kept")
        stored = [sem("stored%d" % n) for n in range(4)]
        hid = sem("hid"); act_s = sem("act_s"); outp = sem("outp"); xb = sem("xb"); x1 = sem("x1")
        halfb = sem("halfb")
        acc_in = [sem("acc_in0"), sem("acc_in1")]
        pt_ps = sem("pt_ps"); pt = sem("pt"); srch = sem("srch"); counted = sem("counted"); total = sem("total")
        sel = sem("sel"); selp = sem("selp"); listed = sem("listed")
        hot = [sem("hot%d" % g) for g in range(CH)]
        hot_used = sem("hot_used"); tok_ps = sem("tok_ps"); tokf = sem("tokf"); tok_g_ = sem("tok_g_"); tok_s_ = sem("tok_s_")
        toks = sem("toks")
        gath = [sem("gath%d" % g) for g in range(4)]
        scat = sem("scat")
        ew = [sem("ew0"), sem("ew1")]
        gt_ps = sem("gt_ps"); gt = sem("gt"); eh = sem("eh"); eact = sem("eact"); eo = sem("eo")
        sc = sem("sc"); ytmp = sem("ytmp"); y = sem("y")

        block = ctx.enter_context(nc.Block())

        def xtile(t):
            return X[:, bass.ds(t * TILE, TILE)].rearrange("p (c d) -> p c d", c=CH)

        def tokens(dram, t, width):
            return dram[bass.ds(t * TILE, TILE), :].rearrange("(c p) d -> p c d", p=P)

        R_W = 16 * 9

        def alone(eng, *waits):
            for s, n in waits:
                ge(eng, s, n)
                eng.sem_inc(passed, 1)

        def b1_flat(e, k):
            return b1[:, :, :].rearrange("p e k -> p (e k)")[:, bass.ds(e * HK + k, 1)]

        def ids_flat(m):
            return ids[:, :, :, :].rearrange("p a s t -> p (a s) t")[:, :, bass.ds(m, 1)]

        def wide(tile, q):
            return tile[:, q, :].rearrange("p (c a) -> p c a", a=1).to_broadcast([P, CH, E])

        def one_hot_group(e, g):
            nc.vector.wait_ge(listed, 1)
            ge(nc.vector, hot_used, (e - 1) * CH + (g + 1))
            mine = hi_f[:, :, :, :].rearrange("p e g n -> p (e g n)")[:, bass.ds(e * (CH * GROUP) + g * GROUP, GROUP)]
            op = nc.vector.tensor_tensor(hi_hot[:, g, :, :], c.count_rows[:, :, :],
                                         mine.rearrange("p (a n) -> p a n", a=1).to_broadcast([P, P, GROUP]),
                                         ALU.is_equal)
            op.then_inc(hot[g], 1)

        @block.sync
        def _(sp):
            if x_dram is not None:
                for t in range(2):
                    sp.dma_start(xtile(t), tokens(x_dram, t, D)).then_inc(x_in[t], 16)
            sp.dma_start(gate[:, :], gated).then_inc(weights, 16)
            sp.dma_start(ws1[:, :], Ws1d).then_inc(weights, 16)
            sp.dma_start(ws2[:, :, :], Ws2d.rearrange("(k p) d -> p k d", p=P)).then_inc(weights, 16)
            sp.dma_start(bs2[:, :], bs2d.rearrange("(a d) -> a d", a=1).to_broadcast([P, D])).then_inc(weights, 16)
            with nc.allow_non_contiguous_dma("biases onto partitions, small"):
                for k in range(HK):
                    sp.dma_start(bs1[:, k:k + 1], bs1d[k * P:(k + 1) * P].rearrange("(p a) -> p a", a=1)).then_inc(weights, 16)
                sp.dma_start(b1[:, :, :], b1d.rearrange("e (k p) -> p (e k)", p=P).rearrange("p (e k) -> p e k", e=E)).then_inc(weights, 16)
            if x_dram is not None:
                with sp.Fori(2, NT - 1, 2) as t:
                    for p in range(2):
                        alone(sp, (x_in[p], t * 8))
                        sp.dma_start(xtile(t + p), tokens(x_dram, t + p, D)).then_inc(x_in[p], 16)

            def store_rows(i, p, live):
                if live(0):
                    alone(sp, (prob, i + 1), (stored[p], (i - p) * 4))
                    sp.dma_start(tokens(table, i, ROW), XN[:, p, :, :]).then_inc(stored[p], 16)

            pipelined(sp, NT, 0, store_rows, 4)

            def store_acc(i, p, live):
                if live(0):
                    alone(sp, (x1, i + 1), (acc_in[p], (i - p) * 8))
                    sp.dma_start(tokens(acc, i, D), xtile(i)).then_inc(acc_in[p], 16)

            pipelined(sp, NT, 0, store_acc)

            def load_expert(e, s, used):
                if used:
                    alone(sp, (ytmp, (e - 1) * 2))
                sp.dma_start(we1[:, s, :], W1d[bass.ds(e * D, D), :]).then_inc(ew[s], 16)
                sp.dma_start(we2[:, s, :, :], W2d[bass.ds(e * HID, HID), :].rearrange("(k p) d -> p k d", p=P)).then_inc(ew[s], 16)
                sp.dma_start(b2[:, s, :], b2d[bass.ds(e, 1), :].to_broadcast([P, D])).then_inc(ew[s], 16)

            for e in range(2):
                load_expert(e, e, False)
            with sp.Fori(2, E - 1, 2) as e:
                for s in range(2):
                    load_expert(e + s, s, True)
            for p in range(2):
                sp.wait_ge(acc_in[p], 8 * NT)
            for p in range(4):
                sp.wait_ge(stored[p], 4 * NT)
            sp.wait_ge(scat, 16 * E * SLOTS)

        @block.gpsimd
        def _(pool):
            pool.wait_ge(weights, R_W)
            pool.tensor_scalar(half_bs2[:, :], bs2[:, :], 0.5, None, ALU.mult).then_inc(halfb, 1)
            pool.wait_ge(halfb, 1)

            def route(i, m, live):
                p = m % 2
                if live(0):
                    ge(pool, varE, i + 1)
                    if live(2):
                        ge(pool, xn, i - 1)
                    pool.tensor_tensor(rstd[:, p, :], ve[:, p, :], c.minus_half[:, :].to_broadcast([P, CH]),
                                       ALU.pow).then_inc(rstd_s, 1)
                if live(2):
                    t = i - 2
                    alone(pool, (xt, t + 1))
                    pool.tensor_copy(XT[:, bass.ds(t * TILE, TILE)], XTs[:, p, :]).then_inc(xt_big, 1)
                if live(3):
                    t, q = i - 3, 1 - p
                    alone(pool, (prob, t + 1))
                    pool.tensor_copy(probs[:, :, bass.ds(t * E, E)], XN[:, (m - 3) % 4, :, D:ROW]).then_inc(prob_kept, 1)
                    pool.tensor_tensor(xtile(t), xtile(t),
                                       half_bs2[:, :].rearrange("p (a d) -> p a d", a=1).to_broadcast([P, CH, D]),
                                       ALU.add).then_inc(xb, 1)

            pipelined(pool, NT, 3, route, 4)

            for p in range(4):
                pool.wait_ge(stored[p], 4 * NT)

            def gather(e, s, half, first):
                g = 2 * s + half
                if half == 0:
                    alone(pool, (toks, e + 1), *([] if first else [(gt_ps, e * 2 - 2)]))
                    pool.tensor_copy(tok_g[:, s, :], tok[:, bass.ds(e * SLOTS, SLOTS)]).then_inc(tok_g_, 1)
                alone(pool, (tok_g_, e + 1),
                      *([] if first else [(gt_ps, e * 2 + (half - 3)), (sc, e * 2 + (half - 3))]))
                for j in range(CH):
                    pool.indirect_dma_start(
                        G[:, g, j, :], None, table[:, :],
                        bass.IndirectOffsetOnAxis(ap=tok_g[:, s, half * CH + j:half * CH + j + 1], axis=0),
                    ).then_inc(gath[g], 16)

            def scatter(e, s, half):
                if half == 0:
                    alone(pool, (toks, e + 1), (scat, e * (16 * SLOTS)))
                    pool.tensor_copy(tok_s[:, s, :], tok[:, bass.ds(e * SLOTS, SLOTS)]).then_inc(tok_s_, 1)
                alone(pool, (tok_s_, e + 1), (y, e * 2 + (half + 1)))
                for j in range(CH):
                    pool.indirect_dma_start(
                        acc[:, :],
                        bass.IndirectOffsetOnAxis(ap=tok_s[:, s, half * CH + j:half * CH + j + 1], axis=0),
                        Y[:, 2 * s + half, j, :], None, compute_op=ALU.add,
                    ).then_inc(scat, 16)

            for e in range(2):
                for half in range(2):
                    gather(e, e, half, True)
            pool.wait_ge(acc_in[0], 8 * NT)
            pool.wait_ge(acc_in[1], 8 * NT)
            gather(2, 0, 0, False)

            def turn_over(e, s, next1, next0):
                scatter(e, s, 0)
                if next1:
                    gather(e + 2, s, 1, False)
                scatter(e, s, 1)
                if next0:
                    gather(e + 3, 1 - s, 0, False)

            turn_over(0, 0, True, True)
            with pool.Fori(1, E - 4, 2) as e:
                turn_over(e, 1, True, True)
                turn_over(e + 1, 0, True, True)
            turn_over(E - 3, 1, True, False)
            turn_over(E - 2, 0, False, False)
            turn_over(E - 1, 1, False, False)

        @block.scalar
        def _(act):
            def hidden(t, p):
                for k in range(HK):
                    ge(act, hid, t * HK + k + 1)
                    if k == 0:
                        ge(act, outp, t - 1)
                    act.activation(hS[:, p, k, :], ps_h[:, k, :], ACT.Gelu_apprx_tanh,
                                   bias=bs1[:, k:k + 1]).then_inc(act_s, 1)

            def route(i, m, h, live):
                p = m % 2
                if live(2):
                    t = i - 2
                    ge(act, shifted, t + 1)
                    ge(act, prob, t - 1)
                    act.activation(ex[:, p, :, :], lg[:, p, :, :], ACT.Exp).then_inc(expd, 1)
                if live(0):
                    ge(act, xt_ps, i + 1)
                    ge(act, xt_big, i - 1)
                    ge(act, logit, i - 1)
                    act.copy(XTs[:, p, :], ps_t[:, 0, :]).then_inc(xt, 1)
                if live(4) and live(0) and p == 0:
                    hidden(h - 2, (m // 2) % 2)

            pipelined_pairs(act, NT, 2, route)

            with act.Fori(EARLY, NT - 1, 2) as t:
                for p in range(2):
                    hidden(t + p, p)

            def expert_hidden(i, p, e, half):
                for k in range(HK):
                    alone(act, (eh, i * HK + k + 1), *([(eo, i - 1)] if k == 0 else []))
                    act.activation(hS[:, p, k, :], ps_h[:, k, :], ACT.Gelu_apprx_tanh,
                                   bias=b1_flat(e, k)).then_inc(eact, 1)

            for i in range(2):
                expert_hidden(i, i, i // 2, i % 2)
            with act.Fori(1, E) as e:
                for half in range(2):
                    expert_hidden(e * 2 + half, half, e, half)

        @block.tensor
        def _(pe):
            pe.wait_ge(weights, R_W)

            def hidden(t, p, slots):
                for k in range(HK):
                    ge(pe, act_s, t * HK + k + 1 - HK)
                    if k == 0:
                        ge(pe, xt_big, t + 1)
                    pe.matmul(ps_h[:, k, :], ws1[:, k * P:(k + 1) * P], XT[:, bass.ds(t * TILE, TILE)],
                              start=True, stop=True).then_inc(hid, 1)
                    if k % 2 == 1:
                        slots(k // 2)

            def output(t, q, slots):
                ge(pe, act_s, t * HK + HK)
                ge(pe, x1, t - 1)
                for n in range(CH):
                    for k in range(HK):
                        op = pe.matmul(ps_o[:, q, n, :], hS[:, q, k, n * P:(n + 1) * P], ws2[:, k, :],
                                       start=(k == 0), stop=(k == HK - 1))
                    if n == CH - 1:
                        op.then_inc(outp, 1)
                    if n % 2 == 1:
                        slots(2 + n // 2)

            def nothing(s):
                pass

            def route(i, m, h, live):
                p = m % 2
                if live(1):
                    t, q = i - 1, 1 - p
                    ge(pe, xt, t + 1)
                    ge(pe, shifted, t)
                    for n in range(CH):
                        op = pe.matmul(ps_t[:, 1, (q * CH + n) * E:(q * CH + n + 1) * E],
                                       XTs[:, q, n * P:(n + 1) * P], gate[:, :], start=True, stop=True)
                    op.then_inc(logit, 1)
                if live(0):
                    ge(pe, xn, i + 1)
                    ge(pe, xt, i)
                    for n in range(CH):
                        op = pe.transpose(ps_t[:, 0, n * P:(n + 1) * P], XN[:, m, n, 0:D], c.ident[:, :])
                    op.then_inc(xt_ps, 1)
                if live(4) and live(0):
                    if p == 0:
                        hidden(h - 2, (m // 2) % 2, nothing)
                    else:
                        output(h - 2, (m // 2) % 2, nothing)

            pipelined_pairs(pe, NT, 1, route)

            hidden(EARLY, EARLY % 2, nothing)
            pe.wait_ge(prob_kept, NT)
            for b in range(CH):
                op = pe.transpose(ps_t[:, 0, b * P:(b + 1) * P], probs[:, b, :], c.ident[:, :])
            op.then_inc(pt_ps, 1)

            def shared(i, p, slots):
                hidden(i, p, slots)
                output(i - 1, 1 - p, slots)

            def count_all(n):
                ge(pe, counted, n * 3 + 3)
                pe.matmul(ps_t[:, 1, 0:3], c.same_e[:, :], cnt[:, :], start=True, stop=True).then_inc(total, 1)

            def rounds(r, places):
                def slots(s):
                    if s in places:
                        count_all(r + places.index(s))
                return slots

            shared(7, 1, rounds(0, [0, 2, 3]))
            shared(8, 0, rounds(3, [1, 3]))
            with pe.Fori(1, 3) as d:
                shared(d * 2 + 7, 1, rounds(d * 5, [0, 2, 3]))
                shared(d * 2 + 8, 0, rounds(d * 5 + 3, [1, 3]))

            def select(i, s):
                if (i, s) == (13, 1):
                    pe.wait_ge(sel, 2)
                    pe.matmul(ps_t[:, 1, 0:1], c.same_e[:, :], ties[:, 0:1], start=True, stop=True)
                    pe.matmul(ps_t[:, 1, 1:2], c.earlier[:, :], ties[:, 1:2], start=True, stop=True).then_inc(selp, 1)
                if (i, s) == (13, 3):
                    pe.wait_ge(sel, 7)
                    pe.matmul(ps_t[:, 1, 2:3], c.earlier[:, :], order[:, TILE - 1:TILE], start=True, stop=True).then_inc(selp, 1)
                if (i, s) == (14, 1):
                    pe.wait_ge(sel, 8)
                    for b in range(CH):
                        op = pe.transpose(ps_t[:, 0, b * P:(b + 1) * P], slot[:, b * P:(b + 1) * P], c.ident[:, :])
                    op.then_inc(selp, 1)

            shared(13, 1, lambda s: select(13, s))
            shared(14, 0, lambda s: select(14, s))

            def list_group(e, g):
                pe.wait_ge(hot[g], e + 1)
                if g == 0:
                    pe.wait_ge(listed, 2)
                    ge(pe, tokf, e)
                for n in range(GROUP):
                    op = pe.matmul(ps_t[:, 1, 0:2 * SLOTS], hi_hot[:, g, :, n],
                                   ids_flat(e + (g * P + n * E)),
                                   start=(g == 0 and n == 0), stop=(g == CH - 1 and n == GROUP - 1))
                op.then_inc(hot_used, 1)

            shared(15, 1, nothing)
            output(15, 1, nothing)
            for s in range(CH):
                list_group(0, s)
            for s in range(CH):
                list_group(1, s)

            def turn(i, g):
                pe.wait_ge(gath[g], gath_count(i, g))
                ge(pe, gt, i)
                for n in range(CH):
                    op = pe.transpose(ps_t[:, 0, n * P:(n + 1) * P], G[:, g, n, 0:D], c.ident[:, :])
                op.then_inc(gt_ps, 1)

            def gath_count(i, g):
                return (i - g) * 16 + 64

            def first_layer(i, g):
                p, s = g % 2, g // 2
                ge(pe, gt, i + 1)
                if p == 0:
                    pe.wait_ge(ew[s], ((i - g) // 4 + 1) * 48 if isinstance(i, int) else (i - g) * 12 + 48)
                for k in range(HK):
                    ge(pe, eact, i * HK + k + 1 - HK)
                    if isinstance(i, int) and i == 0 and k == 0:
                        pe.wait_ge(act_s, NT * HK)
                    pe.matmul(ps_h[:, k, :], we1[:, s, k * P:(k + 1) * P], GT[:, p, :],
                              start=True, stop=True).then_inc(eh, 1)

            def second_layer(i, g):
                p, s = g % 2, g // 2
                ge(pe, eact, i * HK + HK)
                ge(pe, ytmp, i - 1)
                if isinstance(i, int) and i == 0:
                    pe.wait_ge(x1, NT)
                for n in range(CH):
                    for k in range(HK):
                        op = pe.matmul(ps_o[:, p, n, :], hS[:, p, k, n * P:(n + 1) * P], we2[:, s, k, :],
                                       start=(k == 0), stop=(k == HK - 1))
                op.then_inc(eo, 1)

            def step(i, g, e_list, last=False):
                if not last:
                    turn(i + 1, (g + 1) % 4)
                first_layer(i, g)
                if not (isinstance(i, int) and i == 0):
                    second_layer(i - 1, (g + 3) % 4)
                if e_list is not None:
                    for half in range(2):
                        list_group(e_list, (g % 2) * 2 + half)

            turn(0, 0)
            for i in range(4):
                step(i, i, 2 + i // 2)
            with pe.Fori(2, E - 3, 2) as e:
                for g in range(4):
                    step(e * 2 + g, g, e + (2 + g // 2))
            for i in range(2 * E - 4, 2 * E):
                step(i, i % 4, None, i == 2 * E - 1)
            second_layer(2 * E - 1, 3)

        @block.vector
        def _(dve):
            def shared_out(t, q):
                ge(dve, outp, t + 1)
                ge(dve, xb, t + 1)
                dve.scalar_tensor_tensor(xtile(t), ps_o[:, q, :, :], 0.5, xtile(t), ALU.mult, ALU.add).then_inc(x1, 1)

            def route(i, m, h, live):
                p = m % 2
                if live(0):
                    if x_dram is not None:
                        ge(dve, x_in[p], (i - p) * 8 + 16)
                    ge(dve, var, i - 1)
                    xi = xtile(i)
                    for n in range(CH):
                        op = dve.bn_stats(st[:, p, n, :], xi[:, n, :])
                    op.then_inc(stats, 1)
                if live(1):
                    t, q = i - 1, 1 - p
                    ge(dve, rstd_s, t + 1)
                    b = (m - 1) % 4
                    ge(dve, stored[b], (t - b) * 4)
                    ge(dve, xt_ps, t - 3)
                    ge(dve, prob_kept, t - 3)
                    xi = xtile(t)
                    for n in range(CH):
                        op = dve.tensor_scalar(XN[:, b, n, 0:D], xi[:, n, :], mv[:, q, n, 0:1],
                                               rstd[:, q, n:n + 1], ALU.subtract, ALU.mult)
                    op.then_inc(xn, 1)
                if live(0):
                    alone(dve, (stats, i + 1), (xn, i - 1))
                    for n in range(CH):
                        op = dve.bn_aggr(mv[:, p, n, :], st[:, p, n, :])
                    op.then_inc(var, 1)
                    ge(dve, var, i + 1)
                    ge(dve, rstd_s, i - 1)
                    dve.tensor_scalar(ve[:, p, :], mv[:, p, :, 1], EPS, None, ALU.add).then_inc(varE, 1)
                if live(2):
                    t, q = i - 2, p
                    ge(dve, logit, t + 1)
                    ge(dve, shifted, t - 1)
                    lps = ps_t[:, 1, q * CH * E:(q + 1) * CH * E].rearrange("p (c e) -> p c e", c=CH)
                    dve.tensor_reduce(mx[:, q, :], lps, AX_X, ALU.max).then_inc(mxs, 1)
                    ge(dve, mxs, t + 1)
                    ge(dve, expd, t - 1)
                    dve.tensor_tensor(lg[:, q, :, :], lps, wide(mx, q), ALU.subtract).then_inc(shifted, 1)
                if live(3):
                    t, q = i - 3, 1 - p
                    ge(dve, expd, t + 1)
                    dve.tensor_reduce(sm[:, q, :], ex[:, q, :, :], AX_X, ALU.add).then_inc(summed, 1)
                    ge(dve, summed, t + 1)
                    ge(dve, prob, t - 1)
                    dve.reciprocal(rs[:, q, :], sm[:, q, :]).then_inc(inv, 1)
                    ge(dve, inv, t + 1)
                    dve.scalar_tensor_tensor(XN[:, (m - 3) % 4, :, D:ROW], ex[:, q, :, :], 0.5, wide(rs, q),
                                             ALU.mult, ALU.mult).then_inc(prob, 1)
                if p == 1 and live(7 if isinstance(i, int) and i < NT else 0) or isinstance(i, int) and i == NT + 1:
                    shared_out(h - 3, (m // 2 + 1) % 2)

            pipelined_pairs(dve, NT, 3, route)

            dve.memset(thr[:, :], 0).then_inc(srch, 1)
            for b in range(3):
                dve.memset(step_up[:, b:b + 1], (b + 1) << (2 * (ROUNDS - 1))).then_inc(srch, 1)
            dve.wait_ge(pt_ps, 1)
            dve.tensor_copy(PT[:, :], ps_t[:, 0, :]).then_inc(pt, 1)
            dve.wait_ge(pt, 1)
            START, PER = 4, 5

            def search_round(n):
                ge(dve, srch, n * PER + START)
                dve.tensor_tensor(cand[:, :], thr[:, :].to_broadcast([P, 3]), step_up[:, :],
                                  ALU.bitwise_or).then_inc(srch, 1)
                ge(dve, srch, n * PER + (START + 1))
                for b in range(3):
                    dve.tensor_scalar(hit[:, b, :], PT[:, :], cand[:, b:b + 1].bitcast(F32), None, ALU.is_ge, ALU.add,
                                      accum_out=cnt[:, b:b + 1]).then_inc(counted, 1)
                ge(dve, total, n + 1)
                dve.scalar_tensor_tensor(fits[:, :], ps_t[:, 1, 0:3], float(CAP), step_up[:, :],
                                         ALU.is_ge, ALU.mult).then_inc(srch, 1)
                ge(dve, srch, n * PER + (START + 2))
                dve.tensor_reduce(most[:, :], fits[:, :], AX_X, ALU.max).then_inc(srch, 1)
                dve.tensor_scalar(step_up[:, :], step_up[:, :], 2, None, ALU.logical_shift_right).then_inc(srch, 1)
                ge(dve, srch, n * PER + (START + 4))
                dve.tensor_tensor(thr[:, :], thr[:, :], most[:, :], ALU.bitwise_or).then_inc(srch, 1)

            for n in range(3):
                search_round(n)
            shared_out(6, 0)
            for n in range(3, 5):
                search_round(n)
            shared_out(7, 1)
            with dve.Fori(1, 3) as d:
                for n in range(3):
                    search_round(d * 5 + n)
                shared_out(d * 2 + 6, 0)
                for n in range(3, 5):
                    search_round(d * 5 + n)
                shared_out(d * 2 + 7, 1)
            FOUND = ROUNDS * PER + START

            dve.wait_ge(srch, FOUND)
            th = thr[:, :].bitcast(F32)
            dve.tensor_scalar(more[:, :], PT[:, :], th, None, ALU.is_gt, ALU.add, accum_out=ties[:, 0:1]).then_inc(sel, 1)
            dve.tensor_scalar(same[:, :], PT[:, :], th, None, ALU.is_equal, ALU.add, accum_out=ties[:, 1:2]).then_inc(sel, 1)
            dve.wait_ge(sel, 2)
            dve.tensor_tensor_scan(rank[:, :], same[:, :], same[:, :], 0.0, ALU.add, ALU.bypass).then_inc(sel, 1)
            dve.wait_ge(selp, 1)
            dve.tensor_scalar(limit[:, 0:1], ps_t[:, 1, 0:1], -1.0, float(CAP), ALU.mult, ALU.add).then_inc(sel, 1)
            dve.wait_ge(sel, 4)
            dve.tensor_tensor(limit[:, 1:2], limit[:, 0:1], ps_t[:, 1, 1:2], ALU.subtract).then_inc(sel, 1)
            dve.wait_ge(sel, 5)
            dve.scalar_tensor_tensor(rank[:, :], rank[:, :], limit[:, 1:2], same[:, :], ALU.is_le, ALU.mult).then_inc(sel, 1)
            dve.wait_ge(sel, 6)
            dve.tensor_tensor(taken[:, :], more[:, :], rank[:, :], ALU.add).then_inc(srch, 1)
            dve.wait_ge(srch, FOUND + 1)
            dve.tensor_tensor_scan(order[:, :], taken[:, :], taken[:, :], 0.0, ALU.add, ALU.bypass).then_inc(sel, 1)
            shared_out(12, 0)
            dve.wait_ge(selp, 2)
            dve.wait_ge(sel, 7)
            dve.scalar_tensor_tensor(slot[:, :], order[:, :], ps_t[:, 1, 2:3], taken[:, :], ALU.add, ALU.mult).then_inc(sel, 1)
            dve.wait_ge(selp, 3)
            dve.tensor_scalar(slot_i[:, :], ps_t[:, 0, :], -1.0, None, ALU.add).then_inc(sel, 1)
            dve.wait_ge(sel, 9)
            dve.tensor_scalar(hi_i[:, :], slot_i[:, :], 3, None, ALU.arith_shift_right).then_inc(sel, 1)
            dve.tensor_scalar(lo_i[:, :], slot_i[:, :], SLOTS - 1, None, ALU.bitwise_and).then_inc(sel, 1)
            dve.wait_ge(sel, 11)
            dve.tensor_copy(hi_f[:, :, :, :], hi_i[:, :].rearrange("p (g n e) -> p e g n", g=CH, e=E)).then_inc(listed, 1)
            dve.tensor_copy(lo_f[:, :], lo_i[:, :]).then_inc(sel, 1)
            dve.wait_ge(sel, 12)
            for n in range(SLOTS):
                dve.tensor_scalar(lo_hot[:, n, :], lo_f[:, :], float(n), None, ALU.is_equal).then_inc(sel, 1)
            shared_out(13, 1)
            dve.wait_ge(sel, 12 + SLOTS)
            dve.tensor_scalar(ids[:, 0, :, :], lo_hot[:, :, :], c.part[:, :], None, ALU.mult)
            dve.tensor_tensor(ids[:, 1, :, :], lo_hot[:, :, :],
                              c.chunk_of[:, :].rearrange("p (a t) -> p a t", a=1).to_broadcast([P, SLOTS, TILE]),
                              ALU.mult).then_inc(listed, 1)
            dve.wait_ge(listed, 2)
            shared_out(14, 0)

            def join(e):
                dve.wait_ge(hot_used, e * CH + CH)
                ge(dve, toks, e)
                dve.tensor_copy(tok_f[:, :], ps_t[:, 1, 0:2 * SLOTS]).then_inc(tokf, 1)
                dve.wait_ge(tokf, e + 1)
                dve.scalar_tensor_tensor(tok[:, bass.ds(e * SLOTS, SLOTS)], tok_f[:, SLOTS:2 * SLOTS], float(P),
                                         tok_f[:, 0:SLOTS], ALU.mult, ALU.add).then_inc(toks, 1)

            def make_list(e):
                for g in range(CH):
                    one_hot_group(e, g)

            make_list(0)
            shared_out(15, 1)
            join(0)
            make_list(1)
            join(1)

            def turn(i, g):
                p = g % 2
                ge(dve, gt_ps, i + 1)
                ge(dve, eh, i * HK - HK)
                dve.tensor_copy(GT[:, p, :], ps_t[:, 0, :]).then_inc(gt, 1)

            def scores(i, e, g):
                p = g % 2
                dve.wait_ge(gt_ps, i + 1)
                ge(dve, y, i - 1)
                dve.tensor_copy(score[:, p, :], G[:, g, :, bass.ds(e + D, 1)].rearrange("p c a -> p (c a)")).then_inc(sc, 1)

            def out(i, e, g):
                p, s = g % 2, g // 2
                ge(dve, eo, i + 1)
                ge(dve, scat, (i - 3) * 64)
                dve.tensor_tensor(Y[:, g, :, :], ps_o[:, p, :, :],
                                  b2[:, s, :].rearrange("p (a d) -> p a d", a=1).to_broadcast([P, CH, D]),
                                  ALU.add).then_inc(ytmp, 1)
                ge(dve, ytmp, i + 1)
                ge(dve, sc, i + 1)
                dve.tensor_tensor(Y[:, g, :, :], Y[:, g, :, :],
                                  score[:, p, :].rearrange("p (c a) -> p c a", a=1).to_broadcast([P, CH, D]),
                                  ALU.mult).then_inc(y, 1)

            def step(i, g, e_next, e_list, e_join, first=False, last=False):
                if not last:
                    turn(i + 1, (g + 1) % 4)
                if e_join is not None:
                    join(e_join)
                if e_list is not None:
                    for half in range(2):
                        one_hot_group(e_list, (g % 2) * 2 + half)
                if not first:
                    out(i - 1, None, (g + 3) % 4)
                if not last:
                    scores(i + 1, e_next, (g + 1) % 4)

            turn(0, 0)
            scores(0, 0, 0)
            for i in range(4):
                step(i, i, (i + 1) // 2, 2 + i // 2, 2 if i == 2 else None, first=(i == 0))
            with dve.Fori(2, E - 3, 2) as e:
                for g in range(4):
                    step(e * 2 + g, g, e + (g + 1) // 2, e + (2 + g // 2),
                         e + (1 + g // 2) if g % 2 == 0 else None)
            for i in range(2 * E - 4, 2 * E):
                step(i, i % 4, (i + 1) // 2, None, E - 1 if i == 2 * E - 4 else None, last=(i == 2 * E - 1))
            out(2 * E - 1, None, 3)


VECS = ["xw", "r_ll", "k_ll", "v_ll", "g_ll", "d_ll", "u", "ln_w", "ln_b"]
MATS = ["rW", "kW", "vW", "gW", "oW", "la_rk", "la_vg", "lb_rk", "lb_vg", "la_d", "lb_d"]
BANK_K, BANK_V, BANK_R, BANK_G = 0, 1, 2, 2


def attention_block(nc, c, X, x_dram, a):
    with ExitStack() as ctx:
        def sb(name, shape, dt=F32):
            return ctx.enter_context(nc.sbuf_tensor("t_" + name, shape, dt))

        def ps(name, shape):
            return ctx.enter_context(nc.psum_tensor("t_" + name, shape, F32))

        def sem(name):
            c.sems.append(nc.alloc_semaphore(name="t_" + name))
            return c.sems[-1]

        ps_a = ps("ps_a", [P, 2, TILE])
        ps_v = ps("ps_v", [P, 3, TILE])
        ps_y = ps("ps_y", [P, 2, TILE])
        ps_z = ps("ps_z", [P, TILE])

        vec = sb("vec", [P, len(VECS)])
        mats = sb("mats", [P, len(MATS), P])
        pick = sb("pick", [P, HD, P])
        sums = sb("sums", [P, HD + 3, P])
        ident = sb("ident", [P, P])
        eps_col = sb("eps_col", [P, 1])
        minus_half = sb("minus_half", [P, 1])

        st = sb("st", [P, CH, 6])
        mv = sb("mv", [P, 2, CH, 2])
        ve = sb("ve", [P, CH])
        rstd = sb("rstd", [P, CH])
        XN = sb("XN", [P, CH, D])
        xT = sb("xT", [P, 2, TILE + 1])
        dx = sb("dx", [P, 2, TILE])
        lerp = sb("lerp", [P, TILE])
        t_rk = sb("t_rk", [P, TILE])
        t_vg = sb("t_vg", [P, TILE])
        t_d = sb("t_d", [LORA, TILE])
        t_d2 = sb("t_d2", [LORA, TILE])
        corr = sb("corr", [P, 5, TILE])
        mix_d = sb("mix_d", [P, TILE])
        mix = sb("mix", [P, 4, 2, TILE])
        e1 = sb("e1", [P, TILE])
        w = sb("w", [P, 2, TILE])
        kS = sb("kS", [P, 2, TILE])
        rS = sb("rS", [P, 2, TILE])
        vS = sb("vS", [P, 2, TILE])
        v_high = sb("v_high", [P, TILE])
        v_hi = sb("v_hi", [P, TILE], F32R)
        v_lo = sb("v_lo", [P, TILE], F32R)
        pick_r = sb("pick_r", [P, HD, P], F32R)
        ruk = sb("ruk", [P, TILE])
        kv = sb("kv", [P, 2, TILE])
        S = sb("S", [P, 2, HD, TILE + 1])
        prod = sb("prod", [P, HD, TILE])
        bonus = sb("bonus", [P, TILE])
        tg = sb("tg", [P, TILE])
        sg = sb("sg", [P, 2, TILE])
        sq = sb("sq", [P, TILE])
        lnv = sb("lnv", [P, TILE])
        hrstd = sb("hrstd", [P, 2, TILE])
        yn = sb("yn", [P, TILE])
        o = sb("o", [P, TILE])

        loads = sem("loads"); consts = sem("consts"); passed = sem("passed")
        x_in = [sem("x_in0"), sem("x_in1")]
        stats = sem("stats"); aggr = sem("aggr"); ve_s = sem("ve_s"); rstd_s = sem("rstd_s"); xn = sem("xn")
        p_t = sem("p_t"); xt = sem("xt"); dx_s = sem("dx_s"); lerp_s = sem("lerp_s")
        p_rk = sem("p_rk"); p_vg = sem("p_vg"); p_d = sem("p_d")
        th_rk = sem("th_rk"); th_vg = sem("th_vg"); th_d = sem("th_d"); th_d2 = sem("th_d2")
        p_l = sem("p_l"); corr_s = sem("corr_s"); mixed = sem("mixed")
        p_a2 = sem("p_a2"); p_l2 = sem("p_l2"); e1_s = sem("e1_s"); w_s = sem("w_s")
        p_k = sem("p_k"); p_r = sem("p_r"); p_v = sem("p_v"); p_g = sem("p_g"); p_vr = sem("p_vr")
        k_s = sem("k_s"); r_s = sem("r_s"); v_s = sem("v_s"); pick_s = sem("pick_s"); v_high_s = sem("v_high_s"); v_hi_s = sem("v_hi_s"); v_lo_s = sem("v_lo_s"); ruk_s = sem("ruk_s"); carry = sem("carry")
        kv_s = sem("kv_s"); scan_s = sem("scan_s"); prod_s = sem("prod_s")
        p_a = sem("p_a"); bonus_s = sem("bonus_s"); p_y = sem("p_y"); p_yb = sem("p_yb")
        tg_s = sem("tg_s"); sg_s = sem("sg_s"); sq_s = sem("sq_s"); p_var = sem("p_var")
        ln_s = sem("ln_s"); hrstd_s = sem("hrstd_s"); yn_s = sem("yn_s"); aff_s = sem("aff_s")
        o_s = sem("o_s"); p_out = sem("p_out"); x2_s = sem("x2_s")
        LAG = 4

        def mat(name, rows=slice(0, P), cols=slice(0, P)):
            return mats[rows, MATS.index(name), cols]

        def col(name):
            n = VECS.index(name)
            return vec[:, n:n + 1]

        def xtile(t):
            return X[:, bass.ds(t * TILE, TILE)].rearrange("p (c d) -> p c d", c=CH)

        block = ctx.enter_context(nc.Block())

        @block.sync
        def _(sp):
            def load_x(t, p):
                sp.dma_start(xtile(t), x_dram[bass.ds(t * TILE, TILE), :].rearrange("(c p) d -> p c d", p=P)
                             ).then_inc(x_in[p], 16)

            load_x(0, 0)
            sp.dma_start(mats[:, :, :], a["mats"]).then_inc(loads, 16)
            sp.dma_start(vec[:, :], a["vecs"]).then_inc(loads, 16)
            load_x(1, 1)
            sp.dma_start(pick[:, :, :], a["pick"]).then_inc(loads, 16)
            sp.dma_start(sums[:, :, :], a["sums"]).then_inc(loads, 16)
            sp.dma_start(ident[:, :], a["ident"]).then_inc(loads, 16)
            with nc.allow_non_contiguous_dma("starting state, one value per state row"):
                sp.dma_start(S[:, 0, :, 0:1], a["init_state"].rearrange("h i (j a) -> (h i) j a", a=1)).then_inc(loads, 16)
            with sp.Fori(2, NT - 1, 2) as t:
                for p in range(2):
                    sp.wait_ge(x_in[p], t * 8)
                    sp.sem_inc(passed, 1)
                    load_x(t + p, p)

        R_LOADS = 16 * 6

        @block.gpsimd
        def _(pool):
            pool.memset(minus_half[:, :], -0.5).then_inc(consts, 1)
            pool.memset(eps_col[:, :], EPS).then_inc(consts, 1)
            pool.memset(xT[:, 0, 0:1], 0.0).then_inc(consts, 1)
            pool.wait_ge(consts, 3)

            def step(i, p, live):
                q = 1 - p

                def add(n, name):
                    t = i - 1
                    ge(pool, corr_s, t * 5 + (n + 1))
                    if n == 0:
                        ge(pool, p_a2, t)
                        dst = mix_d[:, :]
                    else:
                        ge(pool, {"k": p_k, "r": p_r, "v": p_v, "g": p_g}[name], t - 1)
                        dst = mix[:, n - 1, q, :]
                    pool.tensor_tensor(dst, corr[:, n, :], xT[:, q, 1:TILE + 1], ALU.add).then_inc(mixed, 1)

                def times_r(j):
                    t = i - 2
                    ge(pool, scan_s, t * HD + (j + 1))
                    if j == 0:
                        ge(pool, r_s, t + 1)
                    ge(pool, p_y, (t - 1) * HD + (j + 1))
                    pool.tensor_tensor(prod[:, j, :], S[:, p, j, 0:TILE], rS[:, p, :], ALU.mult).then_inc(prod_s, 1)

                if live(0):
                    ge(pool, ve_s, i + 1)
                    ge(pool, xn, i)
                    pool.tensor_tensor(rstd[:, :], ve[:, :], minus_half[:, :].to_broadcast([P, CH]), ALU.pow).then_inc(rstd_s, 1)
                for n, name in enumerate("dkrv"):
                    if live(1):
                        add(n, name)
                    if live(2):
                        times_r(n)
                if live(2):
                    times_r(4)
                    times_r(5)
                if live(0):
                    ge(pool, xt, i + 1)
                    ge(pool, corr_s, (i - 1) * 5)
                    ge(pool, lerp_s, i - 1)
                    pool.tensor_tensor(dx[:, p, :], xT[:, p, 0:TILE], xT[:, p, 1:TILE + 1], ALU.subtract).then_inc(dx_s, 1)
                if live(1):
                    add(4, "g")
                if live(2):
                    times_r(6)
                    times_r(7)

            pipelined(pool, NT, LAG - 2, step)

        @block.scalar
        def _(act):
            act.wait_ge(loads, R_LOADS)
            act.wait_ge(consts, 3)

            def tanh(dst, src, ready, n, free, m, done, scale=1.0):
                ge(act, ready, n)
                ge(act, free, m)
                act.activation(dst, src, ACT.Tanh, scale=scale).then_inc(done, 1)

            def step(i, p, live):
                q = 1 - p
                bank = lambda n: ps_a[:, (n + p) % 2, :]
                t1, t2, t3 = i - 1, i - 2, i - 3
                if live(3):
                    tanh(tg[:, :], ps_v[:, BANK_G, :], p_g, t3 + 1, sg_s, t3, tg_s, 0.5)
                if live(1):
                    tanh(t_rk[:, :], bank(0), p_rk, t1 + 1, p_l, (t1 - 1) * 5 + 3, th_rk)
                if live(2):
                    ge(act, p_k, t2 + 1)
                    ge(act, kv_s, (t2 - 1) * HD)
                    act.copy(kS[:, p, :], ps_v[:, BANK_K, :]).then_inc(k_s, 1)
                if live(1):
                    tanh(t_vg[:, :], bank(1), p_vg, t1 + 1, p_l, (t1 - 1) * 5 + 5, th_vg)
                if live(2):
                    ge(act, p_v, t2 + 1)
                    ge(act, bonus_s, t2 - 1)
                    ge(act, v_lo_s, t2 - 1)
                    act.copy(vS[:, p, :], ps_v[:, BANK_V, :]).then_inc(v_s, 1)
                if live(1):
                    tanh(t_d[:, :], bank(2)[0:LORA, :], p_d, t1 + 1, p_l, (t1 - 1) * 5 + 1, th_d)
                if live(2):
                    ge(act, p_r, t2 + 1)
                    ge(act, prod_s, (t2 - 1) * HD)
                    act.copy(rS[:, p, :], ps_v[:, BANK_R, :]).then_inc(r_s, 1)
                if live(1):
                    tanh(t_d2[:, :], bank(7)[0:LORA, :], p_a2, t1 + 1, p_l2, t1, th_d2)
                if live(0):
                    ge(act, p_t, i + 1)
                    ge(act, mixed, (i - 1) * 5)
                    ge(act, lerp_s, i - 1)
                    ge(act, xt, i)
                    if p == 1:
                        act.copy(xT[:, 1, 0:1], xT[:, 0, TILE:TILE + 1])
                    act.copy(xT[:, p, 1:TILE + 1], bank(8)).then_inc(xt, 1)
                if live(3):
                    ge(act, p_yb, t3 + 1)
                    ge(act, p_var, t3)
                    act.activation(sq[:, :], ps_y[:, q, :], ACT.Square).then_inc(sq_s, 1)
                if live(1):
                    ge(act, p_l2, t1 + 1)
                    ge(act, w_s, t1)
                    act.activation(e1[:, :], bank(10), ACT.Exp, bias=col("d_ll")).then_inc(e1_s, 1)
                    ge(act, e1_s, t1 + 1)
                    ge(act, scan_s, (t1 - 1) * HD)
                    act.activation(w[:, q, :], e1[:, :], ACT.Exp, scale=-1.0).then_inc(w_s, 1)
                if live(3):
                    ge(act, p_var, t3 + 1)
                    ge(act, hrstd_s, t3)
                    act.activation(lnv[:, :], ps_z[:, :], ACT.Ln, bias=eps_col[:, :]).then_inc(ln_s, 1)
                    ge(act, ln_s, t3 + 1)
                    ge(act, yn_s, t3 - 1)
                    act.activation(hrstd[:, q, :], lnv[:, :], ACT.Exp, scale=-0.5).then_inc(hrstd_s, 1)

            pipelined(act, NT, LAG - 1, step)

        @block.tensor
        def _(pe):
            pe.wait_ge(loads, R_LOADS)

            def mm(dst, lhs, rhs, done, start=True, stop=True):
                pe.matmul(dst, lhs, rhs, start=start, stop=stop).then_inc(done, 1)

            def step(i, p, live):
                q = 1 - p
                bank = lambda n: ps_a[:, (n + p) % 2, :]
                t1, t2, t3, t4 = i - 1, i - 2, i - 3, i - 4

                def y(j):
                    if live(3):
                        ge(pe, prod_s, t3 * HD + (j + 1))
                        if j == 0:
                            ge(pe, yn_s, t3 - 1)
                        mm(ps_y[:, q, :], sums[:, j, :], prod[:, j, :], p_y, j == 0, False)

                def v_of(j):
                    if live(2):
                        if j < 3:
                            ge(pe, [k_s, v_s, r_s][j], t2 + 1)
                        else:
                            ge(pe, kv_s, t2 * HD + (j - 2))
                        if j == 0:
                            ge(pe, v_hi_s, t2 + 1)
                            if isinstance(i, int) and i == 2:
                                pe.wait_ge(pick_s, 1)
                        pe.matmul(ps_v[:, j % 3, :], pick_r[:, j, :], v_hi[:, :],
                                  start=True, stop=False)
                        if j == 0:
                            ge(pe, v_lo_s, t2 + 1)
                        mm(ps_v[:, j % 3, :], pick_r[:, j, :], v_lo[:, :], p_vr, False, True)

                if live(1):
                    ge(pe, lerp_s, t1 + 1)
                    ge(pe, corr_s, t1 * 5)
                    mm(bank(0), mat("la_rk"), lerp[:, :], p_rk)
                if live(2):
                    ge(pe, mixed, t2 * 5 + 2)
                    ge(pe, kv_s, t2 * HD - 1)
                    mm(ps_v[:, BANK_K, :], mat("kW"), mix[:, 0, p, :], p_k)
                if live(3):
                    ge(pe, ruk_s, t3 + 1)
                    ge(pe, ln_s, t3)
                    mm(ps_z[:, :], sums[:, HD, :], ruk[:, :], p_a)
                if live(1):
                    ge(pe, e1_s, t1)
                    mm(bank(1), mat("la_vg"), lerp[:, :], p_vg)
                if live(2):
                    ge(pe, mixed, t2 * 5 + 4)
                    ge(pe, kv_s, t2 * HD)
                    mm(ps_v[:, BANK_V, :], mat("vW"), mix[:, 2, p, :], p_v)
                y(0)
                if live(1):
                    ge(pe, th_rk, t1 + 1)
                    mm(bank(2)[0:LORA, :], mat("la_d", cols=slice(0, LORA)), lerp[:, :], p_d)
                if live(2):
                    ge(pe, mixed, t2 * 5 + 3)
                    ge(pe, sg_s, t2)
                    mm(ps_v[:, BANK_R, :], mat("rW"), mix[:, 1, p, :], p_r)
                y(1)
                if live(1):
                    ge(pe, th_vg, t1 + 1)
                    ge(pe, th_d, t1 + 1)
                    mm(bank(3), mat("lb_d", rows=slice(0, LORA)), t_d[:, :], p_l)
                v_of(0)
                y(2)
                if live(1):
                    mm(bank(4), mat("lb_rk", rows=slice(LORA, P)), t_rk[LORA:P, :], p_l)
                v_of(1)
                y(3)
                if live(4):
                    ge(pe, o_s, t4 + 1)
                    if live(3):
                        ge(pe, bonus_s, t3 + 1)
                    for n in range(CH):
                        op = pe.matmul(ps_z[:, n * P:(n + 1) * P], o[:, n * P:(n + 1) * P], mat("oW"),
                                       start=True, stop=True)
                    op.then_inc(p_out, 1)
                if live(1):
                    ge(pe, corr_s, t1 * 5 + 1)
                    mm(bank(5), mat("lb_rk", rows=slice(0, LORA)), t_rk[0:LORA, :], p_l)
                v_of(2)
                y(4)
                if live(1):
                    ge(pe, corr_s, t1 * 5 + 2)
                    mm(bank(6), mat("lb_vg", rows=slice(0, LORA)), t_vg[0:LORA, :], p_l)
                v_of(3)
                y(5)
                if live(1):
                    ge(pe, mixed, t1 * 5 + 1)
                    ge(pe, corr_s, t1 * 5 + 3)
                    mm(bank(7)[0:LORA, :], mat("la_d", cols=slice(0, LORA)), mix_d[:, :], p_a2)
                v_of(4)
                y(6)
                if live(0):
                    ge(pe, xn, i + 1)
                    ge(pe, corr_s, t1 * 5 + 4)
                    for n in range(CH):
                        op = pe.transpose(bank(8)[:, n * P:(n + 1) * P], XN[:, n, :], ident[:, :])
                    op.then_inc(p_t, 1)
                v_of(5)
                y(7)
                if live(1):
                    ge(pe, th_d2, t1 + 1)
                    mm(bank(9), mat("lb_vg", rows=slice(LORA, P)), t_vg[LORA:P, :], p_l)
                v_of(6)
                if live(3):
                    ge(pe, bonus_s, t3 + 1)
                    mm(ps_y[:, q, :], sums[:, HD + 1, :], bonus[:, :], p_yb, False, True)
                if live(1):
                    if live(0):
                        ge(pe, xt, i + 1)
                    else:
                        ge(pe, corr_s, t1 * 5 + 4)
                    mm(bank(10), mat("lb_d", rows=slice(0, LORA)), t_d2[:, :], p_l2)
                v_of(7)
                if live(3):
                    ge(pe, sq_s, t3 + 1)
                    ge(pe, x2_s, t3)
                    mm(ps_z[:, :], sums[:, HD + 2, :], sq[:, :], p_var)
                if live(2):
                    ge(pe, mixed, t2 * 5 + 5)
                    ge(pe, kv_s, t2 * HD + 6)
                    mm(ps_v[:, BANK_G, :], mat("gW"), mix[:, 3, p, :], p_g)

            pipelined(pe, NT, LAG, step)

        @block.vector
        def _(dve):
            dve.wait_ge(loads, R_LOADS)
            dve.wait_ge(consts, 3)
            dve.tensor_copy(pick_r[:, :, :], pick[:, :, :]).then_inc(pick_s, 1)

            def step(i, p, live):
                q = 1 - p
                bank = lambda n: ps_a[:, (n + p) % 2, :]
                t1, t2, t3, t4 = i - 1, i - 2, i - 3, i - 4

                def correct(n, name, use):
                    if live(1):
                        ge(dve, p_l, t1 * 5 + (n + 1))
                        ge(dve, mixed, (t1 - 1) * 5 + (n + 1))
                        dve.scalar_tensor_tensor(corr[:, n, :], bank(use), col(name + "_ll"), dx[:, q, :],
                                                 ALU.add, ALU.mult).then_inc(corr_s, 1)

                def recur(j):
                    if live(2):
                        ge(dve, p_vr, t2 * HD + (j + 1))
                        ge(dve, scan_s, t2 * HD + (j - 1))
                        dve.tensor_tensor(kv[:, j % 2, :], ps_v[:, j % 3, :], kS[:, p, :], ALU.mult).then_inc(kv_s, 1)
                        ge(dve, kv_s, t2 * HD + (j + 1))
                        if j == 0:
                            ge(dve, w_s, t2 + 1)
                        ge(dve, prod_s, (t2 - 2) * HD + (j + 1))
                        dve.tensor_tensor_scan(S[:, p, j, 1:TILE + 1], w[:, p, :], kv[:, j % 2, :], S[:, p, j, 0:1],
                                               ALU.mult, ALU.add).then_inc(scan_s, 1)

                if live(3):
                    ge(dve, tg_s, t3 + 1)
                    ge(dve, o_s, t3 - 1)
                    dve.scalar_tensor_tensor(sg[:, q, :], tg[:, :], 1.0, ps_v[:, BANK_G, :], ALU.add, ALU.mult).then_inc(sg_s, 1)
                if live(0):
                    ge(dve, x_in[p], (i - p) * 8 + 16)
                    ge(dve, aggr, i)
                    xi = xtile(i)
                    for n in range(CH):
                        op = dve.bn_stats(st[:, n, :], xi[:, n, :])
                    op.then_inc(stats, 1)
                if live(3):
                    ge(dve, p_a, t3 + 1)
                    ge(dve, v_s, t3 + 1)
                    ge(dve, p_yb, t3)
                    dve.tensor_tensor(bonus[:, :], ps_z[:, :], vS[:, q, :], ALU.mult).then_inc(bonus_s, 1)
                if live(0):
                    ge(dve, stats, i + 1)
                    ge(dve, xn, i - 1)
                    dve.sem_inc(passed, 1)
                    for n in range(CH):
                        op = dve.bn_aggr(mv[:, p, n, :], st[:, n, :])
                    op.then_inc(aggr, 1)
                    ge(dve, aggr, i + 1)
                    ge(dve, rstd_s, i)
                    dve.tensor_scalar(ve[:, :], mv[:, p, :, 1], EPS, None, ALU.add).then_inc(ve_s, 1)
                if live(4):
                    ge(dve, hrstd_s, t4 + 1)
                    ge(dve, o_s, t4)
                    dve.tensor_tensor(yn[:, :], ps_y[:, p, :], hrstd[:, p, :], ALU.mult).then_inc(yn_s, 1)
                    ge(dve, yn_s, t4 + 1)
                    dve.tensor_scalar(yn[:, :], yn[:, :], col("ln_w"), col("ln_b"), ALU.mult, ALU.add).then_inc(aff_s, 1)
                    ge(dve, aff_s, t4 + 1)
                    ge(dve, p_out, t4)
                    dve.tensor_tensor(o[:, :], yn[:, :], sg[:, p, :], ALU.mult).then_inc(o_s, 1)
                if live(2):
                    ge(dve, v_s, t2 + 1)
                    ge(dve, p_vr, t2 * HD)
                    ge(dve, v_lo_s, t2)
                    dve.tensor_scalar(v_high[:, :].bitcast(I32), vS[:, p, :].bitcast(I32), HIGH_PART, None,
                                      ALU.bitwise_and).then_inc(v_high_s, 1)
                    ge(dve, v_high_s, t2 + 1)
                    dve.tensor_copy(v_hi[:, :], v_high[:, :]).then_inc(v_hi_s, 1)
                    dve.tensor_tensor(v_lo[:, :], vS[:, p, :], v_high[:, :], ALU.subtract).then_inc(v_lo_s, 1)
                    ge(dve, k_s, t2 + 1)
                    ge(dve, r_s, t2 + 1)
                    ge(dve, p_a, t2)
                    dve.scalar_tensor_tensor(ruk[:, :], rS[:, p, :], col("u"), kS[:, p, :], ALU.mult, ALU.mult).then_inc(ruk_s, 1)
                    if p == 1:
                        ge(dve, scan_s, t2 * HD)
                        ge(dve, prod_s, (t2 - 1) * HD)
                        dve.tensor_copy(S[:, 1, :, 0:1], S[:, 0, :, TILE:TILE + 1]).then_inc(carry, 1)
                    else:
                        dve.sem_inc(carry, 1)
                    ge(dve, carry, t2 + 1)
                correct(0, "d", 3)
                recur(0)
                if live(0):
                    ge(dve, rstd_s, i + 1)
                    ge(dve, p_t, i)
                    xi = xtile(i)
                    for n in range(CH):
                        op = dve.tensor_scalar(XN[:, n, :], xi[:, n, :], mv[:, p, n, 0:1], rstd[:, n:n + 1],
                                               ALU.subtract, ALU.mult)
                    op.then_inc(xn, 1)
                correct(1, "k", 4)
                recur(1)
                if live(4):
                    ge(dve, p_out, t4 + 1)
                    dve.scalar_tensor_tensor(xtile(t4), ps_z[:, :].rearrange("p (c d) -> p c d", c=CH), 0.5, xtile(t4),
                                             ALU.mult, ALU.add).then_inc(x2_s, 1)
                correct(2, "r", 5)
                recur(2)
                correct(3, "v", 6)
                recur(3)
                recur(4)
                recur(5)
                correct(4, "g", 9)
                recur(6)
                recur(7)
                if live(0):
                    ge(dve, dx_s, i + 1)
                    ge(dve, p_d, i)
                    dve.scalar_tensor_tensor(lerp[:, :], dx[:, p, :], col("xw"), xT[:, p, 1:TILE + 1],
                                             ALU.mult, ALU.add).then_inc(lerp_s, 1)

            pipelined(dve, NT, LAG, step)
            dve.wait_ge(x2_s, NT)


class Consts:
    pass


def program(nc, a, out):
    with ExitStack() as ctx:
        def sb(name, shape, dt=F32):
            return ctx.enter_context(nc.sbuf_tensor(name, shape, dt))

        c = Consts()
        c.sems = []
        c.ident = sb("ident", [P, P])
        c.same_e = sb("same_e", [P, P])
        c.earlier = sb("earlier", [P, P])
        c.part = sb("part", [P, 1])
        c.count_rows = sb("count_rows", [P, P, GROUP], BF16)
        c.chunk_of = sb("chunk_of", [P, TILE], BF16)
        c.minus_half = sb("minus_half", [P, 1])
        X = sb("X", [P, NT * TILE])
        table = nc.dram_tensor("table", (T, ROW), F32, kind="Internal").ap()
        x1_dram = nc.dram_tensor("x1_dram", (T, D), F32, kind="Internal").ap()
        x_dram = a["L0_attn_x"].rearrange("b t d -> (b t) d")
        out_dram = out.rearrange("b t d -> (b t) d")
        f = lambda n: a["L0_ffn_" + n]
        w = (f("W1").rearrange("e d h -> (e d) h"), f("b1"), f("W2").rearrange("e h d -> (e h) d"), f("b2"),
             f("gate"), f("Ws1"), f("bs1"), f("Ws2"), f("bs2"))
        attn = {n: a[n] for n in ("mats", "vecs", "pick", "sums", "ident")}
        attn["init_state"] = a["L0_attn_init_state"]
        setup_block(nc, c, a)
        ffn_block(nc, c, X, x_dram, w, table, x1_dram, "_a")
        clear_semaphores(nc, c)
        attention_block(nc, c, X, x1_dram, attn)
        clear_semaphores(nc, c)
        ffn_block(nc, c, X, None, w, table, out_dram, "_b")


INPUTS = ["L0_attn_x", "L0_attn_init_state", "L0_ffn_gate", "L0_ffn_W1", "L0_ffn_b1", "L0_ffn_W2",
          "L0_ffn_b2", "L0_ffn_Ws1", "L0_ffn_bs1", "L0_ffn_Ws2", "L0_ffn_bs2"]


def laid_out(inputs):
    at = {n[len("L0_attn_"):]: np.asarray(v) for n, v in inputs.items() if n.startswith("L0_attn_")}
    both = {"la_rk": ("r_la", "k_la"), "la_vg": ("v_la", "g_la"), "lb_rk": ("r_lb", "k_lb"), "lb_vg": ("v_lb", "g_lb")}
    mats = np.zeros((P, len(MATS), P), np.float32)
    for n, name in enumerate(MATS):
        if name in both:
            m = np.concatenate([at[x] for x in both[name]], axis=0 if name.startswith("la") else 1)
        else:
            m = at[{"la_d": "d_la", "lb_d": "d_lb"}.get(name, name)]
        mats[:m.shape[1], n, :m.shape[0]] = m.T
    vecs = np.stack([np.tile(at[v], HEADS) if v.startswith("ln") else at[v] for v in VECS], axis=1)
    head = np.kron(np.eye(HEADS, dtype=np.float32), np.ones((HD, HD), np.float32))
    one = np.tile(np.eye(HD, dtype=np.float32), (1, HEADS))
    pick = np.stack([head * one[j][:, None] for j in range(HD)], axis=1)
    sums = [head * (one[j][None, :] - np.float32(1 / HD)) for j in range(HD)]
    sums += [head, np.eye(P, dtype=np.float32) - head / HD, head / HD]
    return {"mats": mats, "vecs": vecs, "pick": pick, "sums": np.stack(sums, axis=1).astype(np.float32),
            "ident": np.eye(P, dtype=np.float32)}


def kernel(**inputs):
    import concourse.bacc as bacc
    from concourse.bass_utils import run_bass_kernel_spmd

    nc = bacc.Bacc("TRN2", target_bir_lowering=False, num_devices=1)
    arrays = {n: np.asarray(inputs[n]) for n in INPUTS} | laid_out(inputs)
    arrays = {n: np.ascontiguousarray(v) for n, v in arrays.items()}
    aps = {n: nc.dram_tensor("in_" + n, v.shape, F32, kind="ExternalInput").ap() for n, v in arrays.items()}
    out = nc.dram_tensor("out", (NSEQ, SEQ, D), F32, kind="ExternalOutput").ap()
    program(nc, aps, out)
    ran = run_bass_kernel_spmd(nc, [{"in_" + n: v for n, v in arrays.items()}], core_ids=[0])
    return ran.results[0]["out"]
```

```python
from contextlib import ExitStack

import numpy as np

import concourse.bass as bass
from concourse import mybir

F32 = mybir.dt.float32
I32 = mybir.dt.int32
BF16 = mybir.dt.bfloat16
F32R = mybir.dt.float32r
ALU = mybir.AluOpType
ACT = mybir.ActivationFunctionType
AX_X = mybir.AxisListType.X

P = 128
D = 128
NSEQ, SEQ = 8, 1024
T = NSEQ * SEQ
TILE = 512
CH = TILE // P
NT = T // TILE
E = 8
HID = 512
HK = HID // P
CAP = T // E
SLOTS = CAP // P
HEADS, HD = 16, 8
LORA = 64
EPS = 1e-5
ROW = D + E
ROUNDS = 15
HIGH_PART = -(1 << 12)
EARLY = (NT - 4) // 2
GROUP = 16


def ge(eng, sem, count):
    if isinstance(count, int) and count <= 0:
        return
    eng.wait_ge(sem, count)


def pipelined(eng, n, lag, body, ways=2):
    first = ways * -(-(lag + ways) // ways)
    for i in range(first):
        body(i, i % ways, lambda k, i=i: 0 <= i - k < n)
    with eng.Fori(first, n - ways + 1, ways) as i:
        for m in range(ways):
            body(i + m, m, lambda k: True)
    for i in range(n, n + lag):
        body(i, i % ways, lambda k, i=i: 0 <= i - k < n)


def pipelined_pairs(eng, n, lag, body):
    first = 4 * -(-(lag + 4) // 4)
    for i in range(first):
        body(i, i % 4, i // 2, lambda k, i=i: 0 <= i - k < n)
    with eng.Fori(first // 2, n // 2 - 1, 2) as h:
        for m in range(4):
            body(h * 2 + m, m, h + m // 2, lambda k: True)
    for i in range(n, n + lag):
        body(i, i % 4, i // 2, lambda k, i=i: 0 <= i - k < n)


def setup_block(nc, c, src):
    with ExitStack() as ctx:
        pi = ctx.enter_context(nc.sbuf_tensor("pi", [P, 1], I32))
        pmi = ctx.enter_context(nc.sbuf_tensor("pmi", [P, 2], I32))
        pmf = ctx.enter_context(nc.sbuf_tensor("pmf", [P, 2], F32))
        col = ctx.enter_context(nc.sbuf_tensor("col", [P, 2, P], F32))
        iotas = ctx.enter_context(nc.semaphore("iotas"))
        zeroed = ctx.enter_context(nc.semaphore("zeroed"))
        mods = ctx.enter_context(nc.semaphore("mods"))
        block = ctx.enter_context(nc.Block())

        @block.sync
        def _(sp):
            X, x_dram, w = src
            for t in range(4):
                sp.dma_start(X[:, t * TILE:(t + 1) * TILE].rearrange("p (c d) -> p c d", c=CH),
                             x_dram[t * TILE:(t + 1) * TILE, :].rearrange("(c p) d -> p c d", p=P)).then_inc(c.x_in[t], 16)
                if t == 0:
                    sp.dma_start(c.gate[:, :], w.gate).then_inc(c.gate_in, 16)
            sp.dma_start(c.bs2[:, :], w.bs2.rearrange("(a d) -> a d", a=1).to_broadcast([P, D])).then_inc(c.shared_in, 16)
            sp.dma_start(c.ws1[:, :], w.Ws1).then_inc(c.shared_in, 16)
            sp.dma_start(c.ws2[:, :, :], w.Ws2.rearrange("(k p) d -> p k d", p=P)).then_inc(c.shared_in, 16)
            with nc.allow_non_contiguous_dma("biases onto partitions, small"):
                for k in range(HK):
                    sp.dma_start(c.bs1[:, k:k + 1], w.bs1[k * P:(k + 1) * P].rearrange("(p a) -> p a", a=1)).then_inc(c.shared_in, 16)

        @block.gpsimd
        def _(pool):
            some = {"allow_small_or_imprecise_dtypes": True}
            pool.iota(pi[:, :], pattern=[[0, 1]], base=0, channel_multiplier=1).then_inc(iotas, 1)
            pool.iota(col[:, 0, :], pattern=[[0, NT], [1, E]], base=0, channel_multiplier=0, **some).then_inc(iotas, 1)
            pool.iota(col[:, 1, :], pattern=[[1, NT], [0, E]], base=0, channel_multiplier=0, **some).then_inc(iotas, 1)
            pool.iota(c.part[:, :], pattern=[[0, 1]], base=0, channel_multiplier=1, **some)
            pool.memset(c.minus_half[:, :], -0.5)
            pool.memset(c.ident[:, :], 0.0).then_inc(zeroed, 1)
            pool.wait_ge(zeroed, 1)
            pool.affine_select(out=c.ident[:, :], in_=c.ident[:, :], compare_op=ALU.not_equal, fill=1.0,
                               base=0, pattern=[[-1, P]], channel_multiplier=1)

        @block.vector
        def _(dve):
            dve.wait_ge(iotas, 3)
            dve.tensor_scalar(pmi[:, 0:1], pi[:, :], E - 1, None, ALU.bitwise_and).then_inc(mods, 1)
            dve.tensor_scalar(pmi[:, 1:2], pi[:, :], 3, None, ALU.arith_shift_right).then_inc(mods, 1)
            dve.wait_ge(mods, 2)
            dve.tensor_copy(pmf[:, :], pmi[:, :]).then_inc(mods, 1)
            dve.wait_ge(mods, 3)
            dve.tensor_scalar(c.same_e[:, :], col[:, 0, :], pmf[:, 0:1], None, ALU.is_equal).then_inc(mods, 1)
            dve.wait_ge(mods, 4)
            dve.scalar_tensor_tensor(c.earlier[:, :], col[:, 1, :], pmf[:, 1:2], c.same_e[:, :],
                                     ALU.is_gt, ALU.mult).then_inc(mods, 1)


def clear_semaphores(nc, c):
    nc.clear_and_free_semaphores(c.sems)
    nc.all_engine_barrier()
    c.sems = []


def ffn_block(nc, c, X, x_dram, w, table, acc, tag):
    first = x_dram is not None
    gate, ws1, ws2, bs1, bs2, half_bs2, b1 = c.gate, c.ws1, c.ws2, c.bs1, c.bs2, c.half_bs2, c.b1
    with ExitStack() as ctx:
        def sb(name, shape, dt=F32):
            return ctx.enter_context(nc.sbuf_tensor(name + tag, shape, dt))

        def ps(name, shape):
            return ctx.enter_context(nc.psum_tensor(name + tag, shape, F32))

        def sem(name):
            c.sems.append(nc.alloc_semaphore(name=name + tag))
            return c.sems[-1]

        ps_t = ps("ps_t", [P, 2, TILE])
        ps_h = ps("ps_h", [P, HK, TILE])
        ps_o = ps("ps_o", [P, 2, CH, D])

        we1 = sb("we1", [P, 2, HID])
        we2 = sb("we2", [P, 2, HK, D])
        b2 = sb("b2", [P, 2, D])

        XTs = sb("XTs", [P, 2, TILE])
        XN = sb("XN", [P, 4, CH, ROW])
        st = sb("st", [P, 2, CH, 6])
        mv = sb("mv", [P, 2, CH, 2])
        ve = sb("ve", [P, 2, CH])
        rstd = sb("rstd", [P, 2, CH])
        mx = sb("mx", [P, 2, CH])
        lg = sb("lg", [P, 2, CH, E])
        ex = sb("ex", [P, 2, CH, E])
        sm = sb("sm", [P, 2, CH])
        rs = sb("rs", [P, 2, CH])
        probs = sb("probs", [P, CH, NT * E])

        hS = sb("hS", [P, 2, HK, TILE])

        PT = sb("PT", [P, TILE])
        PT_top = sb("PT_top", [P, TILE], BF16)
        hit = sb("hit", [P, 3, TILE], BF16)
        thr = sb("thr", [P, 1], I32)
        step_up = sb("step_up", [P, 3], I32)
        cand = sb("cand", [P, 3], I32)
        fits = sb("fits", [P, 3], I32)
        most = sb("most", [P, 1], I32)
        cnt = sb("cnt", [P, 3])
        ties = sb("ties", [P, 2])
        more = sb("more", [P, TILE])
        same = sb("same", [P, TILE])
        rank = sb("rank", [P, TILE])
        limit = sb("limit", [P, 2])
        taken = sb("taken", [P, TILE])
        order = more
        slot = sb("slot", [P, TILE])
        slot_i = sb("slot_i", [P, TILE], I32)
        hi_i = sb("hi_i", [P, TILE], I32)
        lo_i = sb("lo_i", [P, TILE], I32)
        hi_f = sb("hi_f", [P, E, CH, GROUP], BF16)
        lo_f = sb("lo_f", [P, TILE], BF16)
        lo_hot = sb("lo_hot", [P, SLOTS, TILE], BF16)
        ids = sb("ids", [P, 2, SLOTS, TILE], BF16)
        hi_hot = sb("hi_hot", [P, CH, P, GROUP], BF16)
        tok_f = sb("tok_f", [P, 2 * SLOTS])
        tok = sb("tok", [P, E * SLOTS], I32)
        tok_g = sb("tok_g", [P, 2, SLOTS], I32)
        tok_s = sb("tok_s", [P, 2, SLOTS], I32)

        G = XN
        score = sb("score", [P, 2, CH])
        Y = sb("Y", [P, 4, CH, D])
        with nc.sbuf_tensor("XT" + tag, [P, NT * TILE], F32) as XT:
            pass
        GT_hi = sb("GT_hi", [P, 2, TILE], F32R)
        GT_lo = sb("GT_lo", [P, 2, TILE], F32R)
        W_hi = sb("W_hi", [P, 2, HID], F32R)
        W_lo = sb("W_lo", [P, 2, HID], F32R)
        GT_high = sb("GT_high", [P, TILE])
        W_high = sb("W_high", [P, HID])

        passed = sem("passed")
        x_in = c.x_in
        var = sem("var"); varE = sem("varE"); rstd_s = sem("rstd_s"); stats = sem("stats")
        xn = sem("xn"); xt_ps = sem("xt_ps"); xt = sem("xt"); xt_big = sem("xt_big")
        logit = sem("logit"); mxs = sem("mxs"); shifted = sem("shifted"); expd = sem("expd")
        summed = sem("summed"); inv = sem("inv"); prob = sem("prob"); prob_kept = sem("prob_kept")
        stored = [sem("stored%d" % n) for n in range(4)]
        hid = sem("hid"); act_s = sem("act_s"); outp = sem("outp"); xb = sem("xb"); x1 = sem("x1")
        halfb = sem("halfb")
        acc_in = [sem("acc_in0"), sem("acc_in1")]
        pt_ps = sem("pt_ps"); pt = sem("pt"); srch = sem("srch"); counted = sem("counted"); total = sem("total")
        sel = sem("sel"); selp = sem("selp"); listed = sem("listed")
        hot = [sem("hot%d" % g) for g in range(CH)]
        hot_used = sem("hot_used"); tokf = sem("tokf"); tok_g_ = sem("tok_g_"); tok_s_ = sem("tok_s_")
        toks = sem("toks")
        gath = [sem("gath%d" % g) for g in range(4)]
        scat = sem("scat")
        y_free = sem("y_free")
        ew = [sem("ew0"), sem("ew1")]
        gt_ps = sem("gt_ps"); gt = sem("gt"); gt_high = sem("gt_high"); gt_lo = sem("gt_lo"); w_high = sem("w_high"); w_parts = sem("w_parts"); eh = sem("eh"); eact = sem("eact"); eo = sem("eo")
        sc = sem("sc"); ytmp = sem("ytmp"); y = sem("y")

        block = ctx.enter_context(nc.Block())

        def xtile(t):
            return X[:, bass.ds(t * TILE, TILE)].rearrange("p (c d) -> p c d", c=CH)

        def tokens(dram, t, width):
            return dram[bass.ds(t * TILE, TILE), :].rearrange("(c p) d -> p c d", p=P)

        def alone(eng, *waits):
            for s, n in waits:
                ge(eng, s, n)
                eng.sem_inc(passed, 1)

        def b1_flat(e, k):
            return b1[:, :, :].rearrange("p e k -> p (e k)")[:, bass.ds(e * HK + k, 1)]

        def ids_flat(m):
            return ids[:, :, :, :].rearrange("p a s t -> p (a s) t")[:, :, bass.ds(m, 1)]

        def wide(tile, q):
            return tile[:, q, :].rearrange("p (c a) -> p c a", a=1).to_broadcast([P, CH, E])

        def one_hot_group(e, g):
            nc.vector.wait_ge(listed, 1)
            ge(nc.vector, hot_used, (e - 1) * CH + (g + 1))
            mine = hi_f[:, :, :, :].rearrange("p e g n -> p (e g n)")[:, bass.ds(e * (CH * GROUP) + g * GROUP, GROUP)]
            op = nc.vector.tensor_tensor(hi_hot[:, g, :, :], c.count_rows[:, :, :],
                                         mine.rearrange("p (a n) -> p a n", a=1).to_broadcast([P, P, GROUP]),
                                         ALU.is_equal)
            op.then_inc(hot[g], 1)

        @block.sync
        def _(sp):
            store_lag = 7 if first else 0

            def rows(i, m, live):
                if first and live(0) and live(4):
                    alone(sp, (x_in[m], (i - m) * 4), (stats, i - 3))
                    sp.dma_start(xtile(i), tokens(x_dram, i, D)).then_inc(x_in[m], 16)
                if live(store_lag):
                    t, q = i - store_lag, (m - store_lag) % 4
                    alone(sp, (prob, t + 1), (stored[q], (t - q) * 4))
                    sp.dma_start(tokens(table, t, ROW), XN[:, q, :, :]).then_inc(stored[q], 16)

            pipelined(sp, NT, store_lag, rows, 4)

            if first:
                with nc.allow_non_contiguous_dma("biases onto partitions, small"):
                    sp.dma_start(b1[:, :, :], w.b1.rearrange("e (k p) -> p (e k)", p=P).rearrange("p (e k) -> p e k", e=E)).then_inc(c.late_in, 16)
                for tile, name in ((c.mats, "mats"), (c.pick, "pick"), (c.sums, "sums")):
                    sp.dma_start(tile[:, :, :], c.attn[name]).then_inc(c.late_in, 16)
                sp.dma_start(c.vec[:, :], c.attn["vecs"]).then_inc(c.late_in, 16)

            def store_acc(i, p, live):
                if live(0):
                    alone(sp, (x1, i + 1), (acc_in[p], (i - p) * 8))
                    sp.dma_start(tokens(acc, i, D), xtile(i)).then_inc(acc_in[p], 16)

            pipelined(sp, NT, 0, store_acc)

            def load_expert(e, s, used):
                if used:
                    alone(sp, (ytmp, (e - 1) * 2))
                sp.dma_start(we1[:, s, :], w.W1[bass.ds(e * D, D), :]).then_inc(ew[s], 16)
                sp.dma_start(we2[:, s, :, :], w.W2[bass.ds(e * HID, HID), :].rearrange("(k p) d -> p k d", p=P)).then_inc(ew[s], 16)
                sp.dma_start(b2[:, s, :], w.b2[bass.ds(e, 1), :].to_broadcast([P, D])).then_inc(ew[s], 16)

            for e in range(2):
                load_expert(e, e, False)
            with sp.Fori(2, E - 1, 2) as e:
                for s in range(2):
                    load_expert(e + s, s, True)
            for p in range(2):
                sp.wait_ge(acc_in[p], 8 * NT)
            for p in range(4):
                sp.wait_ge(stored[p], 4 * NT)
            sp.wait_ge(scat, 16 * E * SLOTS)
            if first:
                sp.wait_ge(c.late_in, c.LATE)

        @block.gpsimd
        def _(pool):
            def route(i, m, live):
                p = m % 2
                if live(0):
                    ge(pool, varE, i + 1)
                    if live(2):
                        ge(pool, xn, i - 1)
                    pool.tensor_tensor(rstd[:, p, :], ve[:, p, :], c.minus_half[:, :].to_broadcast([P, CH]),
                                       ALU.pow).then_inc(rstd_s, 1)
                if live(3):
                    t, q = i - 3, 1 - p
                    alone(pool, (prob, t + 1))
                    pool.tensor_copy(probs[:, :, bass.ds(t * E, E)], XN[:, (m - 3) % 4, :, D:ROW]).then_inc(prob_kept, 1)
                    if first and isinstance(t, int) and t == 0:
                        pool.wait_ge(c.shared_in, c.SHARED)
                        pool.tensor_scalar(half_bs2[:, :], bs2[:, :], 0.5, None, ALU.mult).then_inc(halfb, 1)
                        pool.wait_ge(halfb, 1)
                    pool.tensor_tensor(xtile(t), xtile(t),
                                       half_bs2[:, :].rearrange("p (a d) -> p a d", a=1).to_broadcast([P, CH, D]),
                                       ALU.add).then_inc(xb, 1)

            pipelined(pool, NT, 3, route, 4)

            if first:
                some = {"allow_small_or_imprecise_dtypes": True}
                pool.iota(c.count_rows[:, :, :], pattern=[[1, P], [0, GROUP]], base=0, channel_multiplier=0,
                          **some).then_inc(c.patterns, 1)
                pool.iota(c.chunk_of[:, :], pattern=[[1, CH], [CH, NT], [0, E]], base=0, channel_multiplier=0,
                          **some).then_inc(c.patterns, 1)
            for p in range(4):
                pool.wait_ge(stored[p], 4 * NT)

            def gather(e, s, half, first):
                g = 2 * s + half
                if half == 0:
                    alone(pool, (toks, e + 1), *([] if first else [(gt_ps, e * 2 - 2)]))
                    pool.tensor_copy(tok_g[:, s, :], tok[:, bass.ds(e * SLOTS, SLOTS)]).then_inc(tok_g_, 1)
                alone(pool, (tok_g_, e + 1),
                      *([] if first else [(gt_ps, e * 2 + (half - 3)), (sc, e * 2 + (half - 3))]))
                for j in range(CH):
                    pool.indirect_dma_start(
                        G[:, g, j, :], None, table[:, :],
                        bass.IndirectOffsetOnAxis(ap=tok_g[:, s, half * CH + j:half * CH + j + 1], axis=0),
                    ).then_inc(gath[g], 16)

            def scatter(e, s, half):
                if half == 0:
                    alone(pool, (toks, e + 1), (scat, e * (16 * SLOTS)))
                    pool.sem_inc(y_free, 2)
                    pool.tensor_copy(tok_s[:, s, :], tok[:, bass.ds(e * SLOTS, SLOTS)]).then_inc(tok_s_, 1)
                alone(pool, (tok_s_, e + 1), (y, e * 2 + (half + 1)))
                for j in range(CH):
                    pool.indirect_dma_start(
                        acc[:, :],
                        bass.IndirectOffsetOnAxis(ap=tok_s[:, s, half * CH + j:half * CH + j + 1], axis=0),
                        Y[:, 2 * s + half, j, :], None, compute_op=ALU.add,
                    ).then_inc(scat, 16)

            pool.sem_inc(y_free, 4)
            for e in range(2):
                for half in range(2):
                    gather(e, e, half, True)
            pool.wait_ge(acc_in[0], 8 * NT)
            pool.wait_ge(acc_in[1], 8 * NT)
            gather(2, 0, 0, False)

            def turn_over(e, s, next1, next0):
                scatter(e, s, 0)
                if next1:
                    gather(e + 2, s, 1, False)
                scatter(e, s, 1)
                if next0:
                    gather(e + 3, 1 - s, 0, False)

            turn_over(0, 0, True, True)
            with pool.Fori(1, E - 4, 2) as e:
                turn_over(e, 1, True, True)
                turn_over(e + 1, 0, True, True)
            turn_over(E - 3, 1, True, False)
            turn_over(E - 2, 0, False, False)
            turn_over(E - 1, 1, False, False)

        @block.scalar
        def _(act):
            def hidden(t, p):
                for k in range(HK):
                    ge(act, hid, t * HK + k + 1)
                    if k == 0:
                        ge(act, outp, t - 1)
                    act.activation(hS[:, p, k, :], ps_h[:, k, :], ACT.Gelu_apprx_tanh,
                                   bias=bs1[:, k:k + 1]).then_inc(act_s, 1)

            def route(i, m, h, live):
                p = m % 2
                if live(2):
                    t = i - 2
                    ge(act, shifted, t + 1)
                    ge(act, prob, t - 1)
                    act.activation(ex[:, p, :, :], lg[:, p, :, :], ACT.Exp).then_inc(expd, 1)
                if live(0):
                    ge(act, xt_ps, i + 1)
                    ge(act, xt_big, i - 1)
                    ge(act, logit, i - 1)
                    act.copy(XTs[:, p, :], ps_t[:, 0, :]).then_inc(xt, 1)
                if live(4) and live(0) and p == 0:
                    hidden(h - 2, (m // 2) % 2)

            pipelined_pairs(act, NT, 2, route)

            with act.Fori(EARLY, NT - 1, 2) as t:
                for p in range(2):
                    hidden(t + p, p)

            def expert_hidden(i, p, e, half):
                for k in range(HK):
                    alone(act, (eh, i * HK + k + 1), *([(eo, i - 1)] if k == 0 else []))
                    act.activation(hS[:, p, k, :], ps_h[:, k, :], ACT.Gelu_apprx_tanh,
                                   bias=b1_flat(e, k)).then_inc(eact, 1)

            if first:
                act.wait_ge(c.late_in, c.LATE)
            for i in range(2):
                expert_hidden(i, i, i // 2, i % 2)
            with act.Fori(1, E) as e:
                for half in range(2):
                    expert_hidden(e * 2 + half, half, e, half)

        @block.tensor
        def _(pe):
            def hidden(t, p, slots):
                for k in range(HK):
                    ge(pe, act_s, t * HK + k + 1 - HK)
                    if k == 0:
                        ge(pe, xt_big, t + 1)
                    pe.matmul(ps_h[:, k, :], ws1[:, k * P:(k + 1) * P], XT[:, bass.ds(t * TILE, TILE)],
                              start=True, stop=True).then_inc(hid, 1)
                    slots(k)

            def output(t, q, slots):
                ge(pe, act_s, t * HK + HK)
                ge(pe, x1, t - 1)
                for n in range(CH):
                    for k in range(HK):
                        op = pe.matmul(ps_o[:, q, n, :], hS[:, q, k, n * P:(n + 1) * P], ws2[:, k, :],
                                       start=(k == 0), stop=(k == HK - 1))
                    if n == CH - 1:
                        op.then_inc(outp, 1)
                    slots(HK + n)

            def nothing(s):
                pass

            def route(i, m, h, live):
                p = m % 2
                if live(1):
                    t, q = i - 1, 1 - p
                    ge(pe, xt, t + 1)
                    ge(pe, shifted, t)
                    if first and isinstance(t, int) and t == 0:
                        pe.wait_ge(c.gate_in, 16)
                    for n in range(CH):
                        op = pe.matmul(ps_t[:, 1, (q * CH + n) * E:(q * CH + n + 1) * E],
                                       XTs[:, q, n * P:(n + 1) * P], gate[:, :], start=True, stop=True)
                    op.then_inc(logit, 1)
                if live(0):
                    ge(pe, xn, i + 1)
                    ge(pe, xt, i)
                    for n in range(CH):
                        op = pe.transpose(ps_t[:, 0, n * P:(n + 1) * P], XN[:, m, n, 0:D], c.ident[:, :])
                    op.then_inc(xt_ps, 1)
                if live(4) and live(0):
                    if first and isinstance(i, int) and i == 4:
                        pe.wait_ge(c.shared_in, c.SHARED)
                    if p == 0:
                        hidden(h - 2, (m // 2) % 2, nothing)
                    else:
                        output(h - 2, (m // 2) % 2, nothing)

            pipelined_pairs(pe, NT, 1, route)

            hidden(EARLY, EARLY % 2, nothing)
            pe.wait_ge(prob_kept, NT)
            for b in range(CH):
                op = pe.transpose(ps_t[:, 0, b * P:(b + 1) * P], probs[:, b, :], c.ident[:, :])
            op.then_inc(pt_ps, 1)

            def shared(i, p, slots):
                hidden(i, p, slots)
                output(i - 1, 1 - p, slots)

            def count_all(n):
                ge(pe, counted, n * 3 + 3)
                pe.matmul(ps_t[:, 1, 0:3], c.same_e[:, :], cnt[:, :], start=True, stop=True).then_inc(total, 1)

            def rounds(r, places):
                def slots(s):
                    if s in places:
                        count_all(r + places.index(s))
                return slots

            EVEN, ODD = [1, 4, 7], [2, 5]
            shared(7, 1, rounds(0, EVEN))
            shared(8, 0, rounds(3, ODD))
            with pe.Fori(1, 3) as d:
                shared(d * 2 + 7, 1, rounds(d * 5, EVEN))
                shared(d * 2 + 8, 0, rounds(d * 5 + 3, ODD))

            def select(i, s):
                if (i, s) == (13, 2):
                    pe.wait_ge(sel, 2)
                    pe.matmul(ps_t[:, 1, 0:1], c.same_e[:, :], ties[:, 0:1], start=True, stop=True)
                    pe.matmul(ps_t[:, 1, 1:2], c.earlier[:, :], ties[:, 1:2], start=True, stop=True).then_inc(selp, 1)
                if (i, s) == (13, 6):
                    pe.wait_ge(sel, 7)
                    pe.matmul(ps_t[:, 1, 2:3], c.earlier[:, :], order[:, TILE - 1:TILE], start=True, stop=True).then_inc(selp, 1)
                if (i, s) == (14, 0):
                    pe.wait_ge(sel, 8)
                    for b in range(CH):
                        op = pe.transpose(ps_t[:, 0, b * P:(b + 1) * P], slot[:, b * P:(b + 1) * P], c.ident[:, :])
                    op.then_inc(selp, 1)

            shared(13, 1, lambda s: select(13, s))
            shared(14, 0, lambda s: select(14, s))

            def list_group(e, g):
                pe.wait_ge(hot[g], e + 1)
                if g == 0:
                    pe.wait_ge(listed, 2)
                    ge(pe, tokf, e)
                for n in range(GROUP):
                    op = pe.matmul(ps_t[:, 1, 0:2 * SLOTS], hi_hot[:, g, :, n],
                                   ids_flat(e + (g * P + n * E)),
                                   start=(g == 0 and n == 0), stop=(g == CH - 1 and n == GROUP - 1))
                op.then_inc(hot_used, 1)

            shared(15, 1, nothing)
            for s in range(CH):
                list_group(0, s)
            output(15, 1, nothing)
            for s in range(CH):
                list_group(1, s)

            def turn(i, g):
                pe.wait_ge(gath[g], gath_count(i, g))
                ge(pe, gt_high, i)
                ge(pe, gt_lo, i)
                for n in range(CH):
                    op = pe.transpose(ps_t[:, 0, n * P:(n + 1) * P], G[:, g, n, 0:D], c.ident[:, :])
                op.then_inc(gt_ps, 1)

            def gath_count(i, g):
                return (i - g) * 16 + 64

            def first_layer(i, g):
                p, s = g % 2, g // 2
                ge(pe, gt, i + 1)
                ge(pe, gt_lo, i + 1)
                if p == 0:
                    pe.wait_ge(w_parts, i + 2)
                    pe.wait_ge(ew[s], ((i - g) // 4 + 1) * 48 if isinstance(i, int) else (i - g) * 12 + 48)
                for k in range(HK):
                    ge(pe, eact, i * HK + k + 1 - HK)
                    if isinstance(i, int) and i == 0 and k == 0:
                        pe.wait_ge(act_s, NT * HK)
                    wk = slice(k * P, (k + 1) * P)
                    pe.matmul(ps_h[:, k, :], W_hi[:, s, wk], GT_lo[:, p, :], start=True, stop=False)
                    pe.matmul(ps_h[:, k, :], W_lo[:, s, wk], GT_hi[:, p, :], start=False, stop=False)
                    pe.matmul(ps_h[:, k, :], W_hi[:, s, wk], GT_hi[:, p, :], start=False, stop=True).then_inc(eh, 1)

            def second_layer(i, g):
                p, s = g % 2, g // 2
                ge(pe, eact, i * HK + HK)
                ge(pe, ytmp, i - 1)
                if isinstance(i, int) and i == 0:
                    pe.wait_ge(x1, NT)
                for n in range(CH):
                    for k in range(HK):
                        op = pe.matmul(ps_o[:, p, n, :], hS[:, p, k, n * P:(n + 1) * P], we2[:, s, k, :],
                                       start=(k == 0), stop=(k == HK - 1))
                op.then_inc(eo, 1)

            def step(i, g, e_list, last=False):
                if not last:
                    turn(i + 1, (g + 1) % 4)
                if e_list is not None:
                    for half in range(2):
                        list_group(e_list, (g % 2) * 2 + half)
                first_layer(i, g)
                if not (isinstance(i, int) and i == 0):
                    second_layer(i - 1, (g + 3) % 4)

            turn(0, 0)
            for i in range(4):
                step(i, i, 2 + i // 2)
            with pe.Fori(2, E - 3, 2) as e:
                for g in range(4):
                    step(e * 2 + g, g, e + (2 + g // 2))
            for i in range(2 * E - 4, 2 * E):
                step(i, i % 4, None, i == 2 * E - 1)
            second_layer(2 * E - 1, 3)

        @block.vector
        def _(dve):
            def shared_out(t, q):
                ge(dve, outp, t + 1)
                ge(dve, xb, t + 1)
                dve.scalar_tensor_tensor(xtile(t), ps_o[:, q, :, :], 0.5, xtile(t), ALU.mult, ALU.add).then_inc(x1, 1)

            def route(i, m, h, live):
                p = m % 2
                if live(0):
                    if x_dram is not None:
                        ge(dve, x_in[m], (i - m) * 4 + 16)
                    ge(dve, var, i - 1)
                    xi = xtile(i)
                    for n in range(CH):
                        op = dve.bn_stats(st[:, p, n, :], xi[:, n, :])
                    op.then_inc(stats, 1)
                if live(1):
                    t, q = i - 1, 1 - p
                    ge(dve, rstd_s, t + 1)
                    b = (m - 1) % 4
                    ge(dve, stored[b], (t - b) * 4)
                    ge(dve, xt_ps, t - 3)
                    ge(dve, prob_kept, t - 3)
                    xi = xtile(t)
                    for n in range(CH):
                        op = dve.tensor_scalar(XN[:, b, n, 0:D], xi[:, n, :], mv[:, q, n, 0:1],
                                               rstd[:, q, n:n + 1], ALU.subtract, ALU.mult)
                    op.then_inc(xn, 1)
                if live(0):
                    alone(dve, (stats, i + 1), (xn, i - 1))
                    for n in range(CH):
                        op = dve.bn_aggr(mv[:, p, n, :], st[:, p, n, :])
                    op.then_inc(var, 1)
                    ge(dve, var, i + 1)
                    ge(dve, rstd_s, i - 1)
                    dve.tensor_scalar(ve[:, p, :], mv[:, p, :, 1], EPS, None, ALU.add).then_inc(varE, 1)
                if live(2):
                    t, q = i - 2, p
                    ge(dve, xt, t + 1)
                    dve.tensor_copy(XT[:, bass.ds(t * TILE, TILE)], XTs[:, q, :]).then_inc(xt_big, 1)
                    ge(dve, logit, t + 1)
                    ge(dve, shifted, t - 1)
                    lps = ps_t[:, 1, q * CH * E:(q + 1) * CH * E].rearrange("p (c e) -> p c e", c=CH)
                    dve.tensor_reduce(mx[:, q, :], lps, AX_X, ALU.max).then_inc(mxs, 1)
                    ge(dve, mxs, t + 1)
                    ge(dve, expd, t - 1)
                    dve.tensor_tensor(lg[:, q, :, :], lps, wide(mx, q), ALU.subtract).then_inc(shifted, 1)
                if live(3):
                    t, q = i - 3, 1 - p
                    ge(dve, expd, t + 1)
                    dve.tensor_reduce(sm[:, q, :], ex[:, q, :, :], AX_X, ALU.add).then_inc(summed, 1)
                    ge(dve, summed, t + 1)
                    ge(dve, prob, t - 1)
                    dve.reciprocal(rs[:, q, :], sm[:, q, :]).then_inc(inv, 1)
                    ge(dve, inv, t + 1)
                    dve.scalar_tensor_tensor(XN[:, (m - 3) % 4, :, D:ROW], ex[:, q, :, :], 0.5, wide(rs, q),
                                             ALU.mult, ALU.mult).then_inc(prob, 1)
                if p == 1 and (not isinstance(i, int) or 7 <= i < 7 + 2 * EARLY):
                    shared_out(h - 3, (m // 2 + 1) % 2)

            pipelined_pairs(dve, NT, 3, route)

            dve.memset(thr[:, :], 0).then_inc(srch, 1)
            for b in range(3):
                dve.memset(step_up[:, b:b + 1], (b + 1) << (2 * (ROUNDS - 1))).then_inc(srch, 1)
            dve.wait_ge(pt_ps, 1)
            dve.tensor_copy(PT[:, :], ps_t[:, 0, :]).then_inc(pt, 1)
            dve.wait_ge(pt, 1)
            dve.tensor_copy(PT_top[:, :], PT[:, :].bitcast(BF16).rearrange("p (t a) -> p t a", a=2)[:, :, 1]).then_inc(pt, 1)
            dve.wait_ge(pt, 2)
            START, PER = 4, 5

            def search_round(n, values=PT, beside=None):
                ge(dve, srch, n * PER + START)
                dve.tensor_tensor(cand[:, :], thr[:, :].to_broadcast([P, 3]), step_up[:, :],
                                  ALU.bitwise_or).then_inc(srch, 1)
                ge(dve, srch, n * PER + (START + 1))
                for b in range(3):
                    dve.tensor_scalar(hit[:, b, :], values[:, :], cand[:, b:b + 1].bitcast(F32), None, ALU.is_ge, ALU.add,
                                      accum_out=cnt[:, b:b + 1]).then_inc(counted, 1)
                if beside is not None:
                    shared_out(*beside)
                ge(dve, total, n + 1)
                dve.scalar_tensor_tensor(fits[:, :], ps_t[:, 1, 0:3], float(CAP), step_up[:, :],
                                         ALU.is_ge, ALU.mult).then_inc(srch, 1)
                ge(dve, srch, n * PER + (START + 2))
                dve.tensor_reduce(most[:, :], fits[:, :], AX_X, ALU.max).then_inc(srch, 1)
                dve.tensor_scalar(step_up[:, :], step_up[:, :], 2, None, ALU.logical_shift_right).then_inc(srch, 1)
                ge(dve, srch, n * PER + (START + 4))
                dve.tensor_tensor(thr[:, :], thr[:, :], most[:, :], ALU.bitwise_or).then_inc(srch, 1)

            for n in range(5):
                search_round(n, PT_top, (6, 0) if n == 3 else None)
            with dve.Fori(1, 3) as d:
                for n in range(5):
                    search_round(d * 5 + n, PT, {0: (d * 2 + 5, 1), 3: (d * 2 + 6, 0)}.get(n))
            FOUND = ROUNDS * PER + START

            dve.wait_ge(srch, FOUND)
            th = thr[:, :].bitcast(F32)
            dve.tensor_scalar(more[:, :], PT[:, :], th, None, ALU.is_gt, ALU.add, accum_out=ties[:, 0:1]).then_inc(sel, 1)
            dve.tensor_scalar(same[:, :], PT[:, :], th, None, ALU.is_equal, ALU.add, accum_out=ties[:, 1:2]).then_inc(sel, 1)
            dve.wait_ge(sel, 2)
            dve.tensor_tensor_scan(rank[:, :], same[:, :], same[:, :], 0.0, ALU.add, ALU.bypass).then_inc(sel, 1)
            dve.wait_ge(selp, 1)
            dve.tensor_scalar(limit[:, 0:1], ps_t[:, 1, 0:1], -1.0, float(CAP), ALU.mult, ALU.add).then_inc(sel, 1)
            dve.wait_ge(sel, 4)
            dve.tensor_tensor(limit[:, 1:2], limit[:, 0:1], ps_t[:, 1, 1:2], ALU.subtract).then_inc(sel, 1)
            dve.wait_ge(sel, 5)
            dve.scalar_tensor_tensor(rank[:, :], rank[:, :], limit[:, 1:2], same[:, :], ALU.is_le, ALU.mult).then_inc(sel, 1)
            dve.wait_ge(sel, 6)
            dve.tensor_tensor(taken[:, :], more[:, :], rank[:, :], ALU.add).then_inc(srch, 1)
            dve.wait_ge(srch, FOUND + 1)
            dve.tensor_tensor_scan(order[:, :], taken[:, :], taken[:, :], 0.0, ALU.add, ALU.bypass).then_inc(sel, 1)
            shared_out(11, 1)
            dve.wait_ge(selp, 2)
            dve.wait_ge(sel, 7)
            dve.scalar_tensor_tensor(slot[:, :], order[:, :], ps_t[:, 1, 2:3], taken[:, :], ALU.add, ALU.mult).then_inc(sel, 1)
            shared_out(12, 0)
            dve.wait_ge(selp, 3)
            dve.tensor_scalar(slot_i[:, :], ps_t[:, 0, :], -1.0, None, ALU.add).then_inc(sel, 1)
            dve.wait_ge(sel, 9)
            dve.tensor_scalar(hi_i[:, :], slot_i[:, :], 3, None, ALU.arith_shift_right).then_inc(sel, 1)
            dve.tensor_scalar(lo_i[:, :], slot_i[:, :], SLOTS - 1, None, ALU.bitwise_and).then_inc(sel, 1)
            dve.wait_ge(sel, 11)
            dve.tensor_copy(hi_f[:, :, :, :], hi_i[:, :].rearrange("p (g n e) -> p e g n", g=CH, e=E)).then_inc(listed, 1)
            dve.tensor_copy(lo_f[:, :], lo_i[:, :]).then_inc(sel, 1)
            dve.wait_ge(sel, 12)
            for n in range(SLOTS):
                dve.tensor_scalar(lo_hot[:, n, :], lo_f[:, :], float(n), None, ALU.is_equal).then_inc(sel, 1)
            shared_out(13, 1)
            if first:
                dve.wait_ge(c.patterns, 2)
            dve.wait_ge(sel, 12 + SLOTS)
            dve.tensor_scalar(ids[:, 0, :, :], lo_hot[:, :, :], c.part[:, :], None, ALU.mult)
            dve.tensor_tensor(ids[:, 1, :, :], lo_hot[:, :, :],
                              c.chunk_of[:, :].rearrange("p (a t) -> p a t", a=1).to_broadcast([P, SLOTS, TILE]),
                              ALU.mult).then_inc(listed, 1)
            dve.wait_ge(listed, 2)
            def join(e):
                dve.wait_ge(hot_used, e * CH + CH)
                ge(dve, toks, e)
                dve.tensor_copy(tok_f[:, :], ps_t[:, 1, 0:2 * SLOTS]).then_inc(tokf, 1)
                dve.wait_ge(tokf, e + 1)
                dve.scalar_tensor_tensor(tok[:, bass.ds(e * SLOTS, SLOTS)], tok_f[:, SLOTS:2 * SLOTS], float(P),
                                         tok_f[:, 0:SLOTS], ALU.mult, ALU.add).then_inc(toks, 1)

            def make_list(e):
                for g in range(CH):
                    one_hot_group(e, g)

            make_list(0)
            join(0)
            shared_out(14, 0)
            make_list(1)
            shared_out(15, 1)
            join(1)

            def turn(i, g):
                p = g % 2
                ge(dve, gt_ps, i + 1)
                if isinstance(i, int) and i == 0:
                    dve.wait_ge(hid, NT * HK)
                ge(dve, gt, i)
                ge(dve, gt_lo, i)
                dve.tensor_scalar(GT_high[:, :].bitcast(I32), ps_t[:, 0, :].bitcast(I32), HIGH_PART, None,
                                  ALU.bitwise_and).then_inc(gt_high, 1)
                ge(dve, gt_high, i + 1)
                ge(dve, eh, i * HK - HK)
                dve.tensor_tensor(GT_lo[:, p, :], ps_t[:, 0, :], GT_high[:, :], ALU.subtract).then_inc(gt_lo, 1)
                dve.tensor_copy(GT_hi[:, p, :], GT_high[:, :]).then_inc(gt, 1)

            def split_weights(e, s):
                dve.wait_ge(ew[s], (e - s) * 24 + 48)
                ge(dve, w_parts, e * 2)
                dve.tensor_scalar(W_high[:, :].bitcast(I32), we1[:, s, :].bitcast(I32), HIGH_PART, None,
                                  ALU.bitwise_and).then_inc(w_high, 1)
                ge(dve, w_high, e + 1)
                ge(dve, eh, (e - 1) * (2 * HK))
                dve.tensor_tensor(W_lo[:, s, :], we1[:, s, :], W_high[:, :], ALU.subtract).then_inc(w_parts, 1)
                dve.tensor_copy(W_hi[:, s, :], W_high[:, :]).then_inc(w_parts, 1)

            def scores(i, e, g):
                p = g % 2
                dve.wait_ge(gt_ps, i + 1)
                ge(dve, y, i - 1)
                dve.tensor_copy(score[:, p, :], G[:, g, :, bass.ds(e + D, 1)].rearrange("p c a -> p (c a)")).then_inc(sc, 1)

            def out(i, e, g):
                p, s = g % 2, g // 2
                ge(dve, eo, i + 1)
                ge(dve, y_free, i + (4 - g % 2))
                dve.tensor_tensor(Y[:, g, :, :], ps_o[:, p, :, :],
                                  b2[:, s, :].rearrange("p (a d) -> p a d", a=1).to_broadcast([P, CH, D]),
                                  ALU.add).then_inc(ytmp, 1)
                ge(dve, ytmp, i + 1)
                ge(dve, sc, i + 1)
                dve.tensor_tensor(Y[:, g, :, :], Y[:, g, :, :],
                                  score[:, p, :].rearrange("p (c a) -> p c a", a=1).to_broadcast([P, CH, D]),
                                  ALU.mult).then_inc(y, 1)

            def step(i, g, e, first=False, last=False, lists=True):
                half = g % 2
                if not last:
                    turn(i + 1, (g + 1) % 4)
                if lists == "join":
                    join(e + 2)
                elif lists:
                    for n in range(2):
                        one_hot_group(e + (2 + half), (1 - half) * 2 + n)
                    if half == 1:
                        join(e + 2)
                if half == 1 and not last:
                    split_weights(e + 1, 1 - g // 2)
                if not first:
                    out(i - 1, None, (g + 3) % 4)
                if not last:
                    scores(i + 1, e + half, (g + 1) % 4)

            turn(0, 0)
            split_weights(0, 0)
            scores(0, 0, 0)
            for n in range(2):
                one_hot_group(2, n)
            for i in range(3):
                step(i, i, i // 2, first=(i == 0))
            with dve.Fori(0, E - 5, 2) as e:
                for i in range(3, 7):
                    step(e * 2 + i, i % 4, e + i // 2)
            step(2 * E - 5, 3, E - 3, lists="join")
            for i in range(2 * E - 4, 2 * E):
                step(i, i % 4, i // 2, last=(i == 2 * E - 1), lists=False)
            out(2 * E - 1, None, 3)


VECS = ["xw", "r_ll", "k_ll", "v_ll", "g_ll", "d_ll", "u", "ln_w", "ln_b"]
MATS = ["rW", "kW", "vW", "gW", "oW", "la_rk", "la_vg", "lb_rk", "lb_vg", "la_d", "lb_d"]
BANK_K, BANK_V, BANK_R, BANK_G = 0, 1, 2, 2


def attention_block(nc, c, X, x_dram, init_state):
    with ExitStack() as ctx:
        def sb(name, shape, dt=F32):
            return ctx.enter_context(nc.sbuf_tensor("t_" + name, shape, dt))

        def ps(name, shape):
            return ctx.enter_context(nc.psum_tensor("t_" + name, shape, F32))

        def sem(name):
            c.sems.append(nc.alloc_semaphore(name="t_" + name))
            return c.sems[-1]

        ps_a = ps("ps_a", [P, 2, TILE])
        ps_v = ps("ps_v", [P, 3, TILE])
        ps_y = ps("ps_y", [P, 2, TILE])
        ps_z = ps("ps_z", [P, TILE])

        vec, mats, pick, sums, ident = c.vec, c.mats, c.pick, c.sums, c.ident
        eps_col = sb("eps_col", [P, 1])
        minus_half = sb("minus_half", [P, 1])

        st = sb("st", [P, CH, 6])
        mv = sb("mv", [P, 2, CH, 2])
        ve = sb("ve", [P, CH])
        rstd = sb("rstd", [P, CH])
        XN = sb("XN", [P, CH, D])
        xT = sb("xT", [P, 2, TILE + 1])
        dx = sb("dx", [P, 2, TILE])
        lerp = sb("lerp", [P, TILE])
        t_rk = sb("t_rk", [P, TILE])
        t_vg = sb("t_vg", [P, TILE])
        t_d = sb("t_d", [LORA, TILE])
        t_d2 = sb("t_d2", [LORA, TILE])
        corr = sb("corr", [P, 5, TILE])
        mix_d = sb("mix_d", [P, TILE])
        mix = sb("mix", [P, 4, 2, TILE])
        e1 = sb("e1", [P, TILE])
        w = sb("w", [P, 2, TILE])
        kS = sb("kS", [P, 2, TILE])
        rS = sb("rS", [P, 2, TILE])
        vS = sb("vS", [P, 2, TILE])
        v_hi = sb("v_hi", [P, TILE], F32R)
        v_lo = sb("v_lo", [P, TILE], F32R)
        pick_r = sb("pick_r", [P, HD, P], F32R)
        ruk = sb("ruk", [P, TILE])
        kv = sb("kv", [P, 2, TILE])
        v_high = kv[:, 0, :]
        S = sb("S", [P, 2, HD, TILE + 1])
        prod = sb("prod", [P, HD, TILE])
        bonus = sb("bonus", [P, TILE])
        tg = sb("tg", [P, TILE])
        sg = sb("sg", [P, 2, TILE])
        sq = sb("sq", [P, TILE])
        lnv = sb("lnv", [P, TILE])
        hrstd = sb("hrstd", [P, 2, TILE])
        yn = sb("yn", [P, TILE])
        o = sb("o", [P, TILE])

        loads = sem("loads"); consts = sem("consts"); passed = sem("passed")
        x_in = [sem("x_in0"), sem("x_in1")]
        stats = sem("stats"); aggr = sem("aggr"); ve_s = sem("ve_s"); rstd_s = sem("rstd_s"); xn = sem("xn")
        p_t = sem("p_t"); xt = sem("xt"); dx_s = sem("dx_s"); lerp_s = sem("lerp_s")
        p_rk = sem("p_rk"); p_vg = sem("p_vg"); p_d = sem("p_d")
        th_rk = sem("th_rk"); th_vg = sem("th_vg"); th_d = sem("th_d"); th_d2 = sem("th_d2")
        p_l = sem("p_l"); corr_s = sem("corr_s"); mixed = sem("mixed")
        p_a2 = sem("p_a2"); p_l2 = sem("p_l2"); e1_s = sem("e1_s"); w_s = sem("w_s")
        p_k = sem("p_k"); p_r = sem("p_r"); p_v = sem("p_v"); p_g = sem("p_g"); p_vr = sem("p_vr")
        k_s = sem("k_s"); r_s = sem("r_s"); v_s = sem("v_s"); pick_s = sem("pick_s"); v_high_s = sem("v_high_s"); v_hi_s = sem("v_hi_s"); v_lo_s = sem("v_lo_s"); ruk_s = sem("ruk_s"); carry = sem("carry")
        kv_s = sem("kv_s"); scan_s = sem("scan_s"); prod_s = sem("prod_s")
        p_a = sem("p_a"); bonus_s = sem("bonus_s"); p_y = sem("p_y"); p_yb = sem("p_yb")
        tg_s = sem("tg_s"); sg_s = sem("sg_s"); sq_s = sem("sq_s"); p_var = sem("p_var")
        ln_s = sem("ln_s"); hrstd_s = sem("hrstd_s"); yn_s = sem("yn_s"); aff_s = sem("aff_s")
        o_s = sem("o_s"); p_out = sem("p_out"); x2_s = sem("x2_s")
        LAG = 4

        def mat(name, rows=slice(0, P), cols=slice(0, P)):
            return mats[rows, MATS.index(name), cols]

        def col(name):
            n = VECS.index(name)
            return vec[:, n:n + 1]

        def xtile(t):
            return X[:, bass.ds(t * TILE, TILE)].rearrange("p (c d) -> p c d", c=CH)

        block = ctx.enter_context(nc.Block())

        @block.sync
        def _(sp):
            def load_x(t, p):
                sp.dma_start(xtile(t), x_dram[bass.ds(t * TILE, TILE), :].rearrange("(c p) d -> p c d", p=P)
                             ).then_inc(x_in[p], 16)

            load_x(0, 0)
            load_x(1, 1)
            with nc.allow_non_contiguous_dma("starting state, one value per state row"):
                sp.dma_start(S[:, 0, :, 0:1], init_state.rearrange("h i (j a) -> (h i) j a", a=1)).then_inc(loads, 16)
            with sp.Fori(2, NT - 1, 2) as t:
                for p in range(2):
                    sp.wait_ge(x_in[p], t * 8)
                    sp.sem_inc(passed, 1)
                    load_x(t + p, p)

        @block.gpsimd
        def _(pool):
            pool.memset(minus_half[:, :], -0.5).then_inc(consts, 1)
            pool.memset(eps_col[:, :], EPS).then_inc(consts, 1)
            pool.memset(xT[:, 0, 0:1], 0.0).then_inc(consts, 1)
            pool.wait_ge(consts, 3)

            def step(i, p, live):
                q = 1 - p

                def add(n, name):
                    t = i - 1
                    ge(pool, corr_s, t * 5 + (n + 1))
                    if n == 0:
                        ge(pool, p_a2, t)
                        dst = mix_d[:, :]
                    else:
                        ge(pool, {"k": p_k, "r": p_r, "v": p_v, "g": p_g}[name], t - 1)
                        dst = mix[:, n - 1, q, :]
                    pool.tensor_tensor(dst, corr[:, n, :], xT[:, q, 1:TILE + 1], ALU.add).then_inc(mixed, 1)

                def times_r(j):
                    t = i - 2
                    ge(pool, scan_s, t * HD + (j + 1))
                    if j == 0:
                        ge(pool, r_s, t + 1)
                    ge(pool, p_y, (t - 1) * HD + (j + 1))
                    pool.tensor_tensor(prod[:, j, :], S[:, p, j, 0:TILE], rS[:, p, :], ALU.mult).then_inc(prod_s, 1)

                if live(0):
                    ge(pool, ve_s, i + 1)
                    ge(pool, xn, i)
                    pool.tensor_tensor(rstd[:, :], ve[:, :], minus_half[:, :].to_broadcast([P, CH]), ALU.pow).then_inc(rstd_s, 1)
                for n, name in enumerate("dkrv"):
                    if live(1):
                        add(n, name)
                    if live(2):
                        times_r(n)
                if live(2):
                    times_r(4)
                if live(0):
                    ge(pool, xt, i + 1)
                    ge(pool, corr_s, (i - 1) * 5)
                    ge(pool, lerp_s, i - 1)
                    pool.tensor_tensor(dx[:, p, :], xT[:, p, 0:TILE], xT[:, p, 1:TILE + 1], ALU.subtract).then_inc(dx_s, 1)
                if live(2):
                    times_r(5)
                if live(1):
                    add(4, "g")
                if live(2):
                    times_r(6)
                    times_r(7)

            pipelined(pool, NT, LAG - 2, step)

        @block.scalar
        def _(act):
            act.wait_ge(consts, 3)

            def tanh(dst, src, ready, n, free, m, done, scale=1.0):
                ge(act, ready, n)
                ge(act, free, m)
                act.activation(dst, src, ACT.Tanh, scale=scale).then_inc(done, 1)

            def step(i, p, live):
                q = 1 - p
                bank = lambda n: ps_a[:, (n + p) % 2, :]
                t1, t2, t3, t4 = i - 1, i - 2, i - 3, i - 4
                if live(3):
                    tanh(tg[:, :], ps_v[:, BANK_G, :], p_g, t3 + 1, sg_s, t3, tg_s, 0.5)
                if live(1):
                    tanh(t_rk[:, :], bank(0), p_rk, t1 + 1, p_l, (t1 - 1) * 5 + 3, th_rk)
                if live(2):
                    ge(act, p_k, t2 + 1)
                    ge(act, kv_s, (t2 - 1) * HD)
                    act.copy(kS[:, p, :], ps_v[:, BANK_K, :]).then_inc(k_s, 1)
                    ge(act, p_v, t2 + 1)
                    ge(act, bonus_s, t2 - 1)
                    ge(act, v_lo_s, t2 - 1)
                    act.copy(vS[:, p, :], ps_v[:, BANK_V, :]).then_inc(v_s, 1)
                if live(1):
                    tanh(t_vg[:, :], bank(1), p_vg, t1 + 1, p_l, (t1 - 1) * 5 + 5, th_vg)
                if live(1):
                    tanh(t_d[:, :], bank(2)[0:LORA, :], p_d, t1 + 1, p_l, (t1 - 1) * 5 + 1, th_d)
                if live(2):
                    ge(act, p_r, t2 + 1)
                    ge(act, prod_s, (t2 - 1) * HD)
                    act.copy(rS[:, p, :], ps_v[:, BANK_R, :]).then_inc(r_s, 1)
                if live(4):
                    ge(act, yn_s, t4 + 1)
                    act.activation(yn[:, :], yn[:, :], ACT.Identity, scale=col("ln_w"), bias=col("ln_b")).then_inc(aff_s, 1)
                if live(1):
                    tanh(t_d2[:, :], bank(7)[0:LORA, :], p_a2, t1 + 1, p_l2, t1, th_d2)
                if live(0):
                    ge(act, p_t, i + 1)
                    ge(act, mixed, (i - 1) * 5)
                    ge(act, lerp_s, i - 1)
                    ge(act, xt, i)
                    if p == 1:
                        act.copy(xT[:, 1, 0:1], xT[:, 0, TILE:TILE + 1])
                    act.copy(xT[:, p, 1:TILE + 1], bank(8)).then_inc(xt, 1)
                if live(3):
                    ge(act, p_yb, t3 + 1)
                    ge(act, p_var, t3)
                    act.activation(sq[:, :], ps_y[:, q, :], ACT.Square).then_inc(sq_s, 1)
                if live(1):
                    ge(act, p_l2, t1 + 1)
                    ge(act, w_s, t1)
                    act.activation(e1[:, :], bank(10), ACT.Exp, bias=col("d_ll")).then_inc(e1_s, 1)
                    ge(act, e1_s, t1 + 1)
                    ge(act, scan_s, (t1 - 1) * HD)
                    act.activation(w[:, q, :], e1[:, :], ACT.Exp, scale=-1.0).then_inc(w_s, 1)
                if live(3):
                    ge(act, p_var, t3 + 1)
                    ge(act, hrstd_s, t3)
                    act.activation(lnv[:, :], ps_z[:, :], ACT.Ln, bias=eps_col[:, :]).then_inc(ln_s, 1)
                    ge(act, ln_s, t3 + 1)
                    ge(act, yn_s, t3 - 1)
                    act.activation(hrstd[:, q, :], lnv[:, :], ACT.Exp, scale=-0.5).then_inc(hrstd_s, 1)

            pipelined(act, NT, LAG, step)

        @block.tensor
        def _(pe):
            def mm(dst, lhs, rhs, done, start=True, stop=True):
                pe.matmul(dst, lhs, rhs, start=start, stop=stop).then_inc(done, 1)

            def step(i, p, live):
                q = 1 - p
                bank = lambda n: ps_a[:, (n + p) % 2, :]
                t1, t2, t3, t4 = i - 1, i - 2, i - 3, i - 4

                def y(j):
                    if live(3):
                        ge(pe, prod_s, t3 * HD + (j + 1))
                        if j == 0:
                            ge(pe, yn_s, t3 - 1)
                        mm(ps_y[:, q, :], sums[:, j, :], prod[:, j, :], p_y, j == 0, False)

                def v_of(j):
                    if live(2):
                        if j < 3:
                            ge(pe, [k_s, v_s, r_s][j], t2 + 1)
                        else:
                            ge(pe, kv_s, t2 * HD + (j - 2))
                        if j == 0:
                            ge(pe, v_hi_s, t2 + 1)
                            if isinstance(i, int) and i == 2:
                                pe.wait_ge(pick_s, 1)
                        pe.matmul(ps_v[:, j % 3, :], pick_r[:, j, :], v_hi[:, :],
                                  start=True, stop=False)
                        if j == 0:
                            ge(pe, v_lo_s, t2 + 1)
                        mm(ps_v[:, j % 3, :], pick_r[:, j, :], v_lo[:, :], p_vr, False, True)

                if live(2):
                    ge(pe, mixed, t2 * 5 + 2)
                    ge(pe, kv_s, t2 * HD - 1)
                    mm(ps_v[:, BANK_K, :], mat("kW"), mix[:, 0, p, :], p_k)
                    ge(pe, mixed, t2 * 5 + 4)
                    ge(pe, kv_s, t2 * HD)
                    mm(ps_v[:, BANK_V, :], mat("vW"), mix[:, 2, p, :], p_v)
                if live(1):
                    ge(pe, lerp_s, t1 + 1)
                    ge(pe, corr_s, t1 * 5)
                    mm(bank(0), mat("la_rk"), lerp[:, :], p_rk)
                if live(3):
                    ge(pe, ruk_s, t3 + 1)
                    ge(pe, ln_s, t3)
                    mm(ps_z[:, :], sums[:, HD, :], ruk[:, :], p_a)
                if live(1):
                    ge(pe, e1_s, t1)
                    mm(bank(1), mat("la_vg"), lerp[:, :], p_vg)
                y(0)
                if live(1):
                    ge(pe, th_rk, t1 + 1)
                    mm(bank(2)[0:LORA, :], mat("la_d", cols=slice(0, LORA)), lerp[:, :], p_d)
                if live(2):
                    ge(pe, mixed, t2 * 5 + 3)
                    ge(pe, sg_s, t2)
                    mm(ps_v[:, BANK_R, :], mat("rW"), mix[:, 1, p, :], p_r)
                y(1)
                if live(1):
                    ge(pe, th_vg, t1 + 1)
                    ge(pe, th_d, t1 + 1)
                    mm(bank(3), mat("lb_d", rows=slice(0, LORA)), t_d[:, :], p_l)
                v_of(0)
                y(2)
                if live(1):
                    mm(bank(4), mat("lb_rk", rows=slice(LORA, P)), t_rk[LORA:P, :], p_l)
                v_of(1)
                y(3)
                if live(4):
                    ge(pe, o_s, t4 + 1)
                    if live(3):
                        ge(pe, bonus_s, t3 + 1)
                    for n in range(CH):
                        op = pe.matmul(ps_z[:, n * P:(n + 1) * P], o[:, n * P:(n + 1) * P], mat("oW"),
                                       start=True, stop=True)
                    op.then_inc(p_out, 1)
                if live(1):
                    ge(pe, corr_s, t1 * 5 + 1)
                    mm(bank(5), mat("lb_rk", rows=slice(0, LORA)), t_rk[0:LORA, :], p_l)
                v_of(2)
                y(4)
                if live(1):
                    ge(pe, corr_s, t1 * 5 + 2)
                    mm(bank(6), mat("lb_vg", rows=slice(0, LORA)), t_vg[0:LORA, :], p_l)
                v_of(3)
                y(5)
                if live(1):
                    ge(pe, mixed, t1 * 5 + 1)
                    ge(pe, corr_s, t1 * 5 + 3)
                    mm(bank(7)[0:LORA, :], mat("la_d", cols=slice(0, LORA)), mix_d[:, :], p_a2)
                v_of(4)
                y(6)
                if live(0):
                    ge(pe, xn, i + 1)
                    ge(pe, corr_s, t1 * 5 + 4)
                    for n in range(CH):
                        op = pe.transpose(bank(8)[:, n * P:(n + 1) * P], XN[:, n, :], ident[:, :])
                    op.then_inc(p_t, 1)
                v_of(5)
                y(7)
                if live(1):
                    ge(pe, th_d2, t1 + 1)
                    mm(bank(9), mat("lb_vg", rows=slice(LORA, P)), t_vg[LORA:P, :], p_l)
                v_of(6)
                if live(3):
                    ge(pe, bonus_s, t3 + 1)
                    mm(ps_y[:, q, :], sums[:, HD + 1, :], bonus[:, :], p_yb, False, True)
                if live(1):
                    if live(0):
                        ge(pe, xt, i + 1)
                    else:
                        ge(pe, corr_s, t1 * 5 + 4)
                    mm(bank(10), mat("lb_d", rows=slice(0, LORA)), t_d2[:, :], p_l2)
                v_of(7)
                if live(2):
                    ge(pe, mixed, t2 * 5 + 5)
                    ge(pe, kv_s, t2 * HD + 6)
                    mm(ps_v[:, BANK_G, :], mat("gW"), mix[:, 3, p, :], p_g)
                if live(3):
                    ge(pe, sq_s, t3 + 1)
                    ge(pe, x2_s, t3)
                    mm(ps_z[:, :], sums[:, HD + 2, :], sq[:, :], p_var)

            pipelined(pe, NT, LAG, step)

        @block.vector
        def _(dve):
            dve.wait_ge(consts, 3)
            dve.tensor_copy(pick_r[:, :, :], pick[:, :, :]).then_inc(pick_s, 1)

            def step(i, p, live):
                q = 1 - p
                bank = lambda n: ps_a[:, (n + p) % 2, :]
                t1, t2, t3, t4 = i - 1, i - 2, i - 3, i - 4

                def correct(n, name, use):
                    if live(1):
                        ge(dve, p_l, t1 * 5 + (n + 1))
                        ge(dve, mixed, (t1 - 1) * 5 + (n + 1))
                        dve.scalar_tensor_tensor(corr[:, n, :], bank(use), col(name + "_ll"), dx[:, q, :],
                                                 ALU.add, ALU.mult).then_inc(corr_s, 1)

                def recur(j):
                    if live(2):
                        ge(dve, p_vr, t2 * HD + (j + 1))
                        ge(dve, scan_s, t2 * HD + (j - 1))
                        if j == 0:
                            ge(dve, v_hi_s, t2 + 1)
                            ge(dve, v_lo_s, t2 + 1)
                        dve.tensor_tensor(kv[:, j % 2, :], ps_v[:, j % 3, :], kS[:, p, :], ALU.mult).then_inc(kv_s, 1)
                        ge(dve, kv_s, t2 * HD + (j + 1))
                        if j == 0:
                            ge(dve, w_s, t2 + 1)
                        ge(dve, prod_s, (t2 - 2) * HD + (j + 1))
                        dve.tensor_tensor_scan(S[:, p, j, 1:TILE + 1], w[:, p, :], kv[:, j % 2, :], S[:, p, j, 0:1],
                                               ALU.mult, ALU.add).then_inc(scan_s, 1)

                if live(3):
                    ge(dve, tg_s, t3 + 1)
                    ge(dve, o_s, t3 - 1)
                    dve.scalar_tensor_tensor(sg[:, q, :], tg[:, :], 1.0, ps_v[:, BANK_G, :], ALU.add, ALU.mult).then_inc(sg_s, 1)
                if live(0):
                    ge(dve, x_in[p], (i - p) * 8 + 16)
                    ge(dve, aggr, i)
                    xi = xtile(i)
                    for n in range(CH):
                        op = dve.bn_stats(st[:, n, :], xi[:, n, :])
                    op.then_inc(stats, 1)
                if live(3):
                    ge(dve, p_a, t3 + 1)
                    ge(dve, v_s, t3 + 1)
                    ge(dve, p_yb, t3)
                    dve.tensor_tensor(bonus[:, :], ps_z[:, :], vS[:, q, :], ALU.mult).then_inc(bonus_s, 1)
                if live(0):
                    ge(dve, stats, i + 1)
                    ge(dve, xn, i - 1)
                    dve.sem_inc(passed, 1)
                    for n in range(CH):
                        op = dve.bn_aggr(mv[:, p, n, :], st[:, n, :])
                    op.then_inc(aggr, 1)
                    ge(dve, aggr, i + 1)
                    ge(dve, rstd_s, i)
                    dve.tensor_scalar(ve[:, :], mv[:, p, :, 1], EPS, None, ALU.add).then_inc(ve_s, 1)
                if live(4):
                    ge(dve, hrstd_s, t4 + 1)
                    ge(dve, o_s, t4)
                    dve.tensor_tensor(yn[:, :], ps_y[:, p, :], hrstd[:, p, :], ALU.mult).then_inc(yn_s, 1)
                if live(2):
                    ge(dve, v_s, t2 + 1)
                    ge(dve, p_vr, t2 * HD)
                    ge(dve, scan_s, t2 * HD)
                    dve.tensor_scalar(v_high.bitcast(I32), vS[:, p, :].bitcast(I32), HIGH_PART, None,
                                      ALU.bitwise_and).then_inc(v_high_s, 1)
                    ge(dve, v_high_s, t2 + 1)
                    dve.tensor_copy(v_hi[:, :], v_high).then_inc(v_hi_s, 1)
                    dve.tensor_tensor(v_lo[:, :], vS[:, p, :], v_high, ALU.subtract).then_inc(v_lo_s, 1)
                if live(4):
                    ge(dve, aff_s, t4 + 1)
                    ge(dve, p_out, t4)
                    dve.tensor_tensor(o[:, :], yn[:, :], sg[:, p, :], ALU.mult).then_inc(o_s, 1)
                if live(2):
                    ge(dve, k_s, t2 + 1)
                    ge(dve, r_s, t2 + 1)
                    ge(dve, p_a, t2)
                    dve.scalar_tensor_tensor(ruk[:, :], rS[:, p, :], col("u"), kS[:, p, :], ALU.mult, ALU.mult).then_inc(ruk_s, 1)
                    if p == 1:
                        ge(dve, scan_s, t2 * HD)
                        ge(dve, prod_s, (t2 - 1) * HD)
                        dve.tensor_copy(S[:, 1, :, 0:1], S[:, 0, :, TILE:TILE + 1]).then_inc(carry, 1)
                    else:
                        if isinstance(t2, int) and t2 == 0:
                            dve.wait_ge(loads, 16)
                        dve.sem_inc(carry, 1)
                    ge(dve, carry, t2 + 1)
                correct(0, "d", 3)
                recur(0)
                if live(0):
                    ge(dve, rstd_s, i + 1)
                    ge(dve, p_t, i)
                    xi = xtile(i)
                    for n in range(CH):
                        op = dve.tensor_scalar(XN[:, n, :], xi[:, n, :], mv[:, p, n, 0:1], rstd[:, n:n + 1],
                                               ALU.subtract, ALU.mult)
                    op.then_inc(xn, 1)
                correct(1, "k", 4)
                recur(1)
                if live(4):
                    ge(dve, p_out, t4 + 1)
                    dve.scalar_tensor_tensor(xtile(t4), ps_z[:, :].rearrange("p (c d) -> p c d", c=CH), 0.5, xtile(t4),
                                             ALU.mult, ALU.add).then_inc(x2_s, 1)
                correct(2, "r", 5)
                recur(2)
                correct(3, "v", 6)
                recur(3)
                recur(4)
                recur(5)
                correct(4, "g", 9)
                recur(6)
                if live(0):
                    ge(dve, dx_s, i + 1)
                    ge(dve, p_d, i)
                    dve.scalar_tensor_tensor(lerp[:, :], dx[:, p, :], col("xw"), xT[:, p, 1:TILE + 1],
                                             ALU.mult, ALU.add).then_inc(lerp_s, 1)
                recur(7)

            pipelined(dve, NT, LAG, step)
            dve.wait_ge(x2_s, NT)


class Weights:
    pass


class Consts:
    pass


def program(nc, a, out):
    with ExitStack() as ctx:
        def sb(name, shape, dt=F32):
            return ctx.enter_context(nc.sbuf_tensor(name, shape, dt))

        c = Consts()
        c.sems = []
        c.ident = sb("ident", [P, P])
        c.same_e = sb("same_e", [P, P])
        c.earlier = sb("earlier", [P, P])
        c.part = sb("part", [P, 1])
        c.count_rows = sb("count_rows", [P, P, GROUP], BF16)
        c.chunk_of = sb("chunk_of", [P, TILE], BF16)
        c.minus_half = sb("minus_half", [P, 1])
        X = sb("X", [P, NT * TILE])
        table = nc.dram_tensor("table", (T, ROW), F32, kind="Internal").ap()
        x1_dram = nc.dram_tensor("x1_dram", (T, D), F32, kind="Internal").ap()
        x_dram = a["L0_attn_x"].rearrange("b t d -> (b t) d")
        out_dram = out.rearrange("b t d -> (b t) d")
        f = lambda n: a["L0_ffn_" + n]
        w = Weights()
        w.W1, w.W2 = f("W1").rearrange("e d h -> (e d) h"), f("W2").rearrange("e h d -> (e h) d")
        w.b1, w.b2, w.gate, w.Ws1, w.bs1, w.Ws2, w.bs2 = (f(n) for n in ("b1", "b2", "gate", "Ws1", "bs1", "Ws2", "bs2"))
        c.gate = sb("gate", [P, E])
        c.ws1 = sb("ws1", [P, HID])
        c.ws2 = sb("ws2", [P, HK, D])
        c.bs1 = sb("bs1", [P, HK])
        c.bs2 = sb("bs2", [P, D])
        c.half_bs2 = sb("half_bs2", [P, D])
        c.b1 = sb("b1", [P, E, HK])
        c.vec = sb("vec", [P, len(VECS)])
        c.mats = sb("mats", [P, len(MATS), P])
        c.pick = sb("pick", [P, HD, P])
        c.sums = sb("sums", [P, HD + 3, P])
        c.attn = {n: a[n] for n in ("mats", "vecs", "pick", "sums")}
        c.x_in = [nc.alloc_semaphore(name="x_in%d" % p) for p in range(4)]
        c.gate_in = nc.alloc_semaphore(name="gate_in")
        c.shared_in = nc.alloc_semaphore(name="shared_in")
        c.patterns = nc.alloc_semaphore(name="patterns")
        c.late_in = nc.alloc_semaphore(name="late_in")
        c.SHARED, c.LATE = 16 * (3 + HK), 16 * 5
        c.sems += c.x_in + [c.gate_in, c.shared_in, c.late_in, c.patterns]
        setup_block(nc, c, (X, x_dram, w))
        ffn_block(nc, c, X, x_dram, w, table, x1_dram, "_a")
        clear_semaphores(nc, c)
        attention_block(nc, c, X, x1_dram, a["L0_attn_init_state"])
        clear_semaphores(nc, c)
        ffn_block(nc, c, X, None, w, table, out_dram, "_b")


INPUTS = ["L0_attn_x", "L0_attn_init_state", "L0_ffn_gate", "L0_ffn_W1", "L0_ffn_b1", "L0_ffn_W2",
          "L0_ffn_b2", "L0_ffn_Ws1", "L0_ffn_bs1", "L0_ffn_Ws2", "L0_ffn_bs2"]


def laid_out(inputs):
    at = {n[len("L0_attn_"):]: np.asarray(v) for n, v in inputs.items() if n.startswith("L0_attn_")}
    both = {"la_rk": ("r_la", "k_la"), "la_vg": ("v_la", "g_la"), "lb_rk": ("r_lb", "k_lb"), "lb_vg": ("v_lb", "g_lb")}
    mats = np.zeros((P, len(MATS), P), np.float32)
    for n, name in enumerate(MATS):
        if name in both:
            m = np.concatenate([at[x] for x in both[name]], axis=0 if name.startswith("la") else 1)
        else:
            m = at[{"la_d": "d_la", "lb_d": "d_lb"}.get(name, name)]
        mats[:m.shape[1], n, :m.shape[0]] = m.T
    vecs = np.stack([np.tile(at[v], HEADS) if v.startswith("ln") else at[v] for v in VECS], axis=1)
    head = np.kron(np.eye(HEADS, dtype=np.float32), np.ones((HD, HD), np.float32))
    one = np.tile(np.eye(HD, dtype=np.float32), (1, HEADS))
    pick = np.stack([head * one[j][:, None] for j in range(HD)], axis=1)
    sums = [head * (one[j][None, :] - np.float32(1 / HD)) for j in range(HD)]
    sums += [head, np.eye(P, dtype=np.float32) - head / HD, head / HD]
    return {"mats": mats, "vecs": vecs, "pick": pick, "sums": np.stack(sums, axis=1).astype(np.float32)}


def kernel(**inputs):
    import concourse.bacc as bacc
    from concourse.bass_utils import run_bass_kernel_spmd

    nc = bacc.Bacc("TRN2", target_bir_lowering=False, num_devices=1)
    arrays = {n: np.asarray(inputs[n]) for n in INPUTS} | laid_out(inputs)
    arrays = {n: np.ascontiguousarray(v) for n, v in arrays.items()}
    aps = {n: nc.dram_tensor("in_" + n, v.shape, F32, kind="ExternalInput").ap() for n, v in arrays.items()}
    out = nc.dram_tensor("out", (NSEQ, SEQ, D), F32, kind="ExternalOutput").ap()
    program(nc, aps, out)
    ran = run_bass_kernel_spmd(nc, [{"in_" + n: v for n, v in arrays.items()}], core_ids=[0])
    return ran.results[0]["out"]
```
